# Optimizing a Trainium2 kernel written in Bass

```python
import numpy as np
import jax
import jax.numpy as jnp

def _softmax(x, axis=-1):
    return jax.nn.softmax(x, axis=axis)

def _gelu(x):
    return jax.nn.gelu(x, approximate=True)

def _silu(x):
    return jax.nn.silu(x)

def _sigmoid(x):
    return jax.nn.sigmoid(x)

def _layernorm(x, axis=-1, eps=1e-05):
    m = jnp.mean(x, axis=axis, keepdims=True)
    v = jnp.var(x, axis=axis, keepdims=True)
    return (x - m) / jnp.sqrt(v + eps)

def _scatter_add(tgt, idx, src, axis=0):
    return tgt.at[idx].add(src)

def _segment_sum(src, seg, n):
    return jax.ops.segment_sum(src, seg, n)
kernel_name = 'mk_adj_resnorm_d2_adj_r2_b2a982'

def setup_inputs(seed: int=0):
    np.random.seed(seed)
    _w = jnp.asarray

    def _rec_inputs():
        import jax
        import jax.numpy as jnp
        _gk = jax.random.key(seed)
        x = -0.0001538 + 1 * jax.random.normal(jax.random.fold_in(_gk, 1), (64, 128, 384), jnp.float32)
        _a = jax.random.bernoulli(jax.random.fold_in(_gk, 2), 0.03125, (64, 128, 128))
        _a = jnp.logical_or(_a, jnp.eye(128, dtype=bool))
        adj = _a
        return (x, adj)
    x, adj = _rec_inputs()

    def _L0_gnn_setup():
        import jax, jax.numpy as jnp
        import numpy as np
        B, S, H = (4, 1024, 384)
        NUM_HEADS = 6
        HEAD_SIZE = H // NUM_HEADS
        NEG = -9000000000000000.0

        def _heads(x):
            b, s, _ = x.shape
            return x.reshape(b, s, NUM_HEADS, HEAD_SIZE).transpose(0, 2, 1, 3)
        key = jax.random.key(seed)
        ks = jax.random.split(key, 10)
        seq_inputs = jax.random.normal(ks[0], (B, S, H), dtype=jnp.float32)
        gm = jax.random.randint(ks[1], (B, S, S), 0, 2) > 0
        graph_mask = gm | jnp.eye(S, dtype=bool)[None]
        sc = 1.0 / np.sqrt(H)
        Wq = jax.random.normal(ks[2], (H, H), dtype=jnp.float32) * sc
        bq = jnp.zeros((H,), dtype=jnp.float32)
        Wk = jax.random.normal(ks[3], (H, H), dtype=jnp.float32) * sc
        bk = jnp.zeros((H,), dtype=jnp.float32)
        Wv = jax.random.normal(ks[4], (H, H), dtype=jnp.float32) * sc
        bv = jnp.zeros((H,), dtype=jnp.float32)
        Wf = jax.random.normal(ks[5], (H, H), dtype=jnp.float32) * sc
        bf = jnp.zeros((H,), dtype=jnp.float32)
        return {'seq_inputs': seq_inputs, 'Wq': Wq, 'bq': bq, 'Wk': Wk, 'bk': bk, 'Wv': Wv, 'bv': bv, 'Wf': Wf, 'bf': bf, 'graph_mask': graph_mask}
    _L0_gnn_all = _L0_gnn_setup()
    _L0_gnn_in = {k: v for k, v in _L0_gnn_all.items() if k in ('Wq', 'bq', 'Wk', 'bk', 'Wv', 'bv', 'Wf', 'bf')}
    del _L0_gnn_all

    def _L1_gnn_setup():
        import jax, jax.numpy as jnp
        import numpy as np
        ATT_HEAD = 12
        IN_DIM = 384
        OUT_DIM = IN_DIM // ATT_HEAD
        LEAKY_ALPHA = 0.2
        B, N = (8, 256)
        key = jax.random.key(seed)
        ks = jax.random.split(key, 8)
        feat_in = jax.random.normal(ks[0], (B, N, IN_DIM), dtype=jnp.float32)
        adj = jax.random.randint(ks[1], (B, N, N), 0, 2) > 0
        lim_W = float(np.sqrt(6.0 / (IN_DIM + OUT_DIM)))
        W = jax.random.uniform(ks[2], (ATT_HEAD, IN_DIM, OUT_DIM), minval=-lim_W, maxval=lim_W, dtype=jnp.float32)
        b = jnp.zeros((OUT_DIM,), dtype=jnp.float32)
        lim_w = float(np.sqrt(6.0 / (OUT_DIM + 1)))
        w_src = jax.random.uniform(ks[3], (ATT_HEAD, OUT_DIM, 1), minval=-lim_w, maxval=lim_w, dtype=jnp.float32)
        w_dst = jax.random.uniform(ks[4], (ATT_HEAD, OUT_DIM, 1), minval=-lim_w, maxval=lim_w, dtype=jnp.float32)
        std_H = float(np.sqrt(2.0 / (IN_DIM + IN_DIM)))
        H_w = jax.random.normal(ks[5], (IN_DIM, IN_DIM), dtype=jnp.float32) * std_H
        H_b = jax.random.normal(ks[6], (IN_DIM,), dtype=jnp.float32) * 0.01
        return {'feat_in': feat_in, 'adj': adj, 'W': W, 'b': b, 'w_src': w_src, 'w_dst': w_dst, 'H_w': H_w, 'H_b': H_b}
    _L1_gnn_all = _L1_gnn_setup()
    _L1_gnn_in = {k: v for k, v in _L1_gnn_all.items() if k in ('W', 'b', 'w_src', 'w_dst', 'H_w', 'H_b')}
    del _L1_gnn_all
    return {'x': x, 'adj': adj, 'L0_gnn_Wq': _L0_gnn_in['Wq'], 'L0_gnn_bq': _L0_gnn_in['bq'], 'L0_gnn_Wk': _L0_gnn_in['Wk'], 'L0_gnn_bk': _L0_gnn_in['bk'], 'L0_gnn_Wv': _L0_gnn_in['Wv'], 'L0_gnn_bv': _L0_gnn_in['bv'], 'L0_gnn_Wf': _L0_gnn_in['Wf'], 'L0_gnn_bf': _L0_gnn_in['bf'], 'L1_gnn_W': _L1_gnn_in['W'], 'L1_gnn_b': _L1_gnn_in['b'], 'L1_gnn_w_src': _L1_gnn_in['w_src'], 'L1_gnn_w_dst': _L1_gnn_in['w_dst'], 'L1_gnn_H_w': _L1_gnn_in['H_w'], 'L1_gnn_H_b': _L1_gnn_in['H_b']}

def reference(x, adj, L0_gnn_Wq, L0_gnn_bq, L0_gnn_Wk, L0_gnn_bk, L0_gnn_Wv, L0_gnn_bv, L0_gnn_Wf, L0_gnn_bf, L1_gnn_W, L1_gnn_b, L1_gnn_w_src, L1_gnn_w_dst, L1_gnn_H_w, L1_gnn_H_b):
    import jax
    import jax.numpy as jnp

    def _L0_gnn_ref(seq_inputs, Wq, bq, Wk, bk, Wv, bv, Wf, bf, graph_mask):
        import jax, jax.numpy as jnp
        import numpy as np
        B, S, H = (4, 1024, 384)
        NUM_HEADS = 6
        HEAD_SIZE = H // NUM_HEADS
        NEG = -9000000000000000.0

        def _heads(x):
            b, s, _ = x.shape
            return x.reshape(b, s, NUM_HEADS, HEAD_SIZE).transpose(0, 2, 1, 3)
        q = _heads(seq_inputs @ Wq + bq)
        k = _heads(seq_inputs @ Wk + bk)
        v = _heads(seq_inputs @ Wv + bv)
        scores = jnp.einsum('bhqd,bhkd->bhqk', q, k) / np.sqrt(HEAD_SIZE)
        bias = jnp.where(graph_mask, 0.0, NEG)[:, None]
        probs = jax.nn.softmax(scores + bias, axis=-1)
        ctx = jnp.einsum('bhqk,bhkd->bhqd', probs, v)
        ctx = ctx.transpose(0, 2, 1, 3).reshape(seq_inputs.shape[0], seq_inputs.shape[1], H)
        return ctx @ Wf + bf

    def _L1_gnn_ref(feat_in, adj, W, b, w_src, w_dst, H_w, H_b):
        import jax, jax.numpy as jnp
        import numpy as np
        ATT_HEAD = 12
        IN_DIM = 384
        OUT_DIM = IN_DIM // ATT_HEAD
        LEAKY_ALPHA = 0.2
        B, N = (8, 256)
        h = jnp.einsum('bnd,ade->bane', feat_in, W)
        th = jnp.tanh(h)
        attn_src = jnp.einsum('bane,aeo->bano', th, w_src)
        attn_dst = jnp.einsum('bane,aeo->bano', th, w_dst)
        attn = attn_src + jnp.swapaxes(attn_dst, 2, 3)
        attn = jnp.where(attn >= 0, attn, LEAKY_ALPHA * attn)
        mask = ~adj[:, None, :, :]
        attn = jnp.where(mask, jnp.float32(-999.0), attn)
        attn = jax.nn.softmax(attn, axis=-1)
        feat_out = jnp.einsum('banm,bame->bane', attn, h) + b
        feat_out = jnp.swapaxes(feat_out, 1, 2).reshape(feat_in.shape[0], feat_in.shape[1], -1)
        feat_out = jax.nn.elu(feat_out)
        gate = jax.nn.sigmoid(feat_in @ H_w.T + H_b)
        return gate * feat_out + (1.0 - gate) * feat_in
    x = _layernorm(x + _L0_gnn_ref(x, L0_gnn_Wq, L0_gnn_bq, L0_gnn_Wk, L0_gnn_bk, L0_gnn_Wv, L0_gnn_bv, L0_gnn_Wf, L0_gnn_bf, adj), axis=-1)
    x = _layernorm(x + _L1_gnn_ref(x, adj, L1_gnn_W, L1_gnn_b, L1_gnn_w_src, L1_gnn_w_dst, L1_gnn_H_w, L1_gnn_H_b), axis=-1)
    return x

_drawn_inputs = setup_inputs


def setup_inputs(seed=0):
    import zlib

    import numpy as np

    out = dict(_drawn_inputs(seed))
    spreads = {'L0_gnn_bq': (0.0, 0.1),
     'L0_gnn_bk': (0.0, 2.0),
     'L0_gnn_bv': (0.0, 0.1),
     'L0_gnn_bf': (0.0, 0.1),
     'L1_gnn_b': (0.0, 0.1)}
    factors = {'L1_gnn_H_b': 33.06}
    for name, (base, spread) in spreads.items():
        noise = np.random.default_rng([zlib.crc32(name.encode()), seed]).standard_normal(out[name].shape)
        drawn = base * np.exp(spread * noise) if base else spread * noise
        out[name] = jnp.asarray(drawn.astype(out[name].dtype))
    for name, factor in factors.items():
        out[name] = (out[name] * factor).astype(out[name].dtype)
    return out
```

```python
from contextlib import ExitStack

import concourse.bass as bass
from concourse import mybir

F32 = mybir.dt.float32
F32R = mybir.dt.float32r
BF16 = mybir.dt.bfloat16
F16 = mybir.dt.float16
U8 = mybir.dt.uint8
ALU = mybir.AluOpType
ACT = mybir.ActivationFunctionType
AX = mybir.AxisListType

GRAPHS, N, D = 64, 128, 384
PAIRS = GRAPHS // 2
C = D // 128
H0 = 6
E0 = D // H0
H1 = 12
E1 = D // H1
EPS = 1e-5
SCALE0 = float(E0) ** -0.5
MASKED = 9e15 / SCALE0
PSCALE = 16384.0
WEIGHTS = ("Wq", "Wk", "Wv", "Wf", "W1", "Hw")
DONE_BY_DMA = 16


class Signal:

    def __init__(self, sem, stage, unit, back=0):
        self.sem, self.stage, self.unit, self.back = sem, stage, unit, back


class Turn:

    def __init__(self, eng, t, passed):
        self.eng, self.t, self.loop, self.counts, self.passed = eng, t, not isinstance(t, int), {}, passed

    def count(self, step, turns):
        if not self.loop:
            return max(min(self.t + turns, PAIRS) * step.unit - step.back, 0)
        key = turns, step.unit, step.back
        if key not in self.counts:
            self.counts[key] = self.eng.snap((self.t + turns) * step.unit - step.back)
        return self.counts[key]

    def now(self, step):
        return self.count(step, 1 - step.stage)

    def prev(self, step):
        return self.count(step, -step.stage)

    def apart(self):
        if self.loop:
            self.eng.sem_inc(self.passed, 1)


def turns(eng, passed, body):
    body(Turn(eng, -1, passed), True, False, False)
    body(Turn(eng, 0, passed), True, True, False)
    body(Turn(eng, 1, passed), True, True, True)
    with eng.Fori(2, PAIRS - 1) as t:
        body(Turn(eng, t, passed), True, True, True)
    body(Turn(eng, PAIRS - 1, passed), False, True, True)
    body(Turn(eng, PAIRS, passed), False, False, True)


def two_layer_graph_attention(nc, x, x_t, adj, weights, biases, row_biases, out):
    with ExitStack() as ctx:
        def sb(name, shape, dt=F32):
            return ctx.enter_context(nc.sbuf_tensor(name, shape, dt))

        def signal(name, stage, unit=1):
            return Signal(ctx.enter_context(nc.semaphore(name)), stage, unit)

        def pair_of(name, stage):
            sem = ctx.enter_context(nc.semaphore(name))
            return [Signal(sem, stage, 2, 1 - g) for g in range(2)]

        w_hi = {n: sb(f"{n}_hi", [128, C, D], F32R) for n in WEIGHTS}
        w_lo = {n: sb(f"{n}_lo", [128, C, D], F32R) for n in WEIGHTS}
        qk_bias = {n: sb(f"{n}_col", [128, C]) for n in ("bq", "bk")}
        rows = {n: sb(f"{n}_rows", [128, size]) for n, size in
                (("bv", D), ("bf", D), ("b1", E1), ("Hb", D), ("w_sd", 2 * D))}
        ident = sb("ident", [128, 128])
        ident_bf = sb("ident_bf", [128, 128], BF16)
        half_neg = sb("half_neg", [128, 1])

        xt_raw = sb("xt_raw", [128, C, 2 * N])
        xt_hi = sb("xt_hi", [128, C, 2 * N], F32R)
        xt_lo = sb("xt_lo", [128, C, 2 * N], F32R)
        x_raw = sb("x_raw", [128, 2, D])
        x_bf = sb("x_bf", [128, 2, D])
        adj0 = sb("adj0", [128, 2, N], U8)
        adj1 = sb("adj1", [128, 2, N], U8)
        mask0 = sb("mask0", [128, 2, N], BF16)
        mask1 = sb("mask1", [128, 2, N], BF16)
        q_hi = sb("q_hi", [128, C, 2 * N], F32R)
        q_lo = sb("q_lo", [128, C, 2 * N], F32R)
        k_hi = sb("k_hi", [128, C, 2, 2, N], F32R)
        k_lo = sb("k_lo", [128, C, 2, 2, N], F32R)
        v = sb("v", [128, 2, D])
        v_res = sb("v_res", [128, 2, D])
        v_part = [sb(f"v_part{i}", [128, 2, H0, E0 + 1], BF16) for i in range(3)]
        p0 = sb("p0", [128, 2, H0 * N])
        p0_max = sb("p0_max", [128, 2, H0])
        p0t_hi = sb("p0t_hi", [128, 2, H0 * N], F16)
        p0t_lo = sb("p0t_lo", [128, 2, H0 * N], F16)
        ctx_rcp = sb("ctx_rcp", [128, 2, H0])
        ctx_n = sb("ctx_n", [128, 2, D])
        ctx_hi = sb("ctx_hi", [128, 2, C, N], F32R)
        ctx_lo = sb("ctx_lo", [128, 2, C, N], F32R)
        y = sb("y", [128, 2, D])
        stats = sb("stats", [128, 2, 6])
        moments = sb("moments", [128, 2, 2])
        rstd = sb("rstd", [128, 2, 1])
        x1 = sb("x1", [128, 2, D])

        x1_kept = sb("x1_kept", [128, 2, D])
        x1t_hi = sb("x1t_hi", [128, 2, C, N], F32R)
        x1t_lo = sb("x1t_lo", [128, 2, C, N], F32R)
        th = sb("th", [128, 2, D])
        h_part = [sb(f"h_part{i}", [128, 2, H1, E1 + 1], BF16) for i in range(3)]
        h_res = sb("h_res", [128, 2, D])
        prod = sb("prod", [128, 2, 2 * D])
        sd = sb("sd", [128, 2, 2, H1])
        sd_res = sb("sd_res", [128, 2, 2, H1])
        sd_parts = sb("sd_parts", [128, 2, 2, 64], BF16)
        src_t = sb("src_t", [128, 2, N], BF16)
        dst_t = sb("dst_t", [128, 2, N], BF16)
        dst_row = sb("dst_row", [128, 2, H1, N], BF16)
        z = sb("z", [128, 2, H1 * N])
        z_max = sb("z_max", [128, 2, H1])
        p1t_hi = sb("p1t_hi", [128, 2, H1 * N], F16)
        p1t_lo = sb("p1t_lo", [128, 2, H1 * N], F16)
        f_rcp = sb("f_rcp", [128, 2, H1])
        f = sb("f", [128, 2, D])
        f_neg = sb("f_neg", [128, 2, D])
        gate = sb("gate", [128, 2, D])
        y2 = sb("y2", [128, 2, D])
        stats2 = sb("stats2", [128, 2, 6])
        moments2 = sb("moments2", [128, 2, 2])
        rstd2 = sb("rstd2", [128, 2, 1])
        out_tile = sb("out_tile", [128, 2, D])
        staging = {"Wq": p0[:, 0, :], "Wk": p0[:, 1, :]}
        stage_tile = {"Wq": z[:, 0, 0:C * D], "Wk": z[:, 1, 0:C * D]}

        lin = [ctx.enter_context(nc.psum_tensor(f"lin{i}", [128, 512], F32)) for i in range(2)]
        tp = [ctx.enter_context(nc.psum_tensor(f"tp{i}", [128, 512], F32)) for i in range(2)]
        zp = ctx.enter_context(nc.psum_tensor("zp", [128, 3, 512], F32))
        fp = ctx.enter_context(nc.psum_tensor("fp", [128, 512], F32))

        w_loaded = {n: signal(f"{n}_loaded", 0) for n in WEIGHTS}
        w_hi_ready = {n: signal(f"{n}_hi_ready", 0) for n in WEIGHTS}
        w_lo_ready = {n: signal(f"{n}_lo_ready", 0) for n in WEIGHTS}
        small_loaded = signal("small_loaded", 0)
        ones_ready = signal("ones_ready", 0)
        consts_ready = signal("consts_ready", 0)
        fills_ready = signal("fills_ready", 0)
        passed = ctx.enter_context(nc.semaphore("passed"))

        xt_loaded = signal("xt_loaded", -1, DONE_BY_DMA)
        x_loaded = signal("x_loaded", -1, DONE_BY_DMA)
        adj0_loaded = signal("adj0_loaded", -1, DONE_BY_DMA)
        xt_split = signal("xt_split", -1)
        xt_hi_made = signal("xt_hi_made", -1)
        adj1_loaded = signal("adj1_loaded", 0, DONE_BY_DMA)
        x_bf_ready = signal("x_bf_ready", 0)
        mask0_ready = signal("mask0_ready", 0)
        qk_mm = [signal(f"qk_mm{j}", 0) for j in range(C)]
        qk_hi = [signal(f"qk_hi{j}", 0) for j in range(C)]
        qk_lo = [signal(f"qk_lo{j}", 0) for j in range(C)]
        sc_mm, sc_max = pair_of("sc_mm", 0), pair_of("sc_max", 0)
        sc_sub, sc_exp = pair_of("sc_sub", 0), pair_of("sc_exp", 0)
        v_mm, v_add, v_r = pair_of("v_mm", 0), pair_of("v_add", 0), pair_of("v_r", 0)
        v_done = [pair_of(f"v_done{i}", 0) for i in range(3)]
        pt_mm = [pair_of(f"pt_mm{k}", 0) for k in range(2)]
        pt_hi = [pair_of(f"pt_hi{k}", 0) for k in range(2)]
        pt_lo = [pair_of(f"pt_lo{k}", 0) for k in range(2)]
        ctx_mm, ctx_inv, ctx_ready = pair_of("ctx_mm", 0), pair_of("ctx_inv", 0), pair_of("ctx_ready", 0)
        ct_mm, ct_hi, ct_lo = pair_of("ct_mm", 0), pair_of("ct_hi", 0), pair_of("ct_lo", 0)
        pr_mm, y_ready, y_stats = pair_of("pr_mm", 0), pair_of("y_ready", 0), pair_of("y_stats", 0)
        y_mom, y_var, y_rstd = pair_of("y_mom", 0), pair_of("y_var", 0), pair_of("y_rstd", 0)
        x1_ready = pair_of("x1_ready", 0)

        mask1_ready = signal("mask1_ready", 1)
        x1_copied = pair_of("x1_copied", 1)
        x1t_mm, x1t_h, x1t_l = pair_of("x1t_mm", 1), pair_of("x1t_h", 1), pair_of("x1t_l", 1)
        h_mm, h_tanh, h_r = pair_of("h_mm", 1), pair_of("h_tanh", 1), pair_of("h_r", 1)
        h_done = [pair_of(f"h_done{i}", 1) for i in range(3)]
        g_mm, g_add, g_tanh = pair_of("g_mm", 1), pair_of("g_add", 1), pair_of("g_tanh", 1)
        sd_prod, sd_sum = pair_of("sd_prod", 1), pair_of("sd_sum", 1)
        sd_1, sd_r, sd_2, sd_3 = (signal(f"sd_{i}", 1) for i in ("part1", "res", "part2", "part3"))
        sdt_mm, src_ready, dst_ready = signal("sdt_mm", 1), signal("src_ready", 1), signal("dst_ready", 1)
        dst_flat = [signal(f"dst_flat{g}", 1, 3 * DONE_BY_DMA) for g in range(2)]
        z_mm, z_maxed = pair_of("z_mm", 1), pair_of("z_maxed", 1)
        z_copied, z_leaky = pair_of("z_copied", 1), pair_of("z_leaky", 1)
        z_sub, z_exp = pair_of("z_sub", 1), pair_of("z_exp", 1)
        wt_mm = [pair_of(f"wt_mm{k}", 1) for k in range(3)]
        wt_hi = [pair_of(f"wt_hi{k}", 1) for k in range(3)]
        wt_lo = [pair_of(f"wt_lo{k}", 1) for k in range(3)]
        f_mm, f_inv, f_norm = pair_of("f_mm", 1), pair_of("f_inv", 1), pair_of("f_norm", 1)
        f_bias, f_min, f_exp = pair_of("f_bias", 1), pair_of("f_min", 1), pair_of("f_exp", 1)
        f_elu, f_diff, f_gated = pair_of("f_elu", 1), pair_of("f_diff", 1), pair_of("f_gated", 1)
        y2_ready, y2_stats, y2_mom = pair_of("y2_ready", 1), pair_of("y2_stats", 1), pair_of("y2_mom", 1)
        y2_var, y2_rstd, out_ready = pair_of("y2_var", 1), pair_of("y2_rstd", 1), pair_of("out_ready", 1)
        stored = [signal(f"stored{g}", 1, DONE_BY_DMA) for g in range(2)]

        xt_d = x_t
        x_d = x.rearrange("(t g) n d -> t n g d", g=2)
        adj_d = adj.rearrange("(t g) n m -> t n g m", g=2)
        out_d = out.rearrange("(t g) n d -> t n g d", g=2)

        block = ctx.enter_context(nc.Block())

        @block.sync
        def _(sp):
            sp.dma_start(z[:, 0, 0:C * D], weights["Wq"]).then_inc(w_loaded["Wq"].sem, 16)
            sp.dma_start(z[:, 1, 0:C * D], weights["Wk"]).then_inc(w_loaded["Wk"].sem, 16)
            for n in ("bq", "bk"):
                sp.dma_start(qk_bias[n][:, :], biases[n]).then_inc(small_loaded.sem, 16)
            for n in rows:
                sp.dma_start(rows[n][:, :], row_biases[n].partition_broadcast(128)).then_inc(small_loaded.sem, 16)
            for i, n in enumerate(WEIGHTS[2:]):
                before = WEIGHTS[i]
                sp.wait_ge(w_lo_ready[before].sem, 1)
                sp.dma_start(z[:, i % 2, 0:C * D], weights[n]).then_inc(w_loaded[n].sem, 16)

            def body(turn, prepare, layer0, layer1):
                now, prev, t = turn.now, turn.prev, turn.t
                if prepare:
                    sp.wait_ge(xt_split.sem, prev(xt_split))
                    turn.apart()
                    sp.dma_start(xt_raw[:, :, :], xt_d[t + 1]).then_inc(xt_loaded.sem, 16)
                    sp.wait_ge(x_bf_ready.sem, now(x_bf_ready))
                    turn.apart()
                    sp.dma_start(x_raw[:, :, :], x_d[t + 1]).then_inc(x_loaded.sem, 16)
                    sp.wait_ge(mask0_ready.sem, now(mask0_ready))
                    turn.apart()
                    sp.dma_start(adj0[:, :, :], adj_d[t + 1]).then_inc(adj0_loaded.sem, 16)
                if layer0:
                    sp.wait_ge(mask1_ready.sem, now(mask1_ready))
                    turn.apart()
                    sp.dma_start(adj1[:, :, :], adj_d[t]).then_inc(adj1_loaded.sem, 16)
                if layer1:
                    sp.wait_ge(dst_ready.sem, now(dst_ready))
                    for g in range(2):
                        sp.wait_ge(z_mm[g].sem, prev(z_mm[g]))
                        for part in range(3):
                            dma = sp.dma_start(dst_row[64 + part:65 + part, g, :, :],
                                               dst_t[64 + H1 * part:64 + H1 * (part + 1), g, :])
                            dma.then_inc(dst_flat[g].sem, 16)
                    for g in range(2):
                        sp.wait_ge(out_ready[g].sem, now(out_ready[g]))
                        turn.apart()
                        sp.dma_start(out_d[t - 1, :, g, :], out_tile[:, g, :]).then_inc(stored[g].sem, 16)

            turns(sp, passed, body)
            for g in range(2):
                sp.wait_ge(stored[g].sem, 16 * PAIRS)

        @block.tensor
        def _(pe):
            def product(bank, left_hi, left_lo, right_hi, right_lo):
                passes = [(left_hi, right_hi), (left_hi, right_lo), (left_lo, right_hi)]
                for k in range(C):
                    for i, (a, b) in enumerate(passes):
                        last = pe.matmul(bank, a(k), b(k), start=(k == 0 and i == 0), stop=(k == C - 1 and i == 2))
                return last

            def rows_product(bank, hi, lo, name, wait_weights):
                if wait_weights:
                    pe.wait_ge(w_hi_ready[name].sem, 1)
                    pe.wait_ge(w_lo_ready[name].sem, 1)
                return product(bank[:, 0:D], hi, lo, lambda k: w_hi[name][:, k, :], lambda k: w_lo[name][:, k, :])

            pe.wait_ge(consts_ready.sem, 4)

            def body(turn, prepare, layer0, layer1):
                now, prev, t = turn.now, turn.prev, turn.t
                first = not turn.loop and t == 0
                first1 = not turn.loop and t == 1

                def queries_keys(j):
                    if first:
                        for n in ("Wq", "Wk"):
                            pe.wait_ge(w_hi_ready[n].sem, 1)
                            pe.wait_ge(w_lo_ready[n].sem, 1)
                    if j == 0:
                        pe.wait_ge(xt_split.sem, prev(xt_split))
                    if j < 2:
                        pe.wait_ge(y_ready[1 - j].sem, prev(y_ready[1 - j]))
                    else:
                        pe.wait_ge(qk_hi[0].sem, now(qk_hi[0]))
                        pe.wait_ge(qk_lo[0].sem, now(qk_lo[0]))
                    for i, n in enumerate(("Wq", "Wk")):
                        last = product(lin[j % 2][:, 2 * N * i:2 * N * (i + 1)],
                                       lambda k: w_hi[n][:, k, 128 * j:128 * (j + 1)],
                                       lambda k: w_lo[n][:, k, 128 * j:128 * (j + 1)],
                                       lambda k: xt_hi[:, k, :], lambda k: xt_lo[:, k, :])
                    last.then_inc(qk_mm[j].sem, 1)

                def x1_transposes(g):
                    pe.wait_ge(x1_ready[g].sem, prev(x1_ready[g]))
                    if g == 0:
                        if not first1:
                            pe.wait_ge(wt_hi[2][1].sem, prev(wt_hi[2][1]))
                            pe.wait_ge(wt_lo[2][1].sem, prev(wt_lo[2][1]))
                        else:
                            pe.wait_ge(ct_hi[1].sem, prev(ct_hi[1]))
                            pe.wait_ge(ct_lo[1].sem, prev(ct_lo[1]))
                    else:
                        if not first1:
                            pe.wait_ge(wt_hi[1][1].sem, prev(wt_hi[1][1]))
                            pe.wait_ge(wt_lo[1][1].sem, prev(wt_lo[1][1]))
                        else:
                            pe.wait_ge(pt_hi[1][1].sem, prev(pt_hi[1][1]))
                            pe.wait_ge(pt_lo[1][1].sem, prev(pt_lo[1][1]))
                    for k in range(C):
                        last = pe.transpose(tp[g][:, 128 * k:128 * (k + 1)], x1[:, g, 128 * k:128 * (k + 1)], ident[:, :])
                    last.then_inc(x1t_mm[g].sem, 1)

                def hidden(g):
                    if g == 0:
                        if layer0:
                            pe.wait_ge(qk_hi[1].sem, now(qk_hi[1]))
                            pe.wait_ge(qk_lo[1].sem, now(qk_lo[1]))
                        else:
                            pe.wait_ge(y_ready[0].sem, prev(y_ready[0]))
                    else:
                        if layer0:
                            pe.wait_ge(qk_hi[2].sem, now(qk_hi[2]))
                            pe.wait_ge(qk_lo[2].sem, now(qk_lo[2]))
                        else:
                            pe.wait_ge(y_ready[1].sem, prev(y_ready[1]))
                    pe.wait_ge(x1t_h[g].sem, now(x1t_h[g]))
                    pe.wait_ge(x1t_l[g].sem, now(x1t_l[g]))
                    rows_product(lin[1 - g], lambda k: x1t_hi[:, g, k, :], lambda k: x1t_lo[:, g, k, :],
                                 "W1", first1 and g == 0).then_inc(h_mm[g].sem, 1)

                def values(g):
                    if layer1:
                        pe.wait_ge(h_tanh[g].sem, now(h_tanh[g]))
                        pe.wait_ge(h_done[0][g].sem, now(h_done[0][g]))
                        pe.wait_ge(h_r[g].sem, now(h_r[g]))
                    else:
                        pe.wait_ge(qk_hi[1 + g].sem, now(qk_hi[1 + g]))
                        pe.wait_ge(qk_lo[1 + g].sem, now(qk_lo[1 + g]))
                    rows_product(lin[1 - g], lambda k: xt_hi[:, k, N * g:N * (g + 1)],
                                 lambda k: xt_lo[:, k, N * g:N * (g + 1)], "Wv", first and g == 0)\
                        .then_inc(v_mm[g].sem, 1)

                def gate_rows(g):
                    if layer0:
                        pe.wait_ge(v_add[g].sem, now(v_add[g]))
                    else:
                        pe.wait_ge(h_tanh[g].sem, now(h_tanh[g]))
                        pe.wait_ge(h_done[0][g].sem, now(h_done[0][g]))
                        pe.wait_ge(h_r[g].sem, now(h_r[g]))
                    rows_product(lin[1 - g], lambda k: x1t_hi[:, g, k, :], lambda k: x1t_lo[:, g, k, :],
                                 "Hw", first1 and g == 0).then_inc(g_mm[g].sem, 1)

                def source_target_transposes():
                    pe.wait_ge(sd_3.sem, now(sd_3))
                    pe.wait_ge(x1t_h[0].sem, now(x1t_h[0]))
                    pe.wait_ge(x1t_l[0].sem, now(x1t_l[0]))
                    for g in range(2):
                        last = pe.transpose(tp[0][:, :].bitcast(BF16)[:, N * g:N * (g + 1)],
                                            sd_parts[:, g, :, :].rearrange("p a b -> p (a b)"), ident_bf[:, :])
                    last.then_inc(sdt_mm.sem, 1)

                def scores(g):
                    if g == 0:
                        if not first1:
                            pe.wait_ge(z_copied[1].sem, prev(z_copied[1]))
                        else:
                            pe.wait_ge(sc_sub[1].sem, prev(sc_sub[1]))
                        pe.wait_ge(mask0_ready.sem, now(mask0_ready))
                        for step in qk_hi:
                            pe.wait_ge(step.sem, now(step))
                        for step in qk_lo:
                            pe.wait_ge(step.sem, now(step))
                    elif layer1:
                        pe.wait_ge(z_copied[0].sem, now(z_copied[0]))
                    else:
                        pe.wait_ge(sc_sub[0].sem, now(sc_sub[0]))
                    m = mask0[:, g:g + 1, :]
                    pe.matmul(zp[:, 0, :], ident_bf[:, :], m.to_broadcast([128, 4, N]), start=True, stop=True)
                    pe.matmul(zp[:, 1, 0:2 * N], ident_bf[:, :], m.to_broadcast([128, 2, N]), start=True, stop=True)
                    for j in range(C):
                        o = zp[:, j // 2, 2 * N * (j % 2):2 * N * (j % 2) + 2 * N]
                        qh, ql = q_hi[:, j, N * g:N * (g + 1)], q_lo[:, j, N * g:N * (g + 1)]
                        kh = k_hi[:, j, g, :, :].rearrange("p a n -> p (a n)")
                        kl = k_lo[:, j, g, :, :].rearrange("p a n -> p (a n)")
                        pe.matmul(o, qh, kh, start=False, stop=False, skip_group_check=True)
                        pe.matmul(o, qh, kl, start=False, stop=False, skip_group_check=True)
                        last = pe.matmul(o, ql, kh, start=False, stop=True, skip_group_check=True)
                    last.then_inc(sc_mm[g].sem, 1)

                def weights0_transposes(g):
                    pe.wait_ge(sc_exp[g].sem, now(sc_exp[g]))
                    for half in range(2):
                        bank = tp[1 - half] if g == 0 else tp[half]
                        if g == 0 and half == 0:
                            pe.wait_ge(x1t_h[1].sem, now(x1t_h[1]))
                            pe.wait_ge(x1t_l[1].sem, now(x1t_l[1]))
                        elif g == 0 and layer1:
                            pe.wait_ge(dst_ready.sem, now(dst_ready))
                        elif g == 1 and half == 0:
                            pe.wait_ge(pt_hi[1][0].sem, now(pt_hi[1][0]))
                            pe.wait_ge(pt_lo[1][0].sem, now(pt_lo[1][0]))
                        elif g == 1:
                            pe.wait_ge(ct_hi[0].sem, now(ct_hi[0]))
                            pe.wait_ge(ct_lo[0].sem, now(ct_lo[0]))
                        for i in range(3):
                            c = N * (3 * half + i)
                            last = pe.transpose(bank[:, N * i:N * (i + 1)], p0[:, g, c:c + N], ident[:, :])
                        last.then_inc(pt_mm[half][g].sem, 1)

                def attend0(g):
                    if g:
                        pe.wait_ge(ctx_ready[0].sem, now(ctx_ready[0]))
                    else:
                        if not first1:
                            pe.wait_ge(f_norm[1].sem, prev(f_norm[1]))
                        else:
                            pe.wait_ge(ctx_ready[1].sem, prev(ctx_ready[1]))
                    pe.wait_ge(v_done[0][g].sem, now(v_done[0][g]))
                    pe.wait_ge(v_done[1][g].sem, now(v_done[1][g]))
                    pe.wait_ge(v_done[2][g].sem, now(v_done[2][g]))
                    for h in range(H0):
                        if h % 3 == 0:
                            pe.wait_ge(pt_hi[h // 3][g].sem, now(pt_hi[h // 3][g]))
                            pe.wait_ge(pt_lo[h // 3][g].sem, now(pt_lo[h // 3][g]))
                        o = fp[:, (E0 + 1) * h:(E0 + 1) * (h + 1)]
                        hi, lo = p0t_hi[:, g, N * h:N * (h + 1)], p0t_lo[:, g, N * h:N * (h + 1)]
                        for i in range(3):
                            pe.matmul(o, hi, v_part[i][:, g, h, :], start=(h == 0 and i == 0), stop=False,
                                      skip_group_check=True)
                        for i in range(2):
                            last = pe.matmul(o, lo, v_part[i][:, g, h, :], start=False, stop=(i == 1),
                                             skip_group_check=True)
                    last.then_inc(ctx_mm[g].sem, 1)

                def context_transposes(g):
                    pe.wait_ge(ctx_ready[g].sem, now(ctx_ready[g]))
                    bank = tp[1 - g]
                    pe.wait_ge(pt_hi[0][g].sem, now(pt_hi[0][g]))
                    pe.wait_ge(pt_lo[0][g].sem, now(pt_lo[0][g]))
                    for k in range(C):
                        last = pe.transpose(bank[:, 128 * k:128 * (k + 1)], ctx_n[:, g, 128 * k:128 * (k + 1)], ident[:, :])
                    last.then_inc(ct_mm[g].sem, 1)

                def project(g):
                    pe.wait_ge(ct_hi[g].sem, now(ct_hi[g]))
                    pe.wait_ge(ct_lo[g].sem, now(ct_lo[g]))
                    if layer1:
                        pe.wait_ge(g_add[g].sem, now(g_add[g]))
                    else:
                        pe.wait_ge(v_add[g].sem, now(v_add[g]))
                    rows_product(lin[1 - g], lambda k: ctx_hi[:, g, k, :], lambda k: ctx_lo[:, g, k, :],
                                 "Wf", first and g == 0).then_inc(pr_mm[g].sem, 1)

                def attention1(g):
                    if g == 0:
                        pe.wait_ge(src_ready.sem, now(src_ready))
                        pe.wait_ge(mask1_ready.sem, now(mask1_ready))
                        if layer0:
                            pe.wait_ge(sc_sub[0].sem, now(sc_sub[0]))
                        else:
                            pe.wait_ge(z_copied[1].sem, prev(z_copied[1]))
                    else:
                        if layer0:
                            pe.wait_ge(sc_sub[1].sem, now(sc_sub[1]))
                        else:
                            pe.wait_ge(z_copied[0].sem, now(z_copied[0]))
                    m = mask1[:, g:g + 1, :].to_broadcast([128, 4, N])
                    for b in range(3):
                        pe.matmul(zp[:, b, :], ident_bf[:, :], m, start=True, stop=False)
                    flat(g)
                    flat_rows = dst_row[0:67, g, :, :].rearrange("p a n -> p (a n)")
                    for b in range(3):
                        last = pe.matmul(zp[:, b, :], src_t[0:67, g, :], flat_rows[:, 512 * b:512 * (b + 1)],
                                         start=False, stop=True)
                    last.then_inc(z_mm[g].sem, 1)

                def flat(g):
                    pe.wait_ge(dst_flat[g].sem, now(dst_flat[g]))

                def weights1_transposes(g, k):
                    bank = tp[(1, 0, 1)[k] if g == 0 else (0, 1, 0)[k]]
                    if k == 0:
                        pe.wait_ge(z_exp[g].sem, now(z_exp[g]))
                    if g == 0 and k == 0:
                        if layer0:
                            pe.wait_ge(pt_hi[1][1].sem, now(pt_hi[1][1]))
                            pe.wait_ge(pt_lo[1][1].sem, now(pt_lo[1][1]))
                        else:
                            pe.wait_ge(x1t_h[1].sem, now(x1t_h[1]))
                            pe.wait_ge(x1t_l[1].sem, now(x1t_l[1]))
                    elif g == 0 and k == 1:
                        if layer0:
                            pe.wait_ge(ct_hi[1].sem, now(ct_hi[1]))
                            pe.wait_ge(ct_lo[1].sem, now(ct_lo[1]))
                        else:
                            pe.wait_ge(dst_ready.sem, now(dst_ready))
                    elif g == 0:
                        pe.wait_ge(wt_hi[0][0].sem, now(wt_hi[0][0]))
                        pe.wait_ge(wt_lo[0][0].sem, now(wt_lo[0][0]))
                    elif k == 0:
                        pe.wait_ge(wt_hi[1][0].sem, now(wt_hi[1][0]))
                        pe.wait_ge(wt_lo[1][0].sem, now(wt_lo[1][0]))
                    elif k == 1:
                        pe.wait_ge(wt_hi[2][0].sem, now(wt_hi[2][0]))
                        pe.wait_ge(wt_lo[2][0].sem, now(wt_lo[2][0]))
                    else:
                        pe.wait_ge(wt_hi[0][1].sem, now(wt_hi[0][1]))
                        pe.wait_ge(wt_lo[0][1].sem, now(wt_lo[0][1]))
                    for i in range(4):
                        c = N * (4 * k + i)
                        last = pe.transpose(bank[:, N * i:N * (i + 1)], z[:, g, c:c + N], ident[:, :])
                    last.then_inc(wt_mm[k][g].sem, 1)

                def attend1(g, k):
                    if k == 0:
                        if g:
                            pe.wait_ge(f_norm[0].sem, now(f_norm[0]))
                        else:
                            if layer0:
                                pe.wait_ge(ctx_ready[1].sem, now(ctx_ready[1]))
                            else:
                                pe.wait_ge(f_norm[1].sem, prev(f_norm[1]))
                        pe.wait_ge(h_done[0][g].sem, now(h_done[0][g]))
                        pe.wait_ge(h_done[1][g].sem, now(h_done[1][g]))
                        pe.wait_ge(h_done[2][g].sem, now(h_done[2][g]))
                    pe.wait_ge(wt_hi[k][g].sem, now(wt_hi[k][g]))
                    pe.wait_ge(wt_lo[k][g].sem, now(wt_lo[k][g]))
                    for h in range(4 * k, 4 * k + 4):
                        o = fp[:, (E1 + 1) * h:(E1 + 1) * (h + 1)]
                        hi, lo = p1t_hi[:, g, N * h:N * (h + 1)], p1t_lo[:, g, N * h:N * (h + 1)]
                        for i in range(3):
                            pe.matmul(o, hi, h_part[i][:, g, h, :], start=(h == 0 and i == 0), stop=False,
                                      skip_group_check=True)
                        for i in range(2):
                            last = pe.matmul(o, lo, h_part[i][:, g, h, :], start=False, stop=(i == 1),
                                             skip_group_check=True)
                    if k == 2:
                        last.then_inc(f_mm[g].sem, 1)

                if layer0:
                    queries_keys(0)
                    queries_keys(1)
                if layer1:
                    x1_transposes(0)
                    x1_transposes(1)
                if layer0:
                    queries_keys(2)
                if layer1:
                    hidden(0)
                    hidden(1)
                if layer0:
                    values(0)
                    values(1)
                if layer1:
                    gate_rows(0)
                if layer0:
                    scores(0)
                if layer1:
                    source_target_transposes()
                    gate_rows(1)
                    attention1(0)
                if layer0:
                    weights0_transposes(0)
                    attend0(0)
                    context_transposes(0)
                    scores(1)
                    project(0)
                if layer1:
                    attention1(1)
                if layer0:
                    weights0_transposes(1)
                    attend0(1)
                    context_transposes(1)
                if layer1:
                    weights1_transposes(0, 0)
                    weights1_transposes(0, 1)
                    attend1(0, 0)
                    weights1_transposes(0, 2)
                    attend1(0, 1)
                    attend1(0, 2)
                if layer0:
                    project(1)
                if layer1:
                    weights1_transposes(1, 0)
                    weights1_transposes(1, 1)
                    attend1(1, 0)
                    weights1_transposes(1, 2)
                    attend1(1, 1)
                    attend1(1, 2)

            turns(pe, passed, body)

        @block.scalar
        def _(act):
            for i, n in enumerate(WEIGHTS):
                act.wait_ge(w_loaded[n].sem, 16)
                act.activation(w_hi[n][:, :, :].rearrange("p c d -> p (c d)"), z[:, i % 2, 0:C * D], ACT.Copy)\
                    .then_inc(w_hi_ready[n].sem, 1)

            act.wait_ge(small_loaded.sem, 16 * 7)
            act.wait_ge(fills_ready.sem, 1)

            def body(turn, prepare, layer0, layer1):
                now, prev = turn.now, turn.prev

                def queries_keys(j):
                    act.wait_ge(qk_mm[j].sem, now(qk_mm[j]))
                    if j == 0:
                        act.wait_ge(sc_mm[1].sem, prev(sc_mm[1]))
                    act.activation(q_hi[:, j, :], lin[j % 2][:, 0:2 * N], ACT.Identity, bias=qk_bias["bq"][:, j:j + 1])
                    for half in range(2):
                        p = slice(64 * half, 64 * half + 64)
                        last = act.activation(k_hi[p, j, :, half, :],
                                              lin[j % 2][p, 2 * N:4 * N].rearrange("p (g n) -> p g n", g=2),
                                              ACT.Identity, bias=qk_bias["bk"][p, j:j + 1])
                    last.then_inc(qk_hi[j].sem, 1)

                def x1_high(g):
                    act.wait_ge(x1t_mm[g].sem, now(x1t_mm[g]))
                    act.wait_ge(g_mm[g].sem, prev(g_mm[g]))
                    act.activation(x1t_hi[:, g, :, :].rearrange("p c n -> p (c n)"), tp[g][:, 0:D], ACT.Copy)\
                        .then_inc(x1t_h[g].sem, 1)

                def hidden(g):
                    act.wait_ge(h_mm[g].sem, now(h_mm[g]))
                    act.wait_ge(f_mm[g].sem, prev(f_mm[g]))
                    act.wait_ge(sd_prod[g].sem, prev(sd_prod[g]))
                    act.activation(th[:, g, :], lin[1 - g][:, 0:D], ACT.Tanh).then_inc(h_tanh[g].sem, 1)
                    act.activation(h_part[0][:, g, :, 0:E1], lin[1 - g][:, 0:D].rearrange("p (a e) -> p a e", a=H1),
                                   ACT.Copy).then_inc(h_done[0][g].sem, 1)

                def hidden_part2(g):
                    act.wait_ge(h_r[g].sem, now(h_r[g]))
                    act.activation(h_part[1][:, g, :, 0:E1], h_res[:, g, :].rearrange("p (a e) -> p a e", a=H1),
                                   ACT.Copy).then_inc(h_done[1][g].sem, 1)

                def value_part1(g):
                    act.wait_ge(v_add[g].sem, now(v_add[g]))
                    act.wait_ge(ctx_mm[g].sem, prev(ctx_mm[g]))
                    act.activation(v_part[0][:, g, :, 0:E0], v[:, g, :].rearrange("p (a e) -> p a e", a=H0),
                                   ACT.Copy).then_inc(v_done[0][g].sem, 1)

                def value_part2(g):
                    act.wait_ge(v_r[g].sem, now(v_r[g]))
                    act.activation(v_part[1][:, g, :, 0:E0], v_res[:, g, :].rearrange("p (a e) -> p a e", a=H0),
                                   ACT.Copy).then_inc(v_done[1][g].sem, 1)

                def source_copy():
                    act.wait_ge(sdt_mm.sem, now(sdt_mm))
                    act.wait_ge(z_mm[1].sem, prev(z_mm[1]))
                    act.activation(src_t[0:36, :, :].rearrange("p g n -> p (g n)"),
                                   tp[0][:, :].bitcast(BF16)[0:36, 0:2 * N], ACT.Copy).then_inc(src_ready.sem, 1)

                def gate_tanh(g):
                    act.wait_ge(g_add[g].sem, now(g_add[g]))
                    act.activation(gate[:, g, :], gate[:, g, :], ACT.Tanh, scale=0.5).then_inc(g_tanh[g].sem, 1)

                def scores_exp(g):
                    act.wait_ge(sc_sub[g].sem, now(sc_sub[g]))
                    act.activation(p0[:, g, :], p0[:, g, :], ACT.Exp, scale=SCALE0).then_inc(sc_exp[g].sem, 1)

                def z_copy(g):
                    act.wait_ge(z_mm[g].sem, now(z_mm[g]))
                    act.wait_ge(wt_mm[2][g].sem, prev(wt_mm[2][g]))
                    act.activation(z[:, g, :], zp[:, :, :].rearrange("p b n -> p (b n)"), ACT.Copy)\
                        .then_inc(z_copied[g].sem, 1)

                def weights0_high(g, half):
                    bank = tp[1 - half] if g == 0 else tp[half]
                    act.wait_ge(pt_mm[half][g].sem, now(pt_mm[half][g]))
                    act.activation(p0t_hi[:, g, 3 * N * half:3 * N * (half + 1)], bank[:, 0:3 * N], ACT.Copy,
                                   scale=PSCALE).then_inc(pt_hi[half][g].sem, 1)

                def context_high(g):
                    act.wait_ge(ct_mm[g].sem, now(ct_mm[g]))
                    act.activation(ctx_hi[:, g, :, :].rearrange("p c n -> p (c n)"), tp[1 - g][:, 0:D], ACT.Copy)\
                        .then_inc(ct_hi[g].sem, 1)

                def z_exponent(g):
                    act.wait_ge(z_sub[g].sem, now(z_sub[g]))
                    act.activation(z[:, g, :], z[:, g, :], ACT.Exp).then_inc(z_exp[g].sem, 1)

                def weights1_high(g, k):
                    bank = tp[(1, 0, 1)[k] if g == 0 else (0, 1, 0)[k]]
                    act.wait_ge(wt_mm[k][g].sem, now(wt_mm[k][g]))
                    act.activation(p1t_hi[:, g, 4 * N * k:4 * N * (k + 1)], bank[:, :], ACT.Copy,
                                   scale=PSCALE).then_inc(wt_hi[k][g].sem, 1)

                def elu_exp(g):
                    act.wait_ge(f_min[g].sem, now(f_min[g]))
                    act.activation(f_neg[:, g, :], f_neg[:, g, :], ACT.Exp).then_inc(f_exp[g].sem, 1)

                if layer0:
                    queries_keys(0)
                    queries_keys(1)
                if layer1:
                    x1_high(0)
                    x1_high(1)
                if layer0:
                    queries_keys(2)
                if layer1:
                    hidden(0)
                    hidden(1)
                    hidden_part2(0)
                if layer0:
                    value_part1(0)
                if layer1:
                    hidden_part2(1)
                if layer0:
                    value_part1(1)
                    value_part2(0)
                if layer1:
                    gate_tanh(0)
                if layer0:
                    value_part2(1)
                if layer1:
                    source_copy()
                if layer0:
                    scores_exp(0)
                if layer1:
                    gate_tanh(1)
                    z_copy(0)
                if layer0:
                    weights0_high(0, 0)
                    weights0_high(0, 1)
                    context_high(0)
                    scores_exp(1)
                if layer1:
                    z_copy(1)
                if layer0:
                    weights0_high(1, 0)
                    weights0_high(1, 1)
                if layer1:
                    z_exponent(0)
                if layer0:
                    context_high(1)
                if layer1:
                    for k in range(3):
                        weights1_high(0, k)
                    z_exponent(1)
                    elu_exp(0)
                    for k in range(3):
                        weights1_high(1, k)
                    elu_exp(1)

            turns(act, passed, body)

        @block.vector
        def _(dve):
            dve.memset(src_t[:, :, :], 0.0).then_inc(ones_ready.sem, 1)
            dve.memset(dst_row[:, :, :, :].rearrange("p g a n -> p (g a n)"), 0.0).then_inc(ones_ready.sem, 1)
            dve.wait_ge(ones_ready.sem, 4)
            dve.memset(src_t[64:67, :, :], 1.0).then_inc(consts_ready.sem, 1)
            dve.memset(k_hi[:, :, :, :, :].rearrange("p a b c n -> p (a b c n)").bitcast(F32), 0.0)
            dve.memset(k_lo[:, :, :, :, :].rearrange("p a b c n -> p (a b c n)").bitcast(F32), 0.0)
            for i in range(3):
                dve.memset(v_part[i][:, :, :, E0:], 1.0 if i == 0 else 0.0)
                dve.memset(h_part[i][:, :, :, E1:], 1.0 if i == 0 else 0.0)
            dve.memset(sd_parts[:, :, :, :], 0.0)
            dve.memset(half_neg[:, :], -0.5).then_inc(fills_ready.sem, 1)
            for i, n in enumerate(WEIGHTS):
                dve.wait_ge(w_hi_ready[n].sem, 1)
                dve.tensor_tensor(w_lo[n][:, :, :].rearrange("p c d -> p (c d)"), z[:, i % 2, 0:C * D],
                                  w_hi[n][:, :, :].rearrange("p c d -> p (c d)").bitcast(F32), ALU.subtract)\
                    .then_inc(w_lo_ready[n].sem, 1)
            dve.wait_ge(small_loaded.sem, 16 * 7)
            dve.wait_ge(fills_ready.sem, 1)

            def body(turn, prepare, layer0, layer1):
                now, prev = turn.now, turn.prev

                def queries_keys(j):
                    dve.wait_ge(qk_hi[j].sem, now(qk_hi[j]))
                    if j == 0:
                        dve.wait_ge(sc_mm[1].sem, prev(sc_mm[1]))
                    dve.scalar_tensor_tensor(out=q_lo[:, j, :], in0=lin[j % 2][:, 0:2 * N],
                                             scalar=qk_bias["bq"][:, j:j + 1], in1=q_hi[:, j, :].bitcast(F32),
                                             op0=ALU.add, op1=ALU.subtract)
                    for half in range(2):
                        p = slice(64 * half, 64 * half + 64)
                        last = dve.scalar_tensor_tensor(
                            out=k_lo[p, j, :, half, :],
                            in0=lin[j % 2][p, 2 * N:4 * N].rearrange("p (g n) -> p g n", g=2),
                            scalar=qk_bias["bk"][p, j:j + 1], in1=k_hi[p, j, :, half, :].bitcast(F32),
                            op0=ALU.add, op1=ALU.subtract)
                    last.then_inc(qk_lo[j].sem, 1)

                def x1_low(g):
                    dve.wait_ge(x1t_h[g].sem, now(x1t_h[g]))
                    dve.wait_ge(g_mm[g].sem, prev(g_mm[g]))
                    dve.tensor_tensor(x1t_lo[:, g, :, :].rearrange("p c n -> p (c n)"), tp[g][:, 0:D],
                                      x1t_hi[:, g, :, :].rearrange("p c n -> p (c n)").bitcast(F32), ALU.subtract)\
                        .then_inc(x1t_l[g].sem, 1)

                def hidden_residue(g):
                    dve.wait_ge(h_done[0][g].sem, now(h_done[0][g]))
                    dve.wait_ge(h_done[2][g].sem, prev(h_done[2][g]))
                    dve.tensor_tensor(h_res[:, g, :].rearrange("p (a e) -> p a e", a=H1),
                                      lin[1 - g][:, 0:D].rearrange("p (a e) -> p a e", a=H1),
                                      h_part[0][:, g, :, 0:E1], ALU.subtract).then_inc(h_r[g].sem, 1)

                def value_bias(g):
                    dve.wait_ge(v_mm[g].sem, now(v_mm[g]))
                    dve.wait_ge(v_r[g].sem, prev(v_r[g]))
                    dve.tensor_tensor(v[:, g, :], lin[1 - g][:, 0:D], rows["bv"][:, :], ALU.add)\
                        .then_inc(v_add[g].sem, 1)

                def source_target_sums(g):
                    dve.wait_ge(sd_prod[g].sem, now(sd_prod[g]))
                    dve.tensor_reduce(sd[:, g, :, :], prod[:, g, :].rearrange("p (s a e) -> p s a e", s=2, a=H1),
                                      AX.X, ALU.add).then_inc(sd_sum[g].sem, 1)

                def source_target_parts():
                    def part(i):
                        return sd_parts[:, :, :, H1 * i:H1 * (i + 1)]
                    dve.wait_ge(sd_sum[0].sem, now(sd_sum[0]))
                    dve.wait_ge(sd_sum[1].sem, now(sd_sum[1]))
                    dve.wait_ge(sdt_mm.sem, prev(sdt_mm))
                    for g in range(2):
                        last = dve.tensor_copy(sd_parts[:, g, :, 0:H1], sd[:, g, :, :])
                    last.then_inc(sd_1.sem, 1)
                    dve.wait_ge(sd_1.sem, now(sd_1))
                    for g in range(2):
                        last = dve.tensor_tensor(sd_res[:, g, :, :], sd[:, g, :, :], sd_parts[:, g, :, 0:H1], ALU.subtract)
                    last.then_inc(sd_r.sem, 1)
                    dve.wait_ge(sd_r.sem, now(sd_r))
                    for g in range(2):
                        last = dve.tensor_copy(sd_parts[:, g, :, H1:2 * H1], sd_res[:, g, :, :])
                    last.then_inc(sd_2.sem, 1)
                    dve.wait_ge(sd_2.sem, now(sd_2))
                    for g in range(2):
                        last = dve.tensor_tensor(sd_parts[:, g, :, 2 * H1:3 * H1], sd_res[:, g, :, :],
                                                 sd_parts[:, g, :, H1:2 * H1], ALU.subtract)
                    last.then_inc(sd_3.sem, 1)

                def gate_bias(g):
                    dve.wait_ge(g_mm[g].sem, now(g_mm[g]))
                    dve.wait_ge(f_gated[g].sem, prev(f_gated[g]))
                    dve.tensor_tensor(gate[:, g, :], lin[1 - g][:, 0:D], rows["Hb"][:, :], ALU.add)\
                        .then_inc(g_add[g].sem, 1)

                def target_copy():
                    dve.wait_ge(src_ready.sem, now(src_ready))
                    for step in dst_flat:
                        dve.wait_ge(step.sem, prev(step))
                    dve.tensor_copy(dst_t[64:100, :, :].rearrange("p g n -> p (g n)"),
                                    tp[0][:, :].bitcast(BF16)[64:100, 0:2 * N]).then_inc(dst_ready.sem, 1)

                def scores_max(g):
                    dve.wait_ge(sc_mm[g].sem, now(sc_mm[g]))
                    s = zp[:, 0:2, :].rearrange("p b n -> p (b n)")[:, 0:H0 * N].rearrange("p (a n) -> p a n", a=H0)
                    dve.tensor_reduce(p0_max[:, g, :], s, AX.X, ALU.max).then_inc(sc_max[g].sem, 1)
                    dve.wait_ge(sc_max[g].sem, now(sc_max[g]))
                    dve.wait_ge(pt_mm[1][g].sem, prev(pt_mm[1][g]))
                    dve.tensor_tensor(p0[:, g, :].rearrange("p (a n) -> p a n", a=H0), s,
                                      p0_max[:, g, :].unsqueeze(2).to_broadcast([128, H0, N]), ALU.subtract)\
                        .then_inc(sc_sub[g].sem, 1)

                def weights0_low(g, half):
                    bank = tp[1 - half] if g == 0 else tp[half]
                    c = slice(3 * N * half, 3 * N * (half + 1))
                    dve.wait_ge(pt_hi[half][g].sem, now(pt_hi[half][g]))
                    dve.scalar_tensor_tensor(out=p0t_lo[:, g, c], in0=bank[:, 0:3 * N], scalar=PSCALE,
                                             in1=p0t_hi[:, g, c], op0=ALU.mult, op1=ALU.subtract)\
                        .then_inc(pt_lo[half][g].sem, 1)

                def context_norm(g):
                    dve.wait_ge(ctx_mm[g].sem, now(ctx_mm[g]))
                    s = fp[:, 0:H0 * (E0 + 1)].rearrange("p (a e) -> p a e", a=H0)
                    dve.reciprocal(ctx_rcp[:, g, :].unsqueeze(2), s[:, :, E0:]).then_inc(ctx_inv[g].sem, 1)
                    dve.wait_ge(ctx_inv[g].sem, now(ctx_inv[g]))
                    dve.tensor_tensor(ctx_n[:, g, :].rearrange("p (a e) -> p a e", a=H0), s[:, :, 0:E0],
                                      ctx_rcp[:, g, :].unsqueeze(2).to_broadcast([128, H0, E0]), ALU.mult)\
                        .then_inc(ctx_ready[g].sem, 1)

                def context_low(g):
                    dve.wait_ge(ct_hi[g].sem, now(ct_hi[g]))
                    dve.tensor_tensor(ctx_lo[:, g, :, :].rearrange("p c n -> p (c n)"), tp[1 - g][:, 0:D],
                                      ctx_hi[:, g, :, :].rearrange("p c n -> p (c n)").bitcast(F32), ALU.subtract)\
                        .then_inc(ct_lo[g].sem, 1)

                def residual0(g):
                    dve.wait_ge(pr_mm[g].sem, now(pr_mm[g]))
                    dve.wait_ge(x_bf_ready.sem, now(x_bf_ready))
                    dve.tensor_tensor(y[:, g, :], lin[1 - g][:, 0:D], x_bf[:, g, :], ALU.add).then_inc(y_ready[g].sem, 1)
                    dve.wait_ge(y_ready[g].sem, now(y_ready[g]))
                    dve.bn_stats(stats[:, g, :], y[:, g, :]).then_inc(y_stats[g].sem, 1)
                    dve.wait_ge(y_stats[g].sem, now(y_stats[g]))
                    turn.apart()
                    dve.bn_aggr(moments[:, g, :], stats[:, g, :]).then_inc(y_mom[g].sem, 1)
                    dve.wait_ge(y_mom[g].sem, now(y_mom[g]))
                    dve.tensor_scalar(rstd[:, g, :], moments[:, g, 1:2], EPS, None, ALU.add).then_inc(y_var[g].sem, 1)

                def norm0(g):
                    dve.wait_ge(y_rstd[g].sem, now(y_rstd[g]))
                    if layer1:
                        dve.wait_ge(x1t_mm[g].sem, now(x1t_mm[g]))
                        dve.wait_ge(x1_copied[g].sem, now(x1_copied[g]))
                    dve.tensor_scalar(x1[:, g, :], y[:, g, :], moments[:, g, 0:1], rstd[:, g, :],
                                      ALU.subtract, ALU.mult).then_inc(x1_ready[g].sem, 1)

                def z_leak(g):
                    dve.wait_ge(z_copied[g].sem, now(z_copied[g]))
                    dve.scalar_tensor_tensor(out=z[:, g, :], in0=z[:, g, :], scalar=0.2, in1=z[:, g, :],
                                             op0=ALU.mult, op1=ALU.max).then_inc(z_leaky[g].sem, 1)
                    dve.wait_ge(z_leaky[g].sem, now(z_leaky[g]))
                    dve.wait_ge(z_sub[g].sem, prev(z_sub[g]))
                    dve.tensor_reduce(z_max[:, g, :], z[:, g, :].rearrange("p (a n) -> p a n", a=H1),
                                      AX.X, ALU.max).then_inc(z_maxed[g].sem, 1)

                def weights1_low(g, k):
                    bank = tp[(1, 0, 1)[k] if g == 0 else (0, 1, 0)[k]]
                    c = slice(4 * N * k, 4 * N * (k + 1))
                    dve.wait_ge(wt_hi[k][g].sem, now(wt_hi[k][g]))
                    dve.scalar_tensor_tensor(out=p1t_lo[:, g, c], in0=bank[:, :], scalar=PSCALE,
                                             in1=p1t_hi[:, g, c], op0=ALU.mult, op1=ALU.subtract)\
                        .then_inc(wt_lo[k][g].sem, 1)

                def features_norm(g):
                    dve.wait_ge(f_mm[g].sem, now(f_mm[g]))
                    s = fp[:, 0:H1 * (E1 + 1)].rearrange("p (a e) -> p a e", a=H1)
                    dve.reciprocal(f_rcp[:, g, :].unsqueeze(2), s[:, :, E1:]).then_inc(f_inv[g].sem, 1)
                    dve.wait_ge(f_inv[g].sem, now(f_inv[g]))
                    dve.wait_ge(f_diff[g].sem, prev(f_diff[g]))
                    dve.tensor_tensor(f[:, g, :].rearrange("p (a e) -> p a e", a=H1), s[:, :, 0:E1],
                                      f_rcp[:, g, :].unsqueeze(2).to_broadcast([128, H1, E1]), ALU.mult)\
                        .then_inc(f_norm[g].sem, 1)

                def elu(g):
                    dve.wait_ge(f_exp[g].sem, now(f_exp[g]))
                    dve.scalar_tensor_tensor(out=f[:, g, :], in0=f_neg[:, g, :], scalar=-1.0, in1=f[:, g, :],
                                             op0=ALU.add, op1=ALU.max).then_inc(f_elu[g].sem, 1)

                def mix(g):
                    dve.wait_ge(f_diff[g].sem, now(f_diff[g]))
                    dve.wait_ge(g_tanh[g].sem, now(g_tanh[g]))
                    dve.scalar_tensor_tensor(out=f[:, g, :], in0=gate[:, g, :], scalar=1.0, in1=f[:, g, :],
                                             op0=ALU.add, op1=ALU.mult).then_inc(f_gated[g].sem, 1)
                    dve.wait_ge(f_gated[g].sem, now(f_gated[g]))
                    dve.scalar_tensor_tensor(out=y2[:, g, :], in0=f[:, g, :], scalar=0.25, in1=x1_kept[:, g, :],
                                             op0=ALU.mult, op1=ALU.add).then_inc(y2_ready[g].sem, 1)
                    dve.wait_ge(y2_ready[g].sem, now(y2_ready[g]))
                    dve.bn_stats(stats2[:, g, :], y2[:, g, :]).then_inc(y2_stats[g].sem, 1)
                    dve.wait_ge(y2_stats[g].sem, now(y2_stats[g]))
                    turn.apart()
                    dve.bn_aggr(moments2[:, g, :], stats2[:, g, :]).then_inc(y2_mom[g].sem, 1)
                    dve.wait_ge(y2_mom[g].sem, now(y2_mom[g]))
                    dve.tensor_scalar(rstd2[:, g, :], moments2[:, g, 1:2], EPS / 4, None, ALU.add)\
                        .then_inc(y2_var[g].sem, 1)

                def norm1(g):
                    dve.wait_ge(y2_rstd[g].sem, now(y2_rstd[g]))
                    dve.wait_ge(stored[g].sem, prev(stored[g]))
                    dve.tensor_scalar(out_tile[:, g, :], y2[:, g, :], moments2[:, g, 0:1], rstd2[:, g, :],
                                      ALU.subtract, ALU.mult).then_inc(out_ready[g].sem, 1)

                if layer0:
                    queries_keys(0)
                    queries_keys(1)
                if layer1:
                    x1_low(0)
                    x1_low(1)
                if layer0:
                    queries_keys(2)
                if layer1:
                    hidden_residue(0)
                    hidden_residue(1)
                if layer0:
                    value_bias(0)
                if layer1:
                    source_target_sums(0)
                if layer0:
                    value_bias(1)
                if layer1:
                    gate_bias(0)
                    source_target_sums(1)
                    source_target_parts()
                if layer0:
                    scores_max(0)
                if layer1:
                    target_copy()
                    gate_bias(1)
                    z_leak(0)
                if layer0:
                    weights0_low(0, 0)
                    weights0_low(0, 1)
                    context_norm(0)
                    context_low(0)
                    scores_max(1)
                    residual0(0)
                if layer1:
                    z_leak(1)
                if layer0:
                    norm0(0)
                    weights0_low(1, 0)
                    weights0_low(1, 1)
                    context_norm(1)
                    context_low(1)
                if layer1:
                    for k in range(3):
                        weights1_low(0, k)
                    features_norm(0)
                if layer0:
                    residual0(1)
                if layer1:
                    weights1_low(1, 0)
                    weights1_low(1, 1)
                if layer0:
                    norm0(1)
                if layer1:
                    weights1_low(1, 2)
                    elu(0)
                    features_norm(1)
                    mix(0)
                    elu(1)
                    norm1(0)
                    mix(1)
                    norm1(1)

            turns(dve, passed, body)

        @block.gpsimd
        def _(pool):
            pool.memset(ident[:, :], 1.0).then_inc(ones_ready.sem, 1)
            pool.memset(ident_bf[:, :], 1.0).then_inc(ones_ready.sem, 1)
            pool.wait_ge(ones_ready.sem, 4)
            for tile in (ident, ident_bf):
                pool.affine_select(out=tile[:, :], in_=tile[:, :], compare_op=ALU.is_equal, fill=0.0, base=0,
                                   pattern=[[-1, 128]], channel_multiplier=1).then_inc(consts_ready.sem, 1)
            for g in range(2):
                for part in range(3):
                    last = pool.affine_select(out=dst_row[0:36, g, :, :], in_=dst_row[0:36, g, :, :],
                                              compare_op=ALU.not_equal, fill=1.0, base=-H1 * part,
                                              pattern=[[-1, H1], [0, N]], channel_multiplier=1)
                    last.then_inc(ones_ready.sem, 1)
                    pool.wait_ge(ones_ready.sem, 5 + 3 * g + part)
            pool.memset(rstd[:, :, :], 1.0).then_inc(consts_ready.sem, 1)
            pool.wait_ge(small_loaded.sem, 16 * 7)
            pool.wait_ge(fills_ready.sem, 1)

            def body(turn, prepare, layer0, layer1):
                now, prev = turn.now, turn.prev

                def residual_bias():
                    for step in y_ready:
                        pool.wait_ge(step.sem, prev(step))
                    pool.wait_ge(x_loaded.sem, prev(x_loaded))
                    for g in range(2):
                        last = pool.tensor_tensor(x_bf[:, g, :], x_raw[:, g, :], rows["bf"][:, :], ALU.add)
                    last.then_inc(x_bf_ready.sem, 1)

                def mask(tile, raw, ready):
                    turn.apart()
                    pool.tensor_scalar(tile[:, :, :], raw[:, :, :], -1.0, MASKED, ALU.add, ALU.mult)\
                        .then_inc(ready.sem, 1)

                def keep_x1(g):
                    pool.wait_ge(x1_ready[g].sem, prev(x1_ready[g]))
                    pool.wait_ge(y2_ready[g].sem, prev(y2_ready[g]))
                    turn.apart()
                    pool.tensor_copy(x1_kept[:, g, :], x1[:, g, :]).then_inc(x1_copied[g].sem, 1)

                def source_target_products(g):
                    pool.wait_ge(h_tanh[g].sem, now(h_tanh[g]))
                    pool.wait_ge(sd_sum[g].sem, prev(sd_sum[g]))
                    pool.tensor_tensor(prod[:, g, :].rearrange("p (s d) -> p s d", s=2),
                                       th[:, g:g + 1, :].to_broadcast([128, 2, D]),
                                       rows["w_sd"][:, :].rearrange("p (s d) -> p s d", s=2), ALU.mult)\
                        .then_inc(sd_prod[g].sem, 1)

                def hidden_part3(g):
                    pool.wait_ge(h_done[1][g].sem, now(h_done[1][g]))
                    pool.wait_ge(f_mm[g].sem, prev(f_mm[g]))
                    pool.tensor_tensor(h_part[2][:, g, :, 0:E1], h_res[:, g, :].rearrange("p (a e) -> p a e", a=H1),
                                       h_part[1][:, g, :, 0:E1], ALU.subtract).then_inc(h_done[2][g].sem, 1)

                def value_residue(g):
                    pool.wait_ge(v_done[0][g].sem, now(v_done[0][g]))
                    pool.wait_ge(v_done[2][g].sem, prev(v_done[2][g]))
                    pool.tensor_tensor(v_res[:, g, :].rearrange("p (a e) -> p a e", a=H0),
                                       v[:, g, :].rearrange("p (a e) -> p a e", a=H0),
                                       v_part[0][:, g, :, 0:E0], ALU.subtract).then_inc(v_r[g].sem, 1)

                def value_part3(g):
                    pool.wait_ge(v_done[1][g].sem, now(v_done[1][g]))
                    pool.tensor_tensor(v_part[2][:, g, :, 0:E0], v_res[:, g, :].rearrange("p (a e) -> p a e", a=H0),
                                       v_part[1][:, g, :, 0:E0], ALU.subtract).then_inc(v_done[2][g].sem, 1)

                def split_next_x():
                    pool.wait_ge(xt_loaded.sem, now(xt_loaded))
                    pool.wait_ge(v_mm[1].sem, now(v_mm[1]))
                    turn.apart()
                    pool.tensor_copy(xt_hi[:, :, :].rearrange("p c n -> p (c n)"),
                                     xt_raw[:, :, :].rearrange("p c n -> p (c n)")).then_inc(xt_hi_made.sem, 1)
                    pool.wait_ge(xt_hi_made.sem, now(xt_hi_made))
                    pool.tensor_tensor(xt_lo[:, :, :].rearrange("p c n -> p (c n)"),
                                       xt_raw[:, :, :].rearrange("p c n -> p (c n)"),
                                       xt_hi[:, :, :].rearrange("p c n -> p (c n)").bitcast(F32), ALU.subtract)\
                        .then_inc(xt_split.sem, 1)

                def rstd_power(tile, g, var, ready):
                    pool.wait_ge(var[g].sem, now(var[g]))
                    pool.tensor_tensor(tile[:, g, :], tile[:, g, :], half_neg[:, :], ALU.pow).then_inc(ready[g].sem, 1)

                def z_subtract(g):
                    pool.wait_ge(z_maxed[g].sem, now(z_maxed[g]))
                    zs = z[:, g, :].rearrange("p (a n) -> p a n", a=H1)
                    pool.tensor_tensor(zs, zs, z_max[:, g, :].unsqueeze(2).to_broadcast([128, H1, N]), ALU.subtract)\
                        .then_inc(z_sub[g].sem, 1)

                def features_bias(g):
                    pool.wait_ge(f_norm[g].sem, now(f_norm[g]))
                    fs = f[:, g, :].rearrange("p (a e) -> p a e", a=H1)
                    pool.tensor_tensor(fs, fs, rows["b1"][:, :].unsqueeze(1).to_broadcast([128, H1, E1]), ALU.add)\
                        .then_inc(f_bias[g].sem, 1)
                    pool.wait_ge(f_bias[g].sem, now(f_bias[g]))
                    pool.wait_ge(f_elu[g].sem, prev(f_elu[g]))
                    turn.apart()
                    pool.tensor_scalar(f_neg[:, g, :], f[:, g, :], 0.0, None, ALU.min).then_inc(f_min[g].sem, 1)

                def features_difference(g):
                    pool.wait_ge(f_elu[g].sem, now(f_elu[g]))
                    pool.tensor_tensor(f[:, g, :], f[:, g, :], x1_kept[:, g, :], ALU.subtract).then_inc(f_diff[g].sem, 1)

                if layer0:
                    pool.wait_ge(adj0_loaded.sem, prev(adj0_loaded))
                    pool.wait_ge(sc_mm[1].sem, prev(sc_mm[1]))
                    mask(mask0, adj0, mask0_ready)
                if layer1:
                    keep_x1(0)
                    keep_x1(1)
                    pool.wait_ge(adj1_loaded.sem, prev(adj1_loaded))
                    pool.wait_ge(z_mm[1].sem, prev(z_mm[1]))
                    mask(mask1, adj1, mask1_ready)
                if layer0:
                    residual_bias()
                if layer1:
                    source_target_products(0)
                    source_target_products(1)
                if layer0:
                    value_residue(0)
                    value_residue(1)
                    value_part3(0)
                    value_part3(1)
                if layer1:
                    hidden_part3(0)
                    hidden_part3(1)
                    z_subtract(0)
                if prepare:
                    split_next_x()
                if layer0:
                    rstd_power(rstd, 0, y_var, y_rstd)
                if layer1:
                    z_subtract(1)
                    features_bias(0)
                if layer0:
                    rstd_power(rstd, 1, y_var, y_rstd)
                if layer1:
                    features_difference(0)
                    features_bias(1)
                    rstd_power(rstd2, 0, y2_var, y2_rstd)
                    features_difference(1)
                    rstd_power(rstd2, 1, y2_var, y2_rstd)

            turns(pool, passed, body)


def kernel(x, adj, L0_gnn_Wq, L0_gnn_bq, L0_gnn_Wk, L0_gnn_bk, L0_gnn_Wv, L0_gnn_bv, L0_gnn_Wf, L0_gnn_bf,
           L1_gnn_W, L1_gnn_b, L1_gnn_w_src, L1_gnn_w_dst, L1_gnn_H_w, L1_gnn_H_b):
    import numpy as np
    import concourse.bacc as bacc
    from concourse.bass_utils import run_bass_kernel_spmd

    nc = bacc.Bacc("TRN2", target_bir_lowering=False, num_devices=1)
    arrays = {}

    def given(name, a):
        a = np.ascontiguousarray(a)
        arrays[name] = a
        return nc.dram_tensor(name, a.shape, mybir.dt.from_np(a.dtype), kind="ExternalInput").ap()

    def chunked(a):
        return np.asarray(a).reshape(C, 128, D).transpose(1, 0, 2).reshape(128, C * D)

    x, adj = np.asarray(x), np.asarray(adj)
    x_d = given("x", x)
    x_t = given("x_t", x.reshape(PAIRS, 2 * N, C, 128).transpose(0, 3, 2, 1))
    adj_d = given("adj", adj)
    weights = {
        "Wq": given("Wq", chunked(L0_gnn_Wq)),
        "Wk": given("Wk", chunked(L0_gnn_Wk)),
        "Wv": given("Wv", chunked(L0_gnn_Wv)),
        "Wf": given("Wf", chunked(L0_gnn_Wf)),
        "W1": given("W1", chunked(np.asarray(L1_gnn_W).transpose(1, 0, 2).reshape(D, D))),
        "Hw": given("Hw", chunked(np.asarray(L1_gnn_H_w).T)),
    }
    biases = {
        "bq": given("bq", np.asarray(L0_gnn_bq).reshape(C, 128).T),
        "bk": given("bk", np.asarray(L0_gnn_bk).reshape(C, 128).T),
    }
    w_sd = np.concatenate([np.asarray(L1_gnn_w_src).reshape(D), np.asarray(L1_gnn_w_dst).reshape(D)])
    row_biases = {"bv": given("bv", L0_gnn_bv), "bf": given("bf", L0_gnn_bf), "b1": given("b1", L1_gnn_b),
                  "Hb": given("Hb", L1_gnn_H_b), "w_sd": given("w_sd", w_sd)}
    out = nc.dram_tensor("out", (GRAPHS, N, D), F32, kind="ExternalOutput").ap()
    two_layer_graph_attention(nc, x_d, x_t, adj_d, weights, biases, row_biases, out)
    r = run_bass_kernel_spmd(nc, [arrays], core_ids=[0])
    return r.results[0]["out"]
```

```python
from contextlib import ExitStack

import concourse.bass as bass
from concourse import mybir

F32 = mybir.dt.float32
F32R = mybir.dt.float32r
BF16 = mybir.dt.bfloat16
F16 = mybir.dt.float16
U8 = mybir.dt.uint8
ALU = mybir.AluOpType
ACT = mybir.ActivationFunctionType
AX = mybir.AxisListType

GRAPHS, N, D = 64, 128, 384
PAIRS = GRAPHS // 2
C = D // 128
H0 = 6
E0 = D // H0
H1 = 12
E1 = D // H1
EPS = 1e-5
SCALE0 = float(E0) ** -0.5
MASKED = 9e15 / SCALE0
PSCALE = 16384.0
WEIGHTS = ("Wq", "Wk", "Wv", "Wf", "W1", "Hw")
DONE_BY_DMA = 16
SMALL = 7


class Signal:

    def __init__(self, sem, stage, unit, back=0):
        self.sem, self.stage, self.unit, self.back = sem, stage, unit, back


class Turn:

    def __init__(self, eng, t, passed):
        self.eng, self.t, self.loop, self.counts, self.passed = eng, t, not isinstance(t, int), {}, passed

    def count(self, step, turns):
        if not self.loop:
            return max(min(self.t + turns, PAIRS) * step.unit - step.back, 0)
        key = turns, step.unit, step.back
        if key not in self.counts:
            self.counts[key] = self.eng.snap((self.t + turns) * step.unit - step.back)
        return self.counts[key]

    def now(self, step):
        return self.count(step, 1 - step.stage)

    def prev(self, step):
        return self.count(step, -step.stage)

    def runs(self, stage, back=0):
        return self.loop or 0 <= self.t - back - stage < PAIRS

    def apart(self):
        if self.loop:
            self.eng.sem_inc(self.passed, 1)


def turns(eng, passed, body):
    for t in range(-1, 3):
        body(Turn(eng, t, passed))
    with eng.Fori(3, PAIRS - 1) as t:
        body(Turn(eng, t, passed))
    for t in range(PAIRS - 1, PAIRS + 2):
        body(Turn(eng, t, passed))


LIN_USERS = ("v0", "qk0", "qk1", "qk2", "h0", "h1", "v1", "g0", "g1", "pr0", "pr1")
TP_USERS = ("wt01", "wt00", "wt02", "x1t0", "x1t1", "wt10", "wt12", "wt11", "sdt", "pt00", "pt01", "pt10",
             "pt11", "ct0", "ct1")
ZP_USERS = ("sc0", "sc1", "z0", "z1")
FP_USERS = ("f0", "f1", "ctx0", "ctx1")


def bank_of(users, user, banks=2):
    return users.index(user) % banks


def last_reader(turn, users, user, readers, banks=2):
    at, n = users.index(user), len(users)
    for back in range(1, 3 * n):
        i = (at - back) % n
        turns_back = (i + back - at) // n
        step = readers[users[i]]
        if i % banks == at % banks and turn.runs(step.stage, turns_back):
            return step, turn.count(step, 1 - step.stage - turns_back)
    return None


def two_layer_graph_attention(nc, x, x_t, adj, weights, biases, row_biases, out):
    with ExitStack() as ctx:
        def sb(name, shape, dt=F32):
            return ctx.enter_context(nc.sbuf_tensor(name, shape, dt))

        def signal(name, stage, unit=1):
            return Signal(ctx.enter_context(nc.semaphore(name)), stage, unit)

        def pair_of(name, stage):
            sem = ctx.enter_context(nc.semaphore(name))
            return [Signal(sem, stage, 2, 1 - g) for g in range(2)]

        w_hi = {n: sb(f"{n}_hi", [128, C, D], F32R) for n in WEIGHTS}
        w_lo = {n: sb(f"{n}_lo", [128, C, D], F32R) for n in WEIGHTS}
        qk_bias = {n: sb(f"{n}_col", [128, C]) for n in ("bq", "bk")}
        rows = {n: sb(f"{n}_rows", [128, size]) for n, size in
                (("bf", D), ("b1", E1), ("w_sd", 2 * D))}
        ident = sb("ident", [128, 128])
        ident_bf = sb("ident_bf", [128, 128], BF16)
        half_neg = sb("half_neg", [128, 1])
        bias_rows = sb("bias_rows", [3, 2, D], BF16)
        ones_bf = sb("ones_bf", [3, 128], BF16)

        xt_raw = sb("xt_raw", [128, C, 2 * N])
        xt_hi = sb("xt_hi", [128, C, 2 * N], F32R)
        xt_lo = sb("xt_lo", [128, C, 2 * N], F32R)
        x_raw = sb("x_raw", [128, 2, D])
        x_bf = sb("x_bf", [128, 2, D])
        adj0 = sb("adj0", [128, 2, N], U8)
        adj1 = sb("adj1", [128, 2, N], U8)
        mask0 = sb("mask0", [128, 2, N], BF16)
        mask1 = sb("mask1", [128, 2, N], BF16)
        q_hi = sb("q_hi", [128, C, 2 * N], F32R)
        q_lo = sb("q_lo", [128, C, 2 * N], F32R)
        k_hi = sb("k_hi", [128, C, 2, 2, N], F32R)
        k_lo = sb("k_lo", [128, C, 2, 2, N], F32R)
        v_res = sb("v_res", [128, 2, D])
        v_part = [sb(f"v_part{i}", [128, 2, H0, E0 + 1], BF16) for i in range(3)]
        p0 = sb("p0", [128, 2, H0 * N])
        p0_max = sb("p0_max", [128, 2, H0])
        p0_shift = sb("p0_shift", [128, 2, H0])
        p0t_hi = sb("p0t_hi", [128, 2, H0 * N], F16)
        p0t_lo = sb("p0t_lo", [128, 2, H0 * N], F16)
        ctx_rcp = sb("ctx_rcp", [128, 2, H0])
        ctx_n = sb("ctx_n", [128, 2, D])
        ctx_hi = sb("ctx_hi", [128, 2, C, N], F32R)
        ctx_lo = sb("ctx_lo", [128, 2, C, N], F32R)
        y = sb("y", [128, 2, D])
        stats = sb("stats", [128, 2, 6])
        moments = sb("moments", [128, 2, 2])
        rstd = sb("rstd", [128, 2, 1])
        shift0 = sb("shift0", [128, 2, 1])
        x1 = sb("x1", [128, 2, D])

        x1_kept = sb("x1_kept", [128, 2, D])
        x1t_hi = sb("x1t_hi", [128, 2, C, N], F32R)
        x1t_lo = sb("x1t_lo", [128, 2, C, N], F32R)
        th = sb("th", [128, 2, D])
        h_part = [sb(f"h_part{i}", [128, 2, H1, E1 + 1], BF16) for i in range(3)]
        h_res = sb("h_res", [128, 2, D])
        prod = sb("prod", [128, 2, 2 * D])
        sd = sb("sd", [128, 2, 2, H1])
        sd_res = sb("sd_res", [128, 2, 2, H1])
        sd_parts = sb("sd_parts", [128, 2, 2, 64], BF16)
        src_t = sb("src_t", [128, 2, N], BF16)
        dst_t = sb("dst_t", [128, 2, N], BF16)
        dst_row = sb("dst_row", [128, 2, H1, N], BF16)
        z = sb("z", [128, 2, H1 * N])
        z_max = sb("z_max", [128, 2, H1])
        p1t_hi = sb("p1t_hi", [128, 2, H1 * N], F16)
        p1t_lo = sb("p1t_lo", [128, 2, H1 * N], F16)
        f_rcp = sb("f_rcp", [128, 2, H1])
        f = sb("f", [128, 2, D])
        f_neg = sb("f_neg", [128, 2, D])
        gate = sb("gate", [128, 2, D])
        y2 = sb("y2", [128, 2, D])
        stats2 = sb("stats2", [128, 2, 6])
        moments2 = sb("moments2", [128, 2, 2])
        rstd2 = sb("rstd2", [128, 2, 1])
        shift1 = sb("shift1", [128, 2, 1])
        out_tile = sb("out_tile", [128, 2, D])
        bias_row, bias_res = y2[0:1, :, :], out_tile[0:1, :, :]
        bias_parts = p1t_hi[0:1, :, :].rearrange("p g n -> p (g n)").bitcast(BF16)[:, 0:3 * 2 * D]\
            .rearrange("p (i s d) -> p i s d", i=3, s=2)

        lin = [ctx.enter_context(nc.psum_tensor(f"lin{i}", [128, 512], F32)) for i in range(2)]
        tp = [ctx.enter_context(nc.psum_tensor(f"tp{i}", [128, 512], F32)) for i in range(2)]
        zp = ctx.enter_context(nc.psum_tensor("zp", [128, 3, 512], F32))
        fp = ctx.enter_context(nc.psum_tensor("fp", [128, 512], F32))

        w_loaded = {n: signal(f"{n}_loaded", 0) for n in WEIGHTS}
        w_hi_ready = {n: signal(f"{n}_hi_ready", 0) for n in WEIGHTS}
        w_lo_ready = {n: signal(f"{n}_lo_ready", 0) for n in WEIGHTS}
        small_loaded = signal("small_loaded", 0)
        bias_split = signal("bias_split", 0)
        bias_loaded = signal("bias_loaded", 0)
        ones_ready = signal("ones_ready", 0)
        consts_ready = signal("consts_ready", 0)
        fills_ready = signal("fills_ready", 0)
        passed = ctx.enter_context(nc.semaphore("passed"))

        xt_loaded = signal("xt_loaded", -1, DONE_BY_DMA)
        x_loaded = signal("x_loaded", -1, DONE_BY_DMA)
        adj0_loaded = signal("adj0_loaded", -1, DONE_BY_DMA)
        xt_split = signal("xt_split", -1)
        xt_hi_made = signal("xt_hi_made", -1)
        adj1_loaded = signal("adj1_loaded", 0, DONE_BY_DMA)
        x_bf_ready = signal("x_bf_ready", 0)
        mask0_ready = signal("mask0_ready", 0)
        qk_mm = [signal(f"qk_mm{j}", 0) for j in range(C)]
        qk_hi = [signal(f"qk_hi{j}", 0) for j in range(C)]
        qk_lo = [signal(f"qk_lo{j}", 0) for j in range(C)]
        sc_mm, sc_max = pair_of("sc_mm", 0), pair_of("sc_max", 0)
        sc_shift, sc_exp = pair_of("sc_shift", 0), pair_of("sc_exp", 0)
        v_mm, v_r = pair_of("v_mm", 0), pair_of("v_r", 0)
        v_done = [pair_of(f"v_done{i}", 0) for i in range(3)]
        pt_mm = [pair_of(f"pt_mm{k}", 0) for k in range(2)]
        pt_hi = [pair_of(f"pt_hi{k}", 0) for k in range(2)]
        pt_lo = [pair_of(f"pt_lo{k}", 0) for k in range(2)]
        ctx_mm, ctx_inv, ctx_ready = pair_of("ctx_mm", 0), pair_of("ctx_inv", 0), pair_of("ctx_ready", 0)
        ct_mm, ct_hi, ct_lo = pair_of("ct_mm", 0), pair_of("ct_hi", 0), pair_of("ct_lo", 0)
        pr_mm, y_ready, y_stats = pair_of("pr_mm", 0), pair_of("y_ready", 0), pair_of("y_stats", 0)
        y_mom, y_var, y_rstd = pair_of("y_mom", 0), pair_of("y_var", 0), pair_of("y_rstd", 0)
        x1_ready = pair_of("x1_ready", 0)

        mask1_ready = signal("mask1_ready", 1)
        x1_copied = pair_of("x1_copied", 1)
        x1t_mm, x1t_h, x1t_l = pair_of("x1t_mm", 1), pair_of("x1t_h", 1), pair_of("x1t_l", 1)
        h_mm, h_tanh, h_r = pair_of("h_mm", 1), pair_of("h_tanh", 1), pair_of("h_r", 1)
        h_done = [pair_of(f"h_done{i}", 1) for i in range(3)]
        g_mm, g_tanh, g_plus = pair_of("g_mm", 1), pair_of("g_tanh", 1), pair_of("g_plus", 1)
        sd_prod, sd_sum = pair_of("sd_prod", 1), pair_of("sd_sum", 1)
        sd_1, sd_r, sd_2, sd_3 = (signal(f"sd_{i}", 1) for i in ("part1", "res", "part2", "part3"))
        sdt_mm, src_ready, dst_ready = signal("sdt_mm", 1), signal("src_ready", 1), signal("dst_ready", 1)
        dst_flat = [signal(f"dst_flat{g}", 1, 3 * DONE_BY_DMA) for g in range(2)]
        z_mm, z_maxed = pair_of("z_mm", 1), pair_of("z_maxed", 1)
        z_copied, z_leaky = pair_of("z_copied", 1), pair_of("z_leaky", 1)
        z_sub, z_exp = pair_of("z_sub", 1), pair_of("z_exp", 1)
        wt_mm = [pair_of(f"wt_mm{k}", 2) for k in range(3)]
        wt_hi = [pair_of(f"wt_hi{k}", 2) for k in range(3)]
        wt_lo = [pair_of(f"wt_lo{k}", 2) for k in range(3)]
        f_mm, f_inv, f_norm = pair_of("f_mm", 2), pair_of("f_inv", 2), pair_of("f_norm", 2)
        f_bias, f_min, f_exp = pair_of("f_bias", 2), pair_of("f_min", 2), pair_of("f_exp", 2)
        f_elu, f_diff, f_gated = pair_of("f_elu", 2), pair_of("f_diff", 2), pair_of("f_gated", 2)
        y2_ready, y2_stats, y2_mom = pair_of("y2_ready", 2), pair_of("y2_stats", 2), pair_of("y2_mom", 2)
        y2_var, y2_rstd, out_ready = pair_of("y2_var", 2), pair_of("y2_rstd", 2), pair_of("out_ready", 2)
        stored = [signal(f"stored{g}", 2, DONE_BY_DMA) for g in range(2)]

        norm0_shift, norm1_shift = pair_of("norm0_shift", 0), pair_of("norm1_shift", 2)

        readers = {"sdt": dst_ready}
        for j in range(C):
            readers[f"qk{j}"] = qk_lo[j]
        for g in range(2):
            readers.update({f"v{g}": v_r[g], f"h{g}": h_r[g], f"g{g}": g_tanh[g], f"pr{g}": y_ready[g],
                            f"sc{g}": sc_exp[g], f"z{g}": z_copied[g], f"ctx{g}": ctx_ready[g],
                            f"f{g}": f_norm[g], f"x1t{g}": x1t_l[g], f"ct{g}": ct_lo[g]})
            readers.update({f"pt{g}{half}": pt_lo[half][g] for half in range(2)})
            readers.update({f"wt{g}{k}": wt_lo[k][g] for k in range(3)})

        def lin_bank(user):
            return lin[bank_of(LIN_USERS, user)]

        def tp_bank(user):
            return tp[bank_of(TP_USERS, user)]

        xt_d = x_t
        x_d = x.rearrange("(t g) n d -> t n g d", g=2)
        adj_d = adj.rearrange("(t g) n m -> t n g m", g=2)
        out_d = out.rearrange("(t g) n d -> t n g d", g=2)

        block = ctx.enter_context(nc.Block())

        @block.sync
        def _(sp):
            sp.dma_start(z[:, 0, 0:C * D], weights["Wq"]).then_inc(w_loaded["Wq"].sem, 16)
            sp.dma_start(z[:, 1, 0:C * D], weights["Wk"]).then_inc(w_loaded["Wk"].sem, 16)
            for n in ("bq", "bk"):
                sp.dma_start(qk_bias[n][:, :], biases[n]).then_inc(small_loaded.sem, 16)
            for n in rows:
                sp.dma_start(rows[n][:, :], row_biases[n].partition_broadcast(128)).then_inc(small_loaded.sem, 16)
            for i, n in enumerate(("bv", "Hb")):
                sp.dma_start(bias_row[:, i, :], row_biases[n].unsqueeze(0)).then_inc(small_loaded.sem, 16)
            sp.wait_ge(bias_split.sem, 5)
            sp.dma_start(bias_rows[:, :, :], bias_parts[0:1, :, :, :]).then_inc(bias_loaded.sem, 16)
            for i, n in enumerate(WEIGHTS[2:]):
                before = WEIGHTS[i]
                sp.wait_ge(w_lo_ready[before].sem, 1)
                sp.dma_start(z[:, i % 2, 0:C * D], weights[n]).then_inc(w_loaded[n].sem, 16)

            def body(turn):
                now, prev, t = turn.now, turn.prev, turn.t
                prepare, layer0, layer1, after1 = (turn.runs(stage) for stage in (-1, 0, 1, 2))
                if prepare:
                    sp.wait_ge(xt_split.sem, prev(xt_split))
                    turn.apart()
                    sp.dma_start(xt_raw[:, :, :], xt_d[t + 1]).then_inc(xt_loaded.sem, 16)
                    sp.wait_ge(x_bf_ready.sem, now(x_bf_ready))
                    turn.apart()
                    sp.dma_start(x_raw[:, :, :], x_d[t + 1]).then_inc(x_loaded.sem, 16)
                    sp.wait_ge(mask0_ready.sem, now(mask0_ready))
                    turn.apart()
                    sp.dma_start(adj0[:, :, :], adj_d[t + 1]).then_inc(adj0_loaded.sem, 16)
                if layer0:
                    sp.wait_ge(mask1_ready.sem, now(mask1_ready))
                    turn.apart()
                    sp.dma_start(adj1[:, :, :], adj_d[t]).then_inc(adj1_loaded.sem, 16)
                if layer1:
                    sp.wait_ge(dst_ready.sem, now(dst_ready))
                    for g in range(2):
                        sp.wait_ge(z_mm[g].sem, prev(z_mm[g]))
                        for part in range(3):
                            dma = sp.dma_start(dst_row[64 + part:65 + part, g, :, :],
                                               dst_t[64 + H1 * part:64 + H1 * (part + 1), g, :])
                            dma.then_inc(dst_flat[g].sem, 16)
                if after1:
                    for g in range(2):
                        sp.wait_ge(out_ready[g].sem, now(out_ready[g]))
                        turn.apart()
                        sp.dma_start(out_d[t - 2, :, g, :], out_tile[:, g, :]).then_inc(stored[g].sem, 16)

            turns(sp, passed, body)
            for g in range(2):
                sp.wait_ge(stored[g].sem, 16 * PAIRS)

        @block.tensor
        def _(pe):
            def product(bank, left_hi, left_lo, right_hi, right_lo, opens=True):
                passes = [(left_hi, right_hi), (left_hi, right_lo), (left_lo, right_hi)]
                for k in range(C):
                    for i, (a, b) in enumerate(passes):
                        last = pe.matmul(bank, a(k), b(k), start=(opens and k == 0 and i == 0),
                                         stop=(k == C - 1 and i == 2))
                return last

            def rows_product(bank, hi, lo, name, opens):
                return product(bank[:, 0:D], hi, lo, lambda k: w_hi[name][:, k, :], lambda k: w_lo[name][:, k, :], opens)

            pe.wait_ge(consts_ready.sem, 4)
            pe.wait_ge(fills_ready.sem, 1)

            def body(turn):
                now, prev, t = turn.now, turn.prev, turn.t
                layer0, layer1, after1 = (turn.runs(stage) for stage in (0, 1, 2))
                first = not turn.loop and t == 0
                first1 = not turn.loop and t == 1

                def bank_free(users, user, banks=2):
                    freed = last_reader(turn, users, user, readers, banks)
                    if freed:
                        pe.wait_ge(freed[0].sem, freed[1])

                def queries_keys(j):
                    if first:
                        for n in ("Wq", "Wk"):
                            pe.wait_ge(w_lo_ready[n].sem, 1)
                    pe.wait_ge(xt_split.sem, prev(xt_split))
                    bank_free(LIN_USERS, f"qk{j}")
                    bank = lin_bank(f"qk{j}")
                    for i, n in enumerate(("Wq", "Wk")):
                        last = product(bank[:, 2 * N * i:2 * N * (i + 1)],
                                       lambda k: w_hi[n][:, k, 128 * j:128 * (j + 1)],
                                       lambda k: w_lo[n][:, k, 128 * j:128 * (j + 1)],
                                       lambda k: xt_hi[:, k, :], lambda k: xt_lo[:, k, :])
                    last.then_inc(qk_mm[j].sem, 1)

                def x1_transposes(g):
                    pe.wait_ge(x1_ready[g].sem, prev(x1_ready[g]))
                    bank_free(TP_USERS, f"x1t{g}")
                    bank = tp_bank(f"x1t{g}")
                    for k in range(C):
                        last = pe.transpose(bank[:, 128 * k:128 * (k + 1)], x1[:, g, 128 * k:128 * (k + 1)], ident[:, :])
                    last.then_inc(x1t_mm[g].sem, 1)

                def bias_product(bank, i):
                    pe.matmul(bank[:, 0:D], ones_bf[:, :], bias_rows[:, i, :], start=True, stop=False)

                def hidden(g):
                    bank_free(LIN_USERS, f"h{g}")
                    pe.wait_ge(x1t_l[g].sem, now(x1t_l[g]))
                    if first1:
                        pe.wait_ge(w_lo_ready["W1"].sem, 1)
                    rows_product(lin_bank(f"h{g}"), lambda k: x1t_hi[:, g, k, :], lambda k: x1t_lo[:, g, k, :],
                                 "W1", True).then_inc(h_mm[g].sem, 1)

                def values(g):
                    bank_free(LIN_USERS, f"v{g}")
                    pe.wait_ge(xt_split.sem, prev(xt_split))
                    if first:
                        pe.wait_ge(bias_loaded.sem, 16)
                        pe.wait_ge(w_lo_ready["Wv"].sem, 1)
                    bias_product(lin_bank(f"v{g}"), 0)
                    rows_product(lin_bank(f"v{g}"), lambda k: xt_hi[:, k, N * g:N * (g + 1)],
                                 lambda k: xt_lo[:, k, N * g:N * (g + 1)], "Wv", False).then_inc(v_mm[g].sem, 1)

                def gate_rows(g):
                    bank_free(LIN_USERS, f"g{g}")
                    pe.wait_ge(x1t_l[g].sem, now(x1t_l[g]))
                    if first1:
                        pe.wait_ge(w_lo_ready["Hw"].sem, 1)
                    bias_product(lin_bank(f"g{g}"), 1)
                    rows_product(lin_bank(f"g{g}"), lambda k: x1t_hi[:, g, k, :], lambda k: x1t_lo[:, g, k, :],
                                 "Hw", False).then_inc(g_mm[g].sem, 1)

                def source_target_transposes():
                    pe.wait_ge(sd_3.sem, now(sd_3))
                    bank_free(TP_USERS, "sdt")
                    for g in range(2):
                        last = pe.transpose(tp_bank("sdt")[:, :].bitcast(BF16)[:, N * g:N * (g + 1)],
                                            sd_parts[:, g, :, :].rearrange("p a b -> p (a b)"), ident_bf[:, :])
                    last.then_inc(sdt_mm.sem, 1)

                def scores(g):
                    bank_free(ZP_USERS, f"sc{g}", 1)
                    pe.wait_ge(mask0_ready.sem, now(mask0_ready))
                    for j in range(C):
                        pe.wait_ge(qk_lo[j].sem, now(qk_lo[j]))
                    m = mask0[:, g:g + 1, :]
                    pe.matmul(zp[:, 0, :], ident_bf[:, :], m.to_broadcast([128, 4, N]), start=True, stop=True)
                    pe.matmul(zp[:, 1, 0:2 * N], ident_bf[:, :], m.to_broadcast([128, 2, N]), start=True, stop=True)
                    for j in range(C):
                        o = zp[:, j // 2, 2 * N * (j % 2):2 * N * (j % 2) + 2 * N]
                        qh, ql = q_hi[:, j, N * g:N * (g + 1)], q_lo[:, j, N * g:N * (g + 1)]
                        kh = k_hi[:, j, g, :, :].rearrange("p a n -> p (a n)")
                        kl = k_lo[:, j, g, :, :].rearrange("p a n -> p (a n)")
                        pe.matmul(o, qh, kh, start=False, stop=False, skip_group_check=True)
                        pe.matmul(o, qh, kl, start=False, stop=False, skip_group_check=True)
                        last = pe.matmul(o, ql, kh, start=False, stop=True, skip_group_check=True)
                    last.then_inc(sc_mm[g].sem, 1)

                def weights0_transposes(g, half):
                    pe.wait_ge(sc_exp[g].sem, now(sc_exp[g]))
                    bank_free(TP_USERS, f"pt{g}{half}")
                    bank = tp_bank(f"pt{g}{half}")
                    for i in range(3):
                        c = N * (3 * half + i)
                        last = pe.transpose(bank[:, N * i:N * (i + 1)], p0[:, g, c:c + N], ident[:, :])
                    last.then_inc(pt_mm[half][g].sem, 1)

                def attend0(g):
                    bank_free(FP_USERS, f"ctx{g}", 1)
                    pe.wait_ge(v_done[2][g].sem, now(v_done[2][g]))
                    for h in range(H0):
                        if h % 3 == 0:
                            pe.wait_ge(pt_lo[h // 3][g].sem, now(pt_lo[h // 3][g]))
                        o = fp[:, (E0 + 1) * h:(E0 + 1) * (h + 1)]
                        hi, lo = p0t_hi[:, g, N * h:N * (h + 1)], p0t_lo[:, g, N * h:N * (h + 1)]
                        for i in range(3):
                            pe.matmul(o, hi, v_part[i][:, g, h, :], start=(h == 0 and i == 0), stop=False,
                                      skip_group_check=True)
                        for i in range(2):
                            last = pe.matmul(o, lo, v_part[i][:, g, h, :], start=False, stop=(i == 1),
                                             skip_group_check=True)
                    last.then_inc(ctx_mm[g].sem, 1)

                def context_transposes(g):
                    pe.wait_ge(ctx_ready[g].sem, now(ctx_ready[g]))
                    bank_free(TP_USERS, f"ct{g}")
                    bank = tp_bank(f"ct{g}")
                    for k in range(C):
                        last = pe.transpose(bank[:, 128 * k:128 * (k + 1)], ctx_n[:, g, 128 * k:128 * (k + 1)], ident[:, :])
                    last.then_inc(ct_mm[g].sem, 1)

                def project(g):
                    pe.wait_ge(ct_lo[g].sem, now(ct_lo[g]))
                    bank_free(LIN_USERS, f"pr{g}")
                    if first:
                        pe.wait_ge(w_lo_ready["Wf"].sem, 1)
                    rows_product(lin_bank(f"pr{g}"), lambda k: ctx_hi[:, g, k, :], lambda k: ctx_lo[:, g, k, :],
                                 "Wf", True).then_inc(pr_mm[g].sem, 1)

                def attention1(g):
                    bank_free(ZP_USERS, f"z{g}", 1)
                    pe.wait_ge(src_ready.sem, now(src_ready))
                    pe.wait_ge(mask1_ready.sem, now(mask1_ready))
                    m = mask1[:, g:g + 1, :].to_broadcast([128, 4, N])
                    for b in range(3):
                        pe.matmul(zp[:, b, :], ident_bf[:, :], m, start=True, stop=False)
                    pe.wait_ge(dst_flat[g].sem, now(dst_flat[g]))
                    flat_rows = dst_row[0:67, g, :, :].rearrange("p a n -> p (a n)")
                    for b in range(3):
                        last = pe.matmul(zp[:, b, :], src_t[0:67, g, :], flat_rows[:, 512 * b:512 * (b + 1)],
                                         start=False, stop=True)
                    last.then_inc(z_mm[g].sem, 1)

                def weights1_transposes(g, k):
                    pe.wait_ge(z_exp[g].sem, prev(z_exp[g]))
                    bank_free(TP_USERS, f"wt{g}{k}")
                    bank = tp_bank(f"wt{g}{k}")
                    for i in range(4):
                        c = N * (4 * k + i)
                        last = pe.transpose(bank[:, N * i:N * (i + 1)], z[:, g, c:c + N], ident[:, :])
                    last.then_inc(wt_mm[k][g].sem, 1)

                def attend1(g, k):
                    if k == 0:
                        bank_free(FP_USERS, f"f{g}", 1)
                        pe.wait_ge(h_done[2][g].sem, prev(h_done[2][g]))
                    pe.wait_ge(wt_lo[k][g].sem, now(wt_lo[k][g]))
                    for h in range(4 * k, 4 * k + 4):
                        o = fp[:, (E1 + 1) * h:(E1 + 1) * (h + 1)]
                        hi, lo = p1t_hi[:, g, N * h:N * (h + 1)], p1t_lo[:, g, N * h:N * (h + 1)]
                        for i in range(3):
                            pe.matmul(o, hi, h_part[i][:, g, h, :], start=(h == 0 and i == 0), stop=False,
                                      skip_group_check=True)
                        for i in range(2):
                            last = pe.matmul(o, lo, h_part[i][:, g, h, :], start=False, stop=(i == 1),
                                             skip_group_check=True)
                    if k == 2:
                        last.then_inc(f_mm[g].sem, 1)

                if after1:
                    weights1_transposes(0, 1)
                if layer0:
                    values(0)
                if after1:
                    weights1_transposes(0, 0)
                if layer0:
                    queries_keys(0)
                    queries_keys(1)
                if after1:
                    weights1_transposes(0, 2)
                    attend1(0, 0)
                if layer1:
                    x1_transposes(0)
                if after1:
                    attend1(0, 1)
                if layer0:
                    queries_keys(2)
                if after1:
                    attend1(0, 2)
                if layer1:
                    x1_transposes(1)
                if after1:
                    weights1_transposes(1, 0)
                if layer1:
                    hidden(0)
                if layer0:
                    scores(0)
                if layer1:
                    hidden(1)
                if after1:
                    weights1_transposes(1, 2)
                    weights1_transposes(1, 1)
                if layer0:
                    values(1)
                    scores(1)
                if layer1:
                    source_target_transposes()
                if layer0:
                    weights0_transposes(0, 0)
                if after1:
                    attend1(1, 0)
                if layer0:
                    weights0_transposes(0, 1)
                if after1:
                    attend1(1, 1)
                    attend1(1, 2)
                if layer0:
                    weights0_transposes(1, 0)
                if layer1:
                    attention1(0)
                if layer0:
                    attend0(0)
                    weights0_transposes(1, 1)
                    context_transposes(0)
                if layer1:
                    attention1(1)
                    gate_rows(0)
                if layer0:
                    attend0(1)
                if layer1:
                    gate_rows(1)
                if layer0:
                    project(0)
                    context_transposes(1)
                    project(1)

            turns(pe, passed, body)

        @block.scalar
        def _(act):
            for i, n in enumerate(WEIGHTS):
                act.wait_ge(w_loaded[n].sem, 16)
                act.activation(w_hi[n][:, :, :].rearrange("p c d -> p (c d)"), z[:, i % 2, 0:C * D], ACT.Copy)\
                    .then_inc(w_hi_ready[n].sem, 1)

            act.wait_ge(small_loaded.sem, 16 * SMALL)
            act.wait_ge(fills_ready.sem, 1)

            def body(turn):
                now, prev = turn.now, turn.prev
                prepare, layer0, layer1, after1 = (turn.runs(stage) for stage in (-1, 0, 1, 2))

                def queries_keys(j):
                    act.wait_ge(qk_mm[j].sem, now(qk_mm[j]))
                    act.wait_ge(sc_mm[1].sem, prev(sc_mm[1]))
                    bank = lin_bank(f"qk{j}")
                    act.activation(q_hi[:, j, :], bank[:, 0:2 * N], ACT.Identity, bias=qk_bias["bq"][:, j:j + 1])
                    for half in range(2):
                        p = slice(64 * half, 64 * half + 64)
                        last = act.activation(k_hi[p, j, :, half, :],
                                              bank[p, 2 * N:4 * N].rearrange("p (g n) -> p g n", g=2),
                                              ACT.Identity, bias=qk_bias["bk"][p, j:j + 1])
                    last.then_inc(qk_hi[j].sem, 1)

                def x1_high(g):
                    act.wait_ge(x1t_mm[g].sem, now(x1t_mm[g]))
                    act.wait_ge(g_mm[g].sem, prev(g_mm[g]))
                    act.wait_ge(h_mm[g].sem, prev(h_mm[g]))
                    act.activation(x1t_hi[:, g, :, :].rearrange("p c n -> p (c n)"), tp_bank(f"x1t{g}")[:, 0:D],
                                   ACT.Copy).then_inc(x1t_h[g].sem, 1)

                def keep_x1(g):
                    act.wait_ge(x1_ready[g].sem, prev(x1_ready[g]))
                    act.wait_ge(y2_ready[g].sem, now(y2_ready[g]))
                    act.activation(x1_kept[:, g, :], x1[:, g, :], ACT.Copy).then_inc(x1_copied[g].sem, 1)

                def hidden_tanh(g):
                    act.wait_ge(h_mm[g].sem, now(h_mm[g]))
                    act.wait_ge(sd_prod[g].sem, prev(sd_prod[g]))
                    act.activation(th[:, g, :], lin_bank(f"h{g}")[:, 0:D], ACT.Tanh).then_inc(h_tanh[g].sem, 1)

                def hidden_part1(g):
                    act.wait_ge(f_mm[g].sem, now(f_mm[g]))
                    act.activation(h_part[0][:, g, :, 0:E1],
                                   lin_bank(f"h{g}")[:, 0:D].rearrange("p (a e) -> p a e", a=H1),
                                   ACT.Copy).then_inc(h_done[0][g].sem, 1)

                def hidden_part2(g):
                    act.wait_ge(h_r[g].sem, now(h_r[g]))
                    act.activation(h_part[1][:, g, :, 0:E1], h_res[:, g, :].rearrange("p (a e) -> p a e", a=H1),
                                   ACT.Copy).then_inc(h_done[1][g].sem, 1)

                def value_part1(g):
                    act.wait_ge(v_mm[g].sem, now(v_mm[g]))
                    act.wait_ge(ctx_mm[g].sem, prev(ctx_mm[g]))
                    act.activation(v_part[0][:, g, :, 0:E0],
                                   lin_bank(f"v{g}")[:, 0:D].rearrange("p (a e) -> p a e", a=H0),
                                   ACT.Copy).then_inc(v_done[0][g].sem, 1)

                def value_part2(g):
                    act.wait_ge(v_r[g].sem, now(v_r[g]))
                    act.activation(v_part[1][:, g, :, 0:E0], v_res[:, g, :].rearrange("p (a e) -> p a e", a=H0),
                                   ACT.Copy).then_inc(v_done[1][g].sem, 1)

                def source_copy():
                    act.wait_ge(sdt_mm.sem, now(sdt_mm))
                    act.wait_ge(z_mm[1].sem, prev(z_mm[1]))
                    act.activation(src_t[0:36, :, :].rearrange("p g n -> p (g n)"),
                                   tp_bank("sdt")[:, :].bitcast(BF16)[0:36, 0:2 * N], ACT.Copy)\
                        .then_inc(src_ready.sem, 1)

                def gate_tanh(g):
                    act.wait_ge(g_mm[g].sem, now(g_mm[g]))
                    act.wait_ge(f_gated[g].sem, now(f_gated[g]))
                    act.activation(gate[:, g, :], lin_bank(f"g{g}")[:, 0:D], ACT.Tanh, scale=0.5)\
                        .then_inc(g_tanh[g].sem, 1)

                def gate_plus_one(g):
                    act.wait_ge(g_tanh[g].sem, now(g_tanh[g]))
                    act.activation(gate[:, g, :], gate[:, g, :], ACT.Copy, bias=1.0).then_inc(g_plus[g].sem, 1)

                def scores_exp(g):
                    act.wait_ge(sc_shift[g].sem, now(sc_shift[g]))
                    act.wait_ge(pt_mm[1][g].sem, prev(pt_mm[1][g]))
                    act.wait_ge(pt_mm[0][g].sem, prev(pt_mm[0][g]))
                    for h in range(H0):
                        last = act.activation(p0[:, g, N * h:N * (h + 1)], zp[:, h // 4, N * (h % 4):N * (h % 4 + 1)],
                                              ACT.Exp, bias=p0_shift[:, g, h:h + 1], scale=SCALE0)
                    last.then_inc(sc_exp[g].sem, 1)

                def z_copy(g):
                    act.wait_ge(z_mm[g].sem, now(z_mm[g]))
                    for k in range(3):
                        act.wait_ge(wt_mm[k][g].sem, now(wt_mm[k][g]))
                    act.activation(z[:, g, :], zp[:, :, :].rearrange("p b n -> p (b n)"), ACT.Copy)\
                        .then_inc(z_copied[g].sem, 1)

                def weights0_high(g, half):
                    act.wait_ge(pt_mm[half][g].sem, now(pt_mm[half][g]))
                    act.wait_ge(ctx_mm[g].sem, prev(ctx_mm[g]))
                    act.activation(p0t_hi[:, g, 3 * N * half:3 * N * (half + 1)], tp_bank(f"pt{g}{half}")[:, 0:3 * N],
                                   ACT.Copy, scale=PSCALE).then_inc(pt_hi[half][g].sem, 1)

                def context_high(g):
                    act.wait_ge(ct_mm[g].sem, now(ct_mm[g]))
                    act.wait_ge(pr_mm[g].sem, prev(pr_mm[g]))
                    act.activation(ctx_hi[:, g, :, :].rearrange("p c n -> p (c n)"), tp_bank(f"ct{g}")[:, 0:D],
                                   ACT.Copy).then_inc(ct_hi[g].sem, 1)

                def norm0(g):
                    act.wait_ge(norm0_shift[g].sem, now(norm0_shift[g]))
                    act.wait_ge(x1t_mm[g].sem, now(x1t_mm[g]))
                    act.wait_ge(x1_copied[g].sem, now(x1_copied[g]))
                    act.activation(x1[:, g, :], y[:, g, :], ACT.Identity, bias=shift0[:, g, :], scale=rstd[:, g, :])\
                        .then_inc(x1_ready[g].sem, 1)

                def z_exponent(g):
                    act.wait_ge(z_sub[g].sem, now(z_sub[g]))
                    act.activation(z[:, g, :], z[:, g, :], ACT.Exp).then_inc(z_exp[g].sem, 1)

                def weights1_high(g, k):
                    act.wait_ge(wt_mm[k][g].sem, now(wt_mm[k][g]))
                    act.wait_ge(f_mm[g].sem, prev(f_mm[g]))
                    act.activation(p1t_hi[:, g, 4 * N * k:4 * N * (k + 1)], tp_bank(f"wt{g}{k}")[:, :], ACT.Copy,
                                   scale=PSCALE).then_inc(wt_hi[k][g].sem, 1)

                def elu_exp(g):
                    act.wait_ge(f_min[g].sem, now(f_min[g]))
                    act.activation(f_neg[:, g, :], f_neg[:, g, :], ACT.Exp).then_inc(f_exp[g].sem, 1)

                def norm1(g):
                    act.wait_ge(norm1_shift[g].sem, now(norm1_shift[g]))
                    act.wait_ge(stored[g].sem, prev(stored[g]))
                    act.activation(out_tile[:, g, :], y2[:, g, :], ACT.Identity, bias=shift1[:, g, :],
                                   scale=rstd2[:, g, :]).then_inc(out_ready[g].sem, 1)

                def next_x_high():
                    act.wait_ge(xt_loaded.sem, now(xt_loaded))
                    for j in range(C):
                        act.wait_ge(qk_mm[j].sem, now(qk_mm[j]))
                    act.wait_ge(v_mm[0].sem, now(v_mm[0]))
                    act.wait_ge(v_mm[1].sem, now(v_mm[1]))
                    act.activation(xt_hi[:, :, :].rearrange("p c n -> p (c n)"),
                                   xt_raw[:, :, :].rearrange("p c n -> p (c n)"), ACT.Copy).then_inc(xt_hi_made.sem, 1)

                if layer0:
                    value_part1(0)
                if after1:
                    weights1_high(0, 0)
                    weights1_high(0, 1)
                if layer0:
                    queries_keys(0)
                if after1:
                    weights1_high(0, 2)
                if layer1:
                    x1_high(0)
                if layer0:
                    queries_keys(1)
                    queries_keys(2)
                if layer1:
                    x1_high(1)
                if layer0:
                    value_part2(0)
                if after1:
                    weights1_high(1, 0)
                if layer1:
                    hidden_tanh(0)
                    hidden_part1(0)
                if after1:
                    elu_exp(0)
                if layer1:
                    hidden_tanh(1)
                if after1:
                    weights1_high(1, 2)
                    weights1_high(1, 1)
                if layer0:
                    scores_exp(0)
                    value_part1(1)
                if layer1:
                    source_copy()
                    hidden_part2(0)
                if layer0:
                    weights0_high(0, 0)
                    scores_exp(1)
                    weights0_high(0, 1)
                if layer1:
                    hidden_part1(1)
                if layer0:
                    weights0_high(1, 0)
                if prepare:
                    next_x_high()
                if layer1:
                    z_copy(0)
                if layer0:
                    weights0_high(1, 1)
                if layer1:
                    keep_x1(0)
                if after1:
                    elu_exp(1)
                if layer0:
                    value_part2(1)
                    context_high(0)
                if layer1:
                    z_copy(1)
                if after1:
                    norm1(0)
                if layer1:
                    gate_tanh(0)
                    gate_plus_one(0)
                    gate_tanh(1)
                    gate_plus_one(1)
                if layer0:
                    context_high(1)
                if layer1:
                    z_exponent(0)
                    hidden_part2(1)
                    keep_x1(1)
                    z_exponent(1)
                if after1:
                    norm1(1)
                if layer0:
                    norm0(0)
                    norm0(1)

            turns(act, passed, body)

        @block.vector
        def _(dve):
            dve.memset(src_t[:, :, :], 0.0).then_inc(ones_ready.sem, 1)
            dve.memset(dst_row[:, :, :, :].rearrange("p g a n -> p (g a n)"), 0.0).then_inc(ones_ready.sem, 1)
            dve.wait_ge(ones_ready.sem, 4)
            dve.memset(src_t[64:67, :, :], 1.0).then_inc(consts_ready.sem, 1)
            dve.memset(k_hi[:, :, :, :, :].rearrange("p a b c n -> p (a b c n)").bitcast(F32), 0.0)
            dve.memset(k_lo[:, :, :, :, :].rearrange("p a b c n -> p (a b c n)").bitcast(F32), 0.0)
            for i in range(3):
                dve.memset(v_part[i][:, :, :, E0:], 1.0 if i == 0 else 0.0)
                dve.memset(h_part[i][:, :, :, E1:], 1.0 if i == 0 else 0.0)
            dve.memset(sd_parts[:, :, :, :], 0.0)
            dve.memset(ones_bf[:, :], 1.0)
            dve.memset(half_neg[:, :], -0.5).then_inc(fills_ready.sem, 1)
            dve.wait_ge(small_loaded.sem, 16 * SMALL)
            dve.tensor_copy(bias_parts[:, 0, :, :], bias_row[:, :, :]).then_inc(bias_split.sem, 1)
            dve.wait_ge(bias_split.sem, 1)
            dve.tensor_tensor(bias_res[:, :, :], bias_row[:, :, :], bias_parts[:, 0, :, :], ALU.subtract)\
                .then_inc(bias_split.sem, 1)
            dve.wait_ge(bias_split.sem, 2)
            dve.tensor_copy(bias_parts[:, 1, :, :], bias_res[:, :, :]).then_inc(bias_split.sem, 1)
            dve.wait_ge(bias_split.sem, 3)
            dve.tensor_tensor(bias_res[:, :, :], bias_res[:, :, :], bias_parts[:, 1, :, :], ALU.subtract)\
                .then_inc(bias_split.sem, 1)
            dve.wait_ge(bias_split.sem, 4)
            dve.tensor_copy(bias_parts[:, 2, :, :], bias_res[:, :, :]).then_inc(bias_split.sem, 1)
            for i, n in enumerate(WEIGHTS):
                dve.wait_ge(w_hi_ready[n].sem, 1)
                dve.tensor_tensor(w_lo[n][:, :, :].rearrange("p c d -> p (c d)"), z[:, i % 2, 0:C * D],
                                  w_hi[n][:, :, :].rearrange("p c d -> p (c d)").bitcast(F32), ALU.subtract)\
                    .then_inc(w_lo_ready[n].sem, 1)
            dve.wait_ge(fills_ready.sem, 1)

            def body(turn):
                now, prev = turn.now, turn.prev
                prepare, layer0, layer1, after1 = (turn.runs(stage) for stage in (-1, 0, 1, 2))

                def queries_keys(j):
                    dve.wait_ge(qk_hi[j].sem, now(qk_hi[j]))
                    dve.wait_ge(sc_mm[1].sem, prev(sc_mm[1]))
                    bank = lin_bank(f"qk{j}")
                    dve.scalar_tensor_tensor(out=q_lo[:, j, :], in0=bank[:, 0:2 * N],
                                             scalar=qk_bias["bq"][:, j:j + 1], in1=q_hi[:, j, :].bitcast(F32),
                                             op0=ALU.add, op1=ALU.subtract)
                    for half in range(2):
                        p = slice(64 * half, 64 * half + 64)
                        last = dve.scalar_tensor_tensor(
                            out=k_lo[p, j, :, half, :],
                            in0=bank[p, 2 * N:4 * N].rearrange("p (g n) -> p g n", g=2),
                            scalar=qk_bias["bk"][p, j:j + 1], in1=k_hi[p, j, :, half, :].bitcast(F32),
                            op0=ALU.add, op1=ALU.subtract)
                    last.then_inc(qk_lo[j].sem, 1)

                def x1_low(g):
                    dve.wait_ge(x1t_h[g].sem, now(x1t_h[g]))
                    dve.wait_ge(g_mm[g].sem, prev(g_mm[g]))
                    dve.wait_ge(h_mm[g].sem, prev(h_mm[g]))
                    dve.tensor_tensor(x1t_lo[:, g, :, :].rearrange("p c n -> p (c n)"), tp_bank(f"x1t{g}")[:, 0:D],
                                      x1t_hi[:, g, :, :].rearrange("p c n -> p (c n)").bitcast(F32), ALU.subtract)\
                        .then_inc(x1t_l[g].sem, 1)

                def hidden_residue(g):
                    dve.wait_ge(h_done[0][g].sem, now(h_done[0][g]))
                    dve.wait_ge(h_done[2][g].sem, prev(h_done[2][g]))
                    dve.tensor_tensor(h_res[:, g, :].rearrange("p (a e) -> p a e", a=H1),
                                      lin_bank(f"h{g}")[:, 0:D].rearrange("p (a e) -> p a e", a=H1),
                                      h_part[0][:, g, :, 0:E1], ALU.subtract).then_inc(h_r[g].sem, 1)

                def value_residue(g):
                    dve.wait_ge(v_done[0][g].sem, now(v_done[0][g]))
                    dve.wait_ge(v_done[2][g].sem, prev(v_done[2][g]))
                    dve.tensor_tensor(v_res[:, g, :].rearrange("p (a e) -> p a e", a=H0),
                                      lin_bank(f"v{g}")[:, 0:D].rearrange("p (a e) -> p a e", a=H0),
                                      v_part[0][:, g, :, 0:E0], ALU.subtract).then_inc(v_r[g].sem, 1)

                def source_target_sums(g):
                    dve.wait_ge(sd_prod[g].sem, now(sd_prod[g]))
                    dve.tensor_reduce(sd[:, g, :, :], prod[:, g, :].rearrange("p (s a e) -> p s a e", s=2, a=H1),
                                      AX.X, ALU.add).then_inc(sd_sum[g].sem, 1)

                def source_target_part1():
                    dve.wait_ge(sd_sum[0].sem, now(sd_sum[0]))
                    dve.wait_ge(sd_sum[1].sem, now(sd_sum[1]))
                    dve.wait_ge(sdt_mm.sem, prev(sdt_mm))
                    for g in range(2):
                        last = dve.tensor_copy(sd_parts[:, g, :, 0:H1], sd[:, g, :, :])
                    last.then_inc(sd_1.sem, 1)

                def source_target_residue():
                    dve.wait_ge(sd_1.sem, now(sd_1))
                    for g in range(2):
                        last = dve.tensor_tensor(sd_res[:, g, :, :], sd[:, g, :, :], sd_parts[:, g, :, 0:H1], ALU.subtract)
                    last.then_inc(sd_r.sem, 1)

                def source_target_part2():
                    dve.wait_ge(sd_r.sem, now(sd_r))
                    for g in range(2):
                        last = dve.tensor_copy(sd_parts[:, g, :, H1:2 * H1], sd_res[:, g, :, :])
                    last.then_inc(sd_2.sem, 1)

                def source_target_part3():
                    dve.wait_ge(sd_2.sem, now(sd_2))
                    for g in range(2):
                        last = dve.tensor_tensor(sd_parts[:, g, :, 2 * H1:3 * H1], sd_res[:, g, :, :],
                                                 sd_parts[:, g, :, H1:2 * H1], ALU.subtract)
                    last.then_inc(sd_3.sem, 1)

                def target_copy():
                    dve.wait_ge(src_ready.sem, now(src_ready))
                    for step in dst_flat:
                        dve.wait_ge(step.sem, prev(step))
                    dve.tensor_copy(dst_t[64:100, :, :].rearrange("p g n -> p (g n)"),
                                    tp_bank("sdt")[:, :].bitcast(BF16)[64:100, 0:2 * N]).then_inc(dst_ready.sem, 1)

                def scores_max(g):
                    dve.wait_ge(sc_mm[g].sem, now(sc_mm[g]))
                    s = zp[:, 0:2, :].rearrange("p b n -> p (b n)")[:, 0:H0 * N].rearrange("p (a n) -> p a n", a=H0)
                    dve.tensor_reduce(p0_max[:, g, :], s, AX.X, ALU.max).then_inc(sc_max[g].sem, 1)

                def scores_shift(g):
                    dve.wait_ge(sc_max[g].sem, now(sc_max[g]))
                    dve.wait_ge(sc_exp[g].sem, prev(sc_exp[g]))
                    dve.tensor_scalar(p0_shift[:, g, :], p0_max[:, g, :], -SCALE0, None, ALU.mult)\
                        .then_inc(sc_shift[g].sem, 1)

                def weights0_low(g, half):
                    bank = tp_bank(f"pt{g}{half}")
                    c = slice(3 * N * half, 3 * N * (half + 1))
                    dve.wait_ge(pt_hi[half][g].sem, now(pt_hi[half][g]))
                    dve.wait_ge(ctx_mm[g].sem, prev(ctx_mm[g]))
                    dve.scalar_tensor_tensor(out=p0t_lo[:, g, c], in0=bank[:, 0:3 * N], scalar=PSCALE,
                                             in1=p0t_hi[:, g, c], op0=ALU.mult, op1=ALU.subtract)\
                        .then_inc(pt_lo[half][g].sem, 1)

                def context_inverse(g):
                    dve.wait_ge(ctx_mm[g].sem, now(ctx_mm[g]))
                    s = fp[:, 0:H0 * (E0 + 1)].rearrange("p (a e) -> p a e", a=H0)
                    dve.reciprocal(ctx_rcp[:, g, :].unsqueeze(2), s[:, :, E0:]).then_inc(ctx_inv[g].sem, 1)

                def context_norm(g):
                    dve.wait_ge(ctx_inv[g].sem, now(ctx_inv[g]))
                    s = fp[:, 0:H0 * (E0 + 1)].rearrange("p (a e) -> p a e", a=H0)
                    dve.tensor_tensor(ctx_n[:, g, :].rearrange("p (a e) -> p a e", a=H0), s[:, :, 0:E0],
                                      ctx_rcp[:, g, :].unsqueeze(2).to_broadcast([128, H0, E0]), ALU.mult)\
                        .then_inc(ctx_ready[g].sem, 1)

                def context_low(g):
                    dve.wait_ge(ct_hi[g].sem, now(ct_hi[g]))
                    dve.wait_ge(pr_mm[g].sem, prev(pr_mm[g]))
                    dve.tensor_tensor(ctx_lo[:, g, :, :].rearrange("p c n -> p (c n)"), tp_bank(f"ct{g}")[:, 0:D],
                                      ctx_hi[:, g, :, :].rearrange("p c n -> p (c n)").bitcast(F32), ALU.subtract)\
                        .then_inc(ct_lo[g].sem, 1)

                def add_residual(g):
                    dve.wait_ge(pr_mm[g].sem, now(pr_mm[g]))
                    dve.wait_ge(x_bf_ready.sem, now(x_bf_ready))
                    dve.wait_ge(x1_ready[g].sem, prev(x1_ready[g]))
                    dve.tensor_tensor(y[:, g, :], lin_bank(f"pr{g}")[:, 0:D], x_bf[:, g, :], ALU.add).then_inc(y_ready[g].sem, 1)

                def stats0(g):
                    dve.wait_ge(y_ready[g].sem, now(y_ready[g]))
                    dve.bn_stats(stats[:, g, :], y[:, g, :]).then_inc(y_stats[g].sem, 1)

                def moments0(g):
                    dve.wait_ge(y_stats[g].sem, now(y_stats[g]))
                    turn.apart()
                    dve.bn_aggr(moments[:, g, :], stats[:, g, :]).then_inc(y_mom[g].sem, 1)

                def variance0(g):
                    dve.wait_ge(y_mom[g].sem, now(y_mom[g]))
                    dve.tensor_scalar(rstd[:, g, :], moments[:, g, 1:2], EPS, None, ALU.add).then_inc(y_var[g].sem, 1)

                def shift_norm0(g):
                    dve.wait_ge(y_rstd[g].sem, now(y_rstd[g]))
                    dve.wait_ge(x1_ready[g].sem, prev(x1_ready[g]))
                    dve.scalar_tensor_tensor(out=shift0[:, g, :], in0=moments[:, g, 0:1], scalar=-1.0,
                                             in1=rstd[:, g, :], op0=ALU.mult, op1=ALU.mult)\
                        .then_inc(norm0_shift[g].sem, 1)

                def z_leak(g):
                    dve.wait_ge(z_copied[g].sem, now(z_copied[g]))
                    dve.scalar_tensor_tensor(out=z[:, g, :], in0=z[:, g, :], scalar=0.2, in1=z[:, g, :],
                                             op0=ALU.mult, op1=ALU.max).then_inc(z_leaky[g].sem, 1)

                def z_maxima(g):
                    dve.wait_ge(z_leaky[g].sem, now(z_leaky[g]))
                    dve.wait_ge(z_sub[g].sem, prev(z_sub[g]))
                    dve.tensor_reduce(z_max[:, g, :], z[:, g, :].rearrange("p (a n) -> p a n", a=H1),
                                      AX.X, ALU.max).then_inc(z_maxed[g].sem, 1)

                def weights1_low(g, k):
                    bank = tp_bank(f"wt{g}{k}")
                    c = slice(4 * N * k, 4 * N * (k + 1))
                    dve.wait_ge(wt_hi[k][g].sem, now(wt_hi[k][g]))
                    dve.wait_ge(f_mm[g].sem, prev(f_mm[g]))
                    dve.scalar_tensor_tensor(out=p1t_lo[:, g, c], in0=bank[:, :], scalar=PSCALE,
                                             in1=p1t_hi[:, g, c], op0=ALU.mult, op1=ALU.subtract)\
                        .then_inc(wt_lo[k][g].sem, 1)

                def features_inverse(g):
                    dve.wait_ge(f_mm[g].sem, now(f_mm[g]))
                    s = fp[:, 0:H1 * (E1 + 1)].rearrange("p (a e) -> p a e", a=H1)
                    dve.reciprocal(f_rcp[:, g, :].unsqueeze(2), s[:, :, E1:]).then_inc(f_inv[g].sem, 1)

                def features_norm(g):
                    dve.wait_ge(f_inv[g].sem, now(f_inv[g]))
                    s = fp[:, 0:H1 * (E1 + 1)].rearrange("p (a e) -> p a e", a=H1)
                    dve.wait_ge(f_diff[g].sem, prev(f_diff[g]))
                    dve.tensor_tensor(f[:, g, :].rearrange("p (a e) -> p a e", a=H1), s[:, :, 0:E1],
                                      f_rcp[:, g, :].unsqueeze(2).to_broadcast([128, H1, E1]), ALU.mult)\
                        .then_inc(f_norm[g].sem, 1)

                def elu(g):
                    dve.wait_ge(f_exp[g].sem, now(f_exp[g]))
                    dve.scalar_tensor_tensor(out=f[:, g, :], in0=f_neg[:, g, :], scalar=-1.0, in1=f[:, g, :],
                                             op0=ALU.add, op1=ALU.max).then_inc(f_elu[g].sem, 1)

                def mix(g):
                    dve.wait_ge(f_gated[g].sem, now(f_gated[g]))
                    dve.wait_ge(x1_copied[g].sem, prev(x1_copied[g]))
                    dve.wait_ge(out_ready[g].sem, prev(out_ready[g]))
                    dve.scalar_tensor_tensor(out=y2[:, g, :], in0=f[:, g, :], scalar=0.25, in1=x1_kept[:, g, :],
                                             op0=ALU.mult, op1=ALU.add).then_inc(y2_ready[g].sem, 1)

                def stats1(g):
                    dve.wait_ge(y2_ready[g].sem, now(y2_ready[g]))
                    dve.bn_stats(stats2[:, g, :], y2[:, g, :]).then_inc(y2_stats[g].sem, 1)

                def moments1(g):
                    dve.wait_ge(y2_stats[g].sem, now(y2_stats[g]))
                    turn.apart()
                    dve.bn_aggr(moments2[:, g, :], stats2[:, g, :]).then_inc(y2_mom[g].sem, 1)

                def variance1(g):
                    dve.wait_ge(y2_mom[g].sem, now(y2_mom[g]))
                    dve.tensor_scalar(rstd2[:, g, :], moments2[:, g, 1:2], EPS / 4, None, ALU.add)\
                        .then_inc(y2_var[g].sem, 1)

                def shift_norm1(g):
                    dve.wait_ge(y2_rstd[g].sem, now(y2_rstd[g]))
                    dve.wait_ge(out_ready[g].sem, prev(out_ready[g]))
                    dve.scalar_tensor_tensor(out=shift1[:, g, :], in0=moments2[:, g, 0:1], scalar=-1.0,
                                             in1=rstd2[:, g, :], op0=ALU.mult, op1=ALU.mult)\
                        .then_inc(norm1_shift[g].sem, 1)

                if layer0:
                    value_residue(0)
                if after1:
                    weights1_low(0, 0)
                    weights1_low(0, 1)
                if layer0:
                    queries_keys(0)
                if after1:
                    weights1_low(0, 2)
                if layer1:
                    x1_low(0)
                if layer0:
                    queries_keys(1)
                if after1:
                    features_inverse(0)
                    features_norm(0)
                if layer0:
                    queries_keys(2)
                if after1:
                    weights1_low(1, 0)
                if layer1:
                    x1_low(1)
                    hidden_residue(0)
                if layer0:
                    scores_max(0)
                if after1:
                    elu(0)
                if layer1:
                    source_target_sums(0)
                if layer0:
                    scores_shift(0)
                if after1:
                    weights1_low(1, 2)
                    weights1_low(1, 1)
                if layer1:
                    source_target_sums(1)
                    source_target_part1()
                    source_target_residue()
                    source_target_part2()
                    source_target_part3()
                if layer0:
                    scores_max(1)
                if layer1:
                    target_copy()
                if layer0:
                    scores_shift(1)
                if after1:
                    mix(0)
                    stats1(0)
                if layer0:
                    weights0_low(0, 0)
                if after1:
                    moments1(0)
                    features_inverse(1)
                    variance1(0)
                    features_norm(1)
                if layer0:
                    weights0_low(0, 1)
                    weights0_low(1, 0)
                if layer1:
                    hidden_residue(1)
                if layer0:
                    value_residue(1)
                if after1:
                    shift_norm1(0)
                if layer0:
                    context_inverse(0)
                    context_norm(0)
                if layer1:
                    z_leak(0)
                if layer0:
                    weights0_low(1, 1)
                if after1:
                    elu(1)
                if layer1:
                    z_maxima(0)
                if layer0:
                    context_low(0)
                    context_inverse(1)
                if layer1:
                    z_leak(1)
                if layer0:
                    context_norm(1)
                if layer1:
                    z_maxima(1)
                if layer0:
                    context_low(1)
                if after1:
                    mix(1)
                    stats1(1)
                if layer0:
                    add_residual(0)
                if after1:
                    moments1(1)
                if layer0:
                    stats0(0)
                if after1:
                    variance1(1)
                if layer0:
                    add_residual(1)
                    moments0(0)
                if after1:
                    shift_norm1(1)
                if layer0:
                    variance0(0)
                    stats0(1)
                    moments0(1)
                    variance0(1)
                    shift_norm0(0)
                    shift_norm0(1)

            turns(dve, passed, body)

        @block.gpsimd
        def _(pool):
            pool.memset(ident[:, :], 1.0).then_inc(ones_ready.sem, 1)
            pool.memset(ident_bf[:, :], 1.0).then_inc(ones_ready.sem, 1)
            pool.wait_ge(ones_ready.sem, 4)
            for tile in (ident, ident_bf):
                pool.affine_select(out=tile[:, :], in_=tile[:, :], compare_op=ALU.is_equal, fill=0.0, base=0,
                                   pattern=[[-1, 128]], channel_multiplier=1).then_inc(consts_ready.sem, 1)
            for g in range(2):
                for part in range(3):
                    last = pool.affine_select(out=dst_row[0:36, g, :, :], in_=dst_row[0:36, g, :, :],
                                              compare_op=ALU.not_equal, fill=1.0, base=-H1 * part,
                                              pattern=[[-1, H1], [0, N]], channel_multiplier=1)
                    last.then_inc(ones_ready.sem, 1)
                    pool.wait_ge(ones_ready.sem, 5 + 3 * g + part)
            pool.memset(rstd[:, :, :], 1.0).then_inc(consts_ready.sem, 1)
            pool.wait_ge(small_loaded.sem, 16 * SMALL)
            pool.wait_ge(fills_ready.sem, 1)

            def body(turn):
                now, prev = turn.now, turn.prev
                prepare, layer0, layer1, after1 = (turn.runs(stage) for stage in (-1, 0, 1, 2))

                def residual_bias():
                    for step in y_ready:
                        pool.wait_ge(step.sem, prev(step))
                    pool.wait_ge(x_loaded.sem, prev(x_loaded))
                    for g in range(2):
                        last = pool.tensor_tensor(x_bf[:, g, :], x_raw[:, g, :], rows["bf"][:, :], ALU.add)
                    last.then_inc(x_bf_ready.sem, 1)

                def mask0_bias():
                    pool.wait_ge(adj0_loaded.sem, prev(adj0_loaded))
                    pool.wait_ge(sc_mm[1].sem, prev(sc_mm[1]))
                    turn.apart()
                    pool.tensor_scalar(mask0[:, :, :], adj0[:, :, :], -1.0, MASKED, ALU.add, ALU.mult)\
                        .then_inc(mask0_ready.sem, 1)

                def mask1_bias():
                    pool.wait_ge(adj1_loaded.sem, prev(adj1_loaded))
                    pool.wait_ge(z_mm[1].sem, prev(z_mm[1]))
                    turn.apart()
                    pool.tensor_scalar(mask1[:, :, :], adj1[:, :, :], -1.0, MASKED, ALU.add, ALU.mult)\
                        .then_inc(mask1_ready.sem, 1)

                def source_target_products(g):
                    pool.wait_ge(h_tanh[g].sem, now(h_tanh[g]))
                    pool.wait_ge(sd_sum[g].sem, prev(sd_sum[g]))
                    pool.tensor_tensor(prod[:, g, :].rearrange("p (s d) -> p s d", s=2),
                                       th[:, g:g + 1, :].to_broadcast([128, 2, D]),
                                       rows["w_sd"][:, :].rearrange("p (s d) -> p s d", s=2), ALU.mult)\
                        .then_inc(sd_prod[g].sem, 1)

                def hidden_part3(g):
                    pool.wait_ge(h_done[1][g].sem, now(h_done[1][g]))
                    pool.wait_ge(f_mm[g].sem, now(f_mm[g]))
                    pool.tensor_tensor(h_part[2][:, g, :, 0:E1], h_res[:, g, :].rearrange("p (a e) -> p a e", a=H1),
                                       h_part[1][:, g, :, 0:E1], ALU.subtract).then_inc(h_done[2][g].sem, 1)

                def value_part3(g):
                    pool.wait_ge(v_done[1][g].sem, now(v_done[1][g]))
                    pool.tensor_tensor(v_part[2][:, g, :, 0:E0], v_res[:, g, :].rearrange("p (a e) -> p a e", a=H0),
                                       v_part[1][:, g, :, 0:E0], ALU.subtract).then_inc(v_done[2][g].sem, 1)

                def next_x_low():
                    pool.wait_ge(xt_hi_made.sem, now(xt_hi_made))
                    pool.tensor_tensor(xt_lo[:, :, :].rearrange("p c n -> p (c n)"),
                                       xt_raw[:, :, :].rearrange("p c n -> p (c n)"),
                                       xt_hi[:, :, :].rearrange("p c n -> p (c n)").bitcast(F32), ALU.subtract)\
                        .then_inc(xt_split.sem, 1)

                def deviation0(g):
                    pool.wait_ge(y_var[g].sem, now(y_var[g]))
                    pool.tensor_tensor(rstd[:, g, :], rstd[:, g, :], half_neg[:, :], ALU.pow).then_inc(y_rstd[g].sem, 1)

                def deviation1(g):
                    pool.wait_ge(y2_var[g].sem, now(y2_var[g]))
                    pool.tensor_tensor(rstd2[:, g, :], rstd2[:, g, :], half_neg[:, :], ALU.pow).then_inc(y2_rstd[g].sem, 1)

                def z_subtract(g):
                    pool.wait_ge(z_maxed[g].sem, now(z_maxed[g]))
                    zs = z[:, g, :].rearrange("p (a n) -> p a n", a=H1)
                    pool.tensor_tensor(zs, zs, z_max[:, g, :].unsqueeze(2).to_broadcast([128, H1, N]), ALU.subtract)\
                        .then_inc(z_sub[g].sem, 1)

                def features_bias(g):
                    pool.wait_ge(f_norm[g].sem, now(f_norm[g]))
                    fs = f[:, g, :].rearrange("p (a e) -> p a e", a=H1)
                    pool.tensor_tensor(fs, fs, rows["b1"][:, :].unsqueeze(1).to_broadcast([128, H1, E1]), ALU.add)\
                        .then_inc(f_bias[g].sem, 1)

                def features_negative(g):
                    pool.wait_ge(f_bias[g].sem, now(f_bias[g]))
                    pool.wait_ge(f_elu[g].sem, prev(f_elu[g]))
                    turn.apart()
                    pool.tensor_scalar(f_neg[:, g, :], f[:, g, :], 0.0, None, ALU.min).then_inc(f_min[g].sem, 1)

                def features_difference(g):
                    pool.wait_ge(f_elu[g].sem, now(f_elu[g]))
                    pool.wait_ge(x1_copied[g].sem, prev(x1_copied[g]))
                    pool.tensor_tensor(f[:, g, :], f[:, g, :], x1_kept[:, g, :], ALU.subtract).then_inc(f_diff[g].sem, 1)

                def gated_features(g):
                    pool.wait_ge(f_diff[g].sem, now(f_diff[g]))
                    pool.wait_ge(g_plus[g].sem, prev(g_plus[g]))
                    pool.tensor_tensor(f[:, g, :], f[:, g, :], gate[:, g, :], ALU.mult).then_inc(f_gated[g].sem, 1)

                if layer0:
                    residual_bias()
                if layer1:
                    mask1_bias()
                if layer0:
                    mask0_bias()
                if after1:
                    features_bias(0)
                    features_negative(0)
                if layer1:
                    source_target_products(0)
                    source_target_products(1)
                if layer0:
                    value_part3(0)
                if after1:
                    features_difference(0)
                    gated_features(0)
                    deviation1(0)
                    features_bias(1)
                    features_negative(1)
                if prepare:
                    next_x_low()
                if layer0:
                    value_part3(1)
                if layer1:
                    hidden_part3(0)
                if after1:
                    features_difference(1)
                    gated_features(1)
                if layer1:
                    z_subtract(0)
                    z_subtract(1)
                if after1:
                    deviation1(1)
                if layer0:
                    deviation0(0)
                    deviation0(1)
                if layer1:
                    hidden_part3(1)

            turns(pool, passed, body)


def kernel(x, adj, L0_gnn_Wq, L0_gnn_bq, L0_gnn_Wk, L0_gnn_bk, L0_gnn_Wv, L0_gnn_bv, L0_gnn_Wf, L0_gnn_bf,
           L1_gnn_W, L1_gnn_b, L1_gnn_w_src, L1_gnn_w_dst, L1_gnn_H_w, L1_gnn_H_b):
    import numpy as np
    import concourse.bacc as bacc
    from concourse.bass_utils import run_bass_kernel_spmd

    nc = bacc.Bacc("TRN2", target_bir_lowering=False, num_devices=1)
    arrays = {}

    def given(name, a):
        a = np.ascontiguousarray(a)
        arrays[name] = a
        return nc.dram_tensor(name, a.shape, mybir.dt.from_np(a.dtype), kind="ExternalInput").ap()

    def chunked(a):
        return np.asarray(a).reshape(C, 128, D).transpose(1, 0, 2).reshape(128, C * D)

    x, adj = np.asarray(x), np.asarray(adj)
    x_d = given("x", x)
    x_t = given("x_t", x.reshape(PAIRS, 2 * N, C, 128).transpose(0, 3, 2, 1))
    adj_d = given("adj", adj)
    weights = {
        "Wq": given("Wq", chunked(L0_gnn_Wq)),
        "Wk": given("Wk", chunked(L0_gnn_Wk)),
        "Wv": given("Wv", chunked(L0_gnn_Wv)),
        "Wf": given("Wf", chunked(L0_gnn_Wf)),
        "W1": given("W1", chunked(np.asarray(L1_gnn_W).transpose(1, 0, 2).reshape(D, D))),
        "Hw": given("Hw", chunked(np.asarray(L1_gnn_H_w).T)),
    }
    biases = {
        "bq": given("bq", np.asarray(L0_gnn_bq).reshape(C, 128).T),
        "bk": given("bk", np.asarray(L0_gnn_bk).reshape(C, 128).T),
    }
    w_sd = np.concatenate([np.asarray(L1_gnn_w_src).reshape(D), np.asarray(L1_gnn_w_dst).reshape(D)])
    row_biases = {"bv": given("bv", L0_gnn_bv), "bf": given("bf", L0_gnn_bf), "b1": given("b1", L1_gnn_b),
                  "Hb": given("Hb", L1_gnn_H_b), "w_sd": given("w_sd", w_sd)}
    out = nc.dram_tensor("out", (GRAPHS, N, D), F32, kind="ExternalOutput").ap()
    two_layer_graph_attention(nc, x_d, x_t, adj_d, weights, biases, row_biases, out)
    r = run_bass_kernel_spmd(nc, [arrays], core_ids=[0])
    return r.results[0]["out"]
```

```python
from contextlib import ExitStack

import concourse.bass as bass
from concourse import mybir

F32 = mybir.dt.float32
F32R = mybir.dt.float32r
BF16 = mybir.dt.bfloat16
F16 = mybir.dt.float16
U8 = mybir.dt.uint8
ALU = mybir.AluOpType
ACT = mybir.ActivationFunctionType
AX = mybir.AxisListType

GRAPHS, N, D = 64, 128, 384
PAIRS = GRAPHS // 2
C = D // 128
H0 = 6
E0 = D // H0
H1 = 12
E1 = D // H1
EPS = 1e-5
SCALE0 = float(E0) ** -0.5
MASKED = 9e15 / SCALE0
PSCALE = 16384.0
WEIGHTS = ("Wq", "Wk", "Wv", "Wf", "W1", "Hw")
DONE_BY_DMA = 16
SMALL = 5


class Signal:

    def __init__(self, sem, stage, unit, back=0):
        self.sem, self.stage, self.unit, self.back = sem, stage, unit, back


class Turn:

    def __init__(self, eng, t, passed, counts):
        self.eng, self.t, self.passed, self.counts, self.loop = eng, t, passed, counts, not isinstance(t, int)
        self.behind = 0
        if self.loop:
            self.registers = {(turns, unit, back): eng.snap((t + turns) * unit - back)
                              for turns, unit, back in sorted(counts)}

    def count(self, step, turns):
        turns -= self.behind
        if not self.loop:
            self.counts.add((turns, step.unit, step.back))
            return max(min(self.t + turns, PAIRS) * step.unit - step.back, 0)
        return self.registers[turns, step.unit, step.back]

    def now(self, step):
        return self.count(step, 1 - step.stage)

    def prev(self, step):
        return self.count(step, -step.stage)

    def runs(self, stage, back=0):
        return self.loop or 0 <= self.t - back - stage < PAIRS

    def step(self, stage, function, *which):
        if self.runs(stage):
            function(*which)

    def late(self, stage, function, *which):
        if self.runs(stage, 1):
            self.behind = 1
            function(*which)
            self.behind = 0

    def starts(self, stage):
        return not self.loop and self.pair(stage) == 0

    def pair(self, stage):
        return self.t - self.behind - stage

    def apart(self):
        if self.loop:
            self.eng.sem_inc(self.passed, 1)


def turns(eng, passed, body, prepare=None):
    counts = set()
    for t in range(-1, 4):
        body(Turn(eng, t, passed, counts))
        if t == -1 and prepare:
            prepare()
    with eng.Fori(4, PAIRS - 1) as t:
        body(Turn(eng, t, passed, counts))
    for t in range(PAIRS - 1, PAIRS + 3):
        body(Turn(eng, t, passed, counts))


LIN_USERS = ("g1", "pr0", "pr1", "qk0", "qk1", "v0", "qk2", "h0", "h1", "v1", "g0")
TP_USERS = ("ct1", "wt00", "wt01", "wt02", "x1t0", "wt10", "x1t1", "wt11", "wt12", "pt01", "sdt", "pt00",
             "pt11", "pt10", "ct0")
ZP_USERS = ("z1", "sc0", "sc1", "z0")
FP_USERS = ("f0", "f1", "ctx0", "ctx1")

LATE_USERS = ("g1", "z1", "ct1", "pr0", "pr1")


def bank_of(users, user, banks=2):
    return users.index(user) % banks


def last_reader(turn, users, user, readers, banks=2):
    at, n = users.index(user), len(users)
    for back in range(1, 3 * n):
        i = (at - back) % n
        turns_back = (i + back - at) // n
        step = readers[users[i]]
        turns_back += users[i] in LATE_USERS
        if i % banks == at % banks and turn.runs(step.stage, turns_back):
            return step, turn.count(step, 1 - step.stage - turns_back + turn.behind)
    return None


def two_layer_graph_attention(nc, x, x_t, adj, weights, biases, row_biases, out):
    with ExitStack() as ctx:
        def sb(name, shape, dt=F32):
            return ctx.enter_context(nc.sbuf_tensor(name, shape, dt))

        def signal(name, stage, unit=2):
            return Signal(ctx.enter_context(nc.semaphore(name)), stage, unit)

        def pair_of(name, stage):
            sem = ctx.enter_context(nc.semaphore(name))
            return [Signal(sem, stage, 2, 1 - g) for g in range(2)]

        w_hi = {n: sb(f"{n}_hi", [128, C, D], F32R) for n in WEIGHTS}
        w_lo = {n: sb(f"{n}_lo", [128, C, D], F32R) for n in WEIGHTS}
        column = {n: sb(f"{n}_col", [128, C]) for n in ("bq", "bk", "bv")}
        rows = {n: sb(f"{n}_rows", [128, size]) for n, size in
                (("b1", E1), ("w_sd", 2 * D))}
        ident = sb("ident", [128, 128])
        ident_bf = sb("ident_bf", [128, 128], BF16)
        row_head = sb("row_head", [36, H1], BF16)
        half_neg = sb("half_neg", [128, 1])
        bias_rows = sb("bias_rows", [3, 2, D], BF16)
        ones_bf = sb("ones_bf", [3, 128], BF16)

        xt_raw = sb("xt_raw", [128, C, 2 * N])
        xt_hi = sb("xt_hi", [128, C, 2 * N], F32R)
        xt_lo = sb("xt_lo", [128, C, 2 * N], F32R)
        x_raw = sb("x_raw", [128, 2, D])
        adj0 = sb("adj0", [128, 2, N], U8)
        adj1 = sb("adj1", [128, 2, N], U8)
        mask0 = sb("mask0", [128, 2, N], BF16)
        mask1 = sb("mask1", [128, 2, N], BF16)
        q_hi = sb("q_hi", [128, C, 2 * N], F32R)
        q_lo = sb("q_lo", [128, C, 2 * N], F32R)
        k_hi = sb("k_hi", [128, C, 2, 2, N], F32R)
        k_lo = sb("k_lo", [128, C, 2, 2, N], F32R)
        v_res = sb("v_res", [128, 2, D])
        v_part = [sb(f"v_part{i}", [128, 2, H0, E0 + 1], BF16) for i in range(3)]
        p0 = sb("p0", [128, 2, H0 * N])
        p0_max = sb("p0_max", [128, 2, H0])
        p0_shift = sb("p0_shift", [128, 2, H0])
        p0t_hi = sb("p0t_hi", [128, 2, H0 * N], F16)
        p0t_lo = sb("p0t_lo", [128, 2, H0 * N], F16)
        ctx_rcp = sb("ctx_rcp", [128, 2, H0])
        ctx_n = sb("ctx_n", [128, 2, D])
        ctx_hi = sb("ctx_hi", [128, 2, C, N], F32R)
        ctx_lo = sb("ctx_lo", [128, 2, C, N], F32R)
        y = sb("y", [128, 2, D])
        stats = sb("stats", [128, 2, 6])
        moments = sb("moments", [128, 2, 2])
        rstd = sb("rstd", [128, 2, 1])
        shift0 = sb("shift0", [128, 2, 1])
        x1 = sb("x1", [128, 2, D])

        x1_kept = sb("x1_kept", [128, 2, D])
        x1t_hi = sb("x1t_hi", [128, 2, C, N], F32R)
        x1t_lo = sb("x1t_lo", [128, 2, C, N], F32R)
        th = sb("th", [128, 2, D])
        h_part = [sb(f"h_part{i}", [128, 2, H1, E1 + 1], BF16) for i in range(3)]
        h_res = sb("h_res", [128, 2, D])
        prod = sb("prod", [128, 2, 2 * D])
        sd = sb("sd", [128, 2, 2, H1])
        sd_res = sb("sd_res", [128, 2, 2, H1])
        sd_parts = sb("sd_parts", [128, 2, 2, 64], BF16)
        sd_t = sb("sd_t", [64 + 3 * H1, 2, N], BF16)
        dst_row = sb("dst_row", [3 * H1 + 3, 2, H1, N], BF16)
        z = sb("z", [128, 2, H1 * N])
        z_max = sb("z_max", [128, 2, H1])
        p1t_hi = sb("p1t_hi", [128, 2, H1 * N], F16)
        p1t_lo = sb("p1t_lo", [128, 2, H1 * N], F16)
        f_rcp = sb("f_rcp", [128, 2, H1])
        f = sb("f", [128, 2, D])
        f_neg = sb("f_neg", [128, 2, D])
        gate = sb("gate", [128, 2, D])
        y2 = sb("y2", [128, 2, D])
        stats2 = sb("stats2", [128, 2, 6])
        moments2 = sb("moments2", [128, 2, 2])
        rstd2 = sb("rstd2", [128, 2, 1])
        shift1 = sb("shift1", [128, 2, 1])
        out_tile = sb("out_tile", [128, 2, D])
        bias_row, bias_res = y2[0:1, :, :], out_tile[0:1, :, :]
        bias_parts = p1t_hi[0:1, :, :].rearrange("p g n -> p (g n)").bitcast(BF16)[:, 0:3 * 2 * D]\
            .rearrange("p (i s d) -> p i s d", i=3, s=2)

        lin = [ctx.enter_context(nc.psum_tensor(f"lin{i}", [128, 512], F32)) for i in range(2)]
        tp = [ctx.enter_context(nc.psum_tensor(f"tp{i}", [128, 512], F32)) for i in range(2)]
        zp = ctx.enter_context(nc.psum_tensor("zp", [128, 3, 512], F32))
        fp = ctx.enter_context(nc.psum_tensor("fp", [128, 512], F32))

        w_loaded = {n: signal(f"{n}_loaded", 0, 1) for n in WEIGHTS}
        w_hi_ready = {n: signal(f"{n}_hi_ready", 0, 1) for n in WEIGHTS}
        w_lo_ready = {n: signal(f"{n}_lo_ready", 0, 1) for n in WEIGHTS}
        small_loaded = signal("small_loaded", 0, 1)
        bv_ready = signal("bv_ready", 0, 1)
        bv_mm = signal("bv_mm", 0, 1)
        bias_row_loaded = signal("bias_row_loaded", 0, 1)
        bias_split = signal("bias_split", 0, 1)
        bias_loaded = signal("bias_loaded", 0, 1)
        ones_ready = signal("ones_ready", 0, 1)
        heads_ready = signal("heads_ready", 0, 1)
        flat_ready = signal("flat_ready", 0, 1)
        consts_ready = signal("consts_ready", 0, 1)
        fills_ready = signal("fills_ready", 0, 1)
        passed = ctx.enter_context(nc.semaphore("passed"))

        xt_loaded = signal("xt_loaded", -1, DONE_BY_DMA)
        x_loaded = signal("x_loaded", -1, DONE_BY_DMA)
        adj0_loaded = signal("adj0_loaded", -1, DONE_BY_DMA)
        xt_split = signal("xt_split", -1)
        xt_hi_made = signal("xt_hi_made", -1)
        adj1_loaded = signal("adj1_loaded", 0, DONE_BY_DMA)
        mask0_ready = signal("mask0_ready", 0)
        qk_mm = [signal(f"qk_mm{j}", 0) for j in range(C)]
        qk_hi = [signal(f"qk_hi{j}", 0) for j in range(C)]
        qk_lo = [signal(f"qk_lo{j}", 0) for j in range(C)]
        sc_mm, sc_max = pair_of("sc_mm", 0), pair_of("sc_max", 0)
        sc_shift, sc_exp = pair_of("sc_shift", 0), pair_of("sc_exp", 0)
        v_mm, v_raw, v_r = pair_of("v_mm", 0), pair_of("v_raw", 0), pair_of("v_r", 0)
        v_done = [pair_of(f"v_done{i}", 0) for i in range(3)]
        pt_mm = [pair_of(f"pt_mm{k}", 0) for k in range(2)]
        pt_hi = [pair_of(f"pt_hi{k}", 0) for k in range(2)]
        pt_lo = [pair_of(f"pt_lo{k}", 0) for k in range(2)]
        ctx_mm, ctx_inv, ctx_ready = pair_of("ctx_mm", 0), pair_of("ctx_inv", 0), pair_of("ctx_ready", 0)
        ct_mm, ct_hi, ct_lo = pair_of("ct_mm", 0), pair_of("ct_hi", 0), pair_of("ct_lo", 0)
        pr_mm, y_ready, y_stats = pair_of("pr_mm", 0), pair_of("y_ready", 0), pair_of("y_stats", 0)
        y_mom, y_var, y_rstd = pair_of("y_mom", 0), pair_of("y_var", 0), pair_of("y_rstd", 0)
        x1_ready = pair_of("x1_ready", 0)

        mask1_ready = signal("mask1_ready", 1)
        x1_copied = pair_of("x1_copied", 1)
        x1t_mm, x1t_h, x1t_l = pair_of("x1t_mm", 1), pair_of("x1t_h", 1), pair_of("x1t_l", 1)
        h_mm, h_tanh, h_r = pair_of("h_mm", 1), pair_of("h_tanh", 1), pair_of("h_r", 1)
        h_raw = pair_of("h_raw", 1)
        h_done = [pair_of(f"h_done{i}", 1) for i in range(3)]
        g_mm, g_tanh, g_plus = pair_of("g_mm", 1), pair_of("g_tanh", 1), pair_of("g_plus", 1)
        sd_prod, sd_sum = pair_of("sd_prod", 1), pair_of("sd_sum", 1)
        sd_1, sd_r, sd_2, sd_3 = (signal(f"sd_{i}", 1) for i in ("part1", "res", "part2", "part3"))
        sdt_mm, sd_copied = signal("sdt_mm", 1), signal("sd_copied", 1)
        dst_flat = [signal(f"dst_flat{g}", 1, 3 * DONE_BY_DMA) for g in range(2)]
        z_mm, z_maxed = pair_of("z_mm", 1), pair_of("z_maxed", 1)
        z_copied, z_leaky = pair_of("z_copied", 1), pair_of("z_leaky", 1)
        z_sub, z_exp = pair_of("z_sub", 1), pair_of("z_exp", 1)
        wt_mm = [pair_of(f"wt_mm{k}", 2) for k in range(3)]
        wt_hi = [pair_of(f"wt_hi{k}", 2) for k in range(3)]
        wt_lo = [pair_of(f"wt_lo{k}", 2) for k in range(3)]
        f_mm, f_inv, f_norm = pair_of("f_mm", 2), pair_of("f_inv", 2), pair_of("f_norm", 2)
        f_bias, f_min, f_exp = pair_of("f_bias", 2), pair_of("f_min", 2), pair_of("f_exp", 2)
        f_elu, f_diff, f_gated = pair_of("f_elu", 2), pair_of("f_diff", 2), pair_of("f_gated", 2)
        y2_ready, y2_stats, y2_mom = pair_of("y2_ready", 2), pair_of("y2_stats", 2), pair_of("y2_mom", 2)
        y2_var, y2_rstd, out_ready = pair_of("y2_var", 2), pair_of("y2_rstd", 2), pair_of("out_ready", 2)
        stored = [signal(f"stored{g}", 2, DONE_BY_DMA) for g in range(2)]

        norm0_shift, norm1_shift = pair_of("norm0_shift", 0), pair_of("norm1_shift", 2)

        readers = {"sdt": sd_copied}
        for j in range(C):
            readers[f"qk{j}"] = qk_lo[j]
        for g in range(2):
            readers.update({f"v{g}": v_raw[g], f"h{g}": h_raw[g], f"g{g}": g_tanh[g], f"pr{g}": y_ready[g],
                            f"sc{g}": sc_exp[g], f"z{g}": z_copied[g], f"ctx{g}": ctx_ready[g],
                            f"f{g}": f_norm[g], f"x1t{g}": x1t_l[g], f"ct{g}": ct_lo[g]})
            readers.update({f"pt{g}{half}": pt_lo[half][g] for half in range(2)})
            readers.update({f"wt{g}{k}": wt_lo[k][g] for k in range(3)})

        def lin_bank(user):
            return lin[bank_of(LIN_USERS, user)]

        def tp_bank(user):
            return tp[bank_of(TP_USERS, user)]

        staging = {"Wq": z[:, 0, 0:C * D], "Wk": z[:, 1, 0:C * D],
                   "Wv": p0[:, :, :].rearrange("p g n -> p (g n)")[:, 0:C * D],
                   "Wf": prod[:, :, :].rearrange("p g n -> p (g n)")[:, 0:C * D],
                   "W1": p1t_lo[:, :, :].rearrange("p g n -> p (g n)").bitcast(F32)[:, 0:C * D]}
        staging["Hw"] = staging["Wq"]

        xt_d = x_t
        x_d = x.rearrange("(t g) n d -> t n g d", g=2)
        adj_d = adj.rearrange("(t g) n m -> t n g m", g=2)
        out_d = out.rearrange("(t g) n d -> t n g d", g=2)

        block = ctx.enter_context(nc.Block())

        @block.sync
        def _(sp):
            for i, n in enumerate(("bf", "Hb")):
                sp.dma_start(bias_row[:, i, :], row_biases[n].unsqueeze(0)).then_inc(bias_row_loaded.sem, 16)
            for n in ("Wq", "Wk", "Wv"):
                sp.dma_start(staging[n], weights[n]).then_inc(w_loaded[n].sem, 16)

            def other_loads():
                for n in ("bq", "bk", "bv"):
                    sp.dma_start(column[n][:, :], biases[n]).then_inc(small_loaded.sem, 16)
                for n in ("Wf", "W1"):
                    sp.dma_start(staging[n], weights[n]).then_inc(w_loaded[n].sem, 16)
                for n in rows:
                    sp.dma_start(rows[n][:, :], row_biases[n].partition_broadcast(128)).then_inc(small_loaded.sem, 16)
                sp.wait_ge(w_lo_ready["Wq"].sem, 1)
                sp.dma_start(staging["Hw"], weights["Hw"]).then_inc(w_loaded["Hw"].sem, 16)
                sp.wait_ge(bias_split.sem, 6)
                sp.dma_start(bias_rows[:, :, :], bias_parts[0:1, :, :, :]).then_inc(bias_loaded.sem, 16)

            def body(turn):
                now, prev = turn.now, turn.prev

                def load_transposed_x():
                    sp.wait_ge(xt_split.sem, prev(xt_split))
                    turn.apart()
                    sp.dma_start(xt_raw[:, :, :], xt_d[turn.pair(-1)]).then_inc(xt_loaded.sem, 16)

                def load_x():
                    sp.wait_ge(y_ready[1].sem, now(y_ready[1]))
                    turn.apart()
                    sp.dma_start(x_raw[:, :, :], x_d[turn.pair(-1)]).then_inc(x_loaded.sem, 16)

                def load_adj0():
                    sp.wait_ge(mask0_ready.sem, now(mask0_ready))
                    turn.apart()
                    sp.dma_start(adj0[:, :, :], adj_d[turn.pair(-1)]).then_inc(adj0_loaded.sem, 16)

                def load_adj1():
                    sp.wait_ge(mask1_ready.sem, now(mask1_ready))
                    turn.apart()
                    sp.dma_start(adj1[:, :, :], adj_d[turn.pair(0)]).then_inc(adj1_loaded.sem, 16)

                def targets_flat():
                    sp.wait_ge(sd_copied.sem, now(sd_copied))
                    turn.apart()
                    for g in range(2):
                        sp.wait_ge(z_mm[g].sem, prev(z_mm[g]))
                        turn.apart()
                        for part in range(3):
                            dma = sp.dma_start(dst_row[3 * H1 + part:3 * H1 + part + 1, g, :, :],
                                               sd_t[64 + H1 * part:64 + H1 * (part + 1), g, :])
                            dma.then_inc(dst_flat[g].sem, 16)

                def store(g):
                    sp.wait_ge(out_ready[g].sem, now(out_ready[g]))
                    turn.apart()
                    sp.dma_start(out_d[turn.pair(2), :, g, :], out_tile[:, g, :]).then_inc(stored[g].sem, 16)

                turn.late(0, load_adj1)
                turn.late(-1, load_x)
                turn.step(-1, load_transposed_x)
                turn.step(1, targets_flat)
                turn.step(-1, load_adj0)
                turn.late(2, store, 0)
                turn.late(2, store, 1)

            turns(sp, passed, body, other_loads)
            for g in range(2):
                sp.wait_ge(stored[g].sem, 16 * PAIRS)

        @block.tensor
        def _(pe):
            def product(bank, left_hi, left_lo, right_hi, right_lo, opens=True):
                passes = [(left_hi, right_hi), (left_hi, right_lo), (left_lo, right_hi)]
                for k in range(C):
                    for i, (a, b) in enumerate(passes):
                        last = pe.matmul(bank, a(k), b(k), start=(opens and k == 0 and i == 0),
                                         stop=(k == C - 1 and i == 2))
                return last

            def rows_product(bank, hi, lo, name, opens):
                return product(bank[:, 0:D], hi, lo, lambda k: w_hi[name][:, k, :], lambda k: w_lo[name][:, k, :], opens)

            pe.wait_ge(consts_ready.sem, 3)
            pe.wait_ge(fills_ready.sem, 1)

            def body(turn):
                now, prev, t = turn.now, turn.prev, turn.t

                def bank_free(users, user, banks=2):
                    freed = last_reader(turn, users, user, readers, banks)
                    if freed:
                        pe.wait_ge(freed[0].sem, freed[1])

                def queries_keys(j):
                    if turn.starts(0):
                        for n in ("Wq", "Wk"):
                            pe.wait_ge(w_lo_ready[n].sem, 1)
                    pe.wait_ge(xt_split.sem, prev(xt_split))
                    bank_free(LIN_USERS, f"qk{j}")
                    bank = lin_bank(f"qk{j}")
                    for i, n in enumerate(("Wq", "Wk")):
                        last = product(bank[:, 2 * N * i:2 * N * (i + 1)],
                                       lambda k: w_hi[n][:, k, 128 * j:128 * (j + 1)],
                                       lambda k: w_lo[n][:, k, 128 * j:128 * (j + 1)],
                                       lambda k: xt_hi[:, k, :], lambda k: xt_lo[:, k, :])
                    last.then_inc(qk_mm[j].sem, 2)

                def x1_transposes(g):
                    pe.wait_ge(x1_ready[g].sem, prev(x1_ready[g]))
                    bank_free(TP_USERS, f"x1t{g}")
                    bank = tp_bank(f"x1t{g}")
                    for k in range(C):
                        last = pe.transpose(bank[:, 128 * k:128 * (k + 1)], x1[:, g, 128 * k:128 * (k + 1)], ident[:, :])
                    last.then_inc(x1t_mm[g].sem, 1)

                def bias_product(bank, i):
                    pe.matmul(bank[:, 0:D], ones_bf[:, :], bias_rows[:, i, :], start=True, stop=False)

                def hidden(g):
                    bank_free(LIN_USERS, f"h{g}")
                    pe.wait_ge(x1t_l[g].sem, now(x1t_l[g]))
                    if turn.starts(1):
                        pe.wait_ge(w_lo_ready["W1"].sem, 1)
                    rows_product(lin_bank(f"h{g}"), lambda k: x1t_hi[:, g, k, :], lambda k: x1t_lo[:, g, k, :],
                                 "W1", True).then_inc(h_mm[g].sem, 1)

                def values(g):
                    bank_free(LIN_USERS, f"v{g}")
                    pe.wait_ge(xt_split.sem, prev(xt_split))
                    if turn.starts(0):
                        pe.wait_ge(w_lo_ready["Wv"].sem, 1)
                    rows_product(lin_bank(f"v{g}"), lambda k: xt_hi[:, k, N * g:N * (g + 1)],
                                 lambda k: xt_lo[:, k, N * g:N * (g + 1)], "Wv", True).then_inc(v_mm[g].sem, 1)

                def gate_rows(g):
                    bank_free(LIN_USERS, f"g{g}")
                    pe.wait_ge(x1t_l[g].sem, now(x1t_l[g]))
                    if turn.starts(1):
                        pe.wait_ge(w_lo_ready["Hw"].sem, 1)
                    bias_product(lin_bank(f"g{g}"), 1)
                    rows_product(lin_bank(f"g{g}"), lambda k: x1t_hi[:, g, k, :], lambda k: x1t_lo[:, g, k, :],
                                 "Hw", False).then_inc(g_mm[g].sem, 1)

                def source_target_transposes():
                    pe.wait_ge(sd_3.sem, now(sd_3))
                    bank_free(TP_USERS, "sdt")
                    for g in range(2):
                        last = pe.transpose(tp_bank("sdt")[:, :].bitcast(BF16)[:, N * g:N * (g + 1)],
                                            sd_parts[:, g, :, :].rearrange("p a b -> p (a b)"), ident_bf[:, :])
                    last.then_inc(sdt_mm.sem, 2)

                def values_bias():
                    pe.wait_ge(w_lo_ready["Wf"].sem, 1)
                    pe.wait_ge(bv_ready.sem, 2)
                    rows_product(fp, lambda k: x1t_hi[:, 0, k, :], lambda k: x1t_lo[:, 0, k, :],
                                 "Wf", True).then_inc(bv_mm.sem, 1)

                def scores(g):
                    if turn.starts(0) and g == 0:
                        values_bias()
                    bank_free(ZP_USERS, f"sc{g}", 1)
                    pe.wait_ge(mask0_ready.sem, now(mask0_ready))
                    for j in range(C):
                        pe.wait_ge(qk_lo[j].sem, now(qk_lo[j]))
                    m = mask0[:, g:g + 1, :]
                    pe.matmul(zp[:, 0, :], ident_bf[:, :], m.to_broadcast([128, 4, N]), start=True, stop=True)
                    pe.matmul(zp[:, 1, 0:2 * N], ident_bf[:, :], m.to_broadcast([128, 2, N]), start=True, stop=True)
                    for j in range(C):
                        o = zp[:, j // 2, 2 * N * (j % 2):2 * N * (j % 2) + 2 * N]
                        qh, ql = q_hi[:, j, N * g:N * (g + 1)], q_lo[:, j, N * g:N * (g + 1)]
                        kh = k_hi[:, j, g, :, :].rearrange("p a n -> p (a n)")
                        kl = k_lo[:, j, g, :, :].rearrange("p a n -> p (a n)")
                        pe.matmul(o, qh, kh, start=False, stop=False, skip_group_check=True)
                        pe.matmul(o, qh, kl, start=False, stop=False, skip_group_check=True)
                        last = pe.matmul(o, ql, kh, start=False, stop=True, skip_group_check=True)
                    last.then_inc(sc_mm[g].sem, 1)

                def weights0_transposes(g, half):
                    pe.wait_ge(sc_exp[g].sem, now(sc_exp[g]))
                    bank_free(TP_USERS, f"pt{g}{half}")
                    bank = tp_bank(f"pt{g}{half}")
                    for i in range(3):
                        c = N * (3 * half + i)
                        last = pe.transpose(bank[:, N * i:N * (i + 1)], p0[:, g, c:c + N], ident[:, :])
                    last.then_inc(pt_mm[half][g].sem, 1)

                def attend0(g):
                    if turn.starts(0) and g == 0:
                        pe.wait_ge(bias_split.sem, 1)
                    bank_free(FP_USERS, f"ctx{g}", 1)
                    pe.wait_ge(v_done[2][g].sem, now(v_done[2][g]))
                    for h in range(H0):
                        if h % 3 == 0:
                            pe.wait_ge(pt_lo[h // 3][g].sem, now(pt_lo[h // 3][g]))
                        o = fp[:, (E0 + 1) * h:(E0 + 1) * (h + 1)]
                        hi, lo = p0t_hi[:, g, N * h:N * (h + 1)], p0t_lo[:, g, N * h:N * (h + 1)]
                        for i in range(3):
                            pe.matmul(o, hi, v_part[i][:, g, h, :], start=(h == 0 and i == 0), stop=False,
                                      skip_group_check=True)
                        for i in range(2):
                            last = pe.matmul(o, lo, v_part[i][:, g, h, :], start=False, stop=(i == 1),
                                             skip_group_check=True)
                    last.then_inc(ctx_mm[g].sem, 1)

                def context_transposes(g):
                    pe.wait_ge(ctx_ready[g].sem, now(ctx_ready[g]))
                    bank_free(TP_USERS, f"ct{g}")
                    bank = tp_bank(f"ct{g}")
                    for k in range(C):
                        last = pe.transpose(bank[:, 128 * k:128 * (k + 1)], ctx_n[:, g, 128 * k:128 * (k + 1)], ident[:, :])
                    last.then_inc(ct_mm[g].sem, 1)

                def project(g):
                    pe.wait_ge(ct_lo[g].sem, now(ct_lo[g]))
                    bank_free(LIN_USERS, f"pr{g}")
                    if turn.starts(0):
                        pe.wait_ge(bias_loaded.sem, 16)
                    bias_product(lin_bank(f"pr{g}"), 0)
                    rows_product(lin_bank(f"pr{g}"), lambda k: ctx_hi[:, g, k, :], lambda k: ctx_lo[:, g, k, :],
                                 "Wf", False).then_inc(pr_mm[g].sem, 1)

                def attention1(g):
                    bank_free(ZP_USERS, f"z{g}", 1)
                    if turn.starts(1):
                        pe.wait_ge(flat_ready.sem, 2)
                    pe.wait_ge(sd_copied.sem, now(sd_copied))
                    pe.wait_ge(mask1_ready.sem, now(mask1_ready))
                    m = mask1[:, g:g + 1, :].to_broadcast([128, 4, N])
                    for b in range(3):
                        pe.matmul(zp[:, b, :], ident_bf[:, :], m, start=True, stop=False)
                    pe.wait_ge(dst_flat[g].sem, now(dst_flat[g]))
                    flat_rows = dst_row[:, g, :, :].rearrange("p a n -> p (a n)")
                    for b in range(3):
                        last = pe.matmul(zp[:, b, :], sd_t[0:3 * H1 + 3, g, :], flat_rows[:, 512 * b:512 * (b + 1)],
                                         start=False, stop=True)
                    last.then_inc(z_mm[g].sem, 1)

                def weights1_transposes(g, k):
                    pe.wait_ge(z_exp[g].sem, prev(z_exp[g]))
                    bank_free(TP_USERS, f"wt{g}{k}")
                    bank = tp_bank(f"wt{g}{k}")
                    for i in range(4):
                        c = N * (4 * k + i)
                        last = pe.transpose(bank[:, N * i:N * (i + 1)], z[:, g, c:c + N], ident[:, :])
                    last.then_inc(wt_mm[k][g].sem, 1)

                def attend1(g, k):
                    if k == 0:
                        bank_free(FP_USERS, f"f{g}", 1)
                        pe.wait_ge(h_done[2][g].sem, prev(h_done[2][g]))
                    pe.wait_ge(wt_lo[k][g].sem, now(wt_lo[k][g]))
                    for h in range(4 * k, 4 * k + 4):
                        o = fp[:, (E1 + 1) * h:(E1 + 1) * (h + 1)]
                        hi, lo = p1t_hi[:, g, N * h:N * (h + 1)], p1t_lo[:, g, N * h:N * (h + 1)]
                        for i in range(3):
                            pe.matmul(o, hi, h_part[i][:, g, h, :], start=(h == 0 and i == 0), stop=False,
                                      skip_group_check=True)
                        for i in range(2):
                            last = pe.matmul(o, lo, h_part[i][:, g, h, :], start=False, stop=(i == 1),
                                             skip_group_check=True)
                    if k == 2:
                        last.then_inc(f_mm[g].sem, 1)

                turn.late(1, gate_rows, 1)
                turn.late(1, attention1, 1)
                turn.late(0, context_transposes, 1)
                turn.late(0, project, 0)
                turn.late(0, project, 1)
                turn.step(0, queries_keys, 0)
                turn.step(2, weights1_transposes, 0, 0)
                turn.step(2, weights1_transposes, 0, 1)
                turn.step(0, queries_keys, 1)
                turn.step(2, attend1, 0, 0)
                turn.step(2, weights1_transposes, 0, 2)
                turn.step(0, values, 0)
                turn.step(2, attend1, 0, 1)
                turn.step(1, x1_transposes, 0)
                turn.step(0, queries_keys, 2)
                turn.step(2, attend1, 0, 2)
                turn.step(1, hidden, 0)
                turn.step(2, weights1_transposes, 1, 0)
                turn.step(1, x1_transposes, 1)
                turn.step(0, scores, 0)
                turn.step(1, hidden, 1)
                turn.step(2, weights1_transposes, 1, 1)
                turn.step(2, weights1_transposes, 1, 2)
                turn.step(0, values, 1)
                turn.step(2, attend1, 1, 0)
                turn.step(2, attend1, 1, 1)
                turn.step(0, weights0_transposes, 0, 1)
                turn.step(2, attend1, 1, 2)
                turn.step(0, scores, 1)
                turn.step(1, source_target_transposes)
                turn.step(0, weights0_transposes, 0, 0)
                turn.step(1, gate_rows, 0)
                turn.step(0, attend0, 0)
                turn.step(0, weights0_transposes, 1, 1)
                turn.step(0, weights0_transposes, 1, 0)
                turn.step(1, attention1, 0)
                turn.step(0, context_transposes, 0)
                turn.step(0, attend0, 1)

            turns(pe, passed, body)

        @block.scalar
        def _(act):
            def weight_high(n):
                act.wait_ge(w_loaded[n].sem, 16)
                act.activation(w_hi[n][:, :, :].rearrange("p c d -> p (c d)"), staging[n], ACT.Copy)\
                    .then_inc(w_hi_ready[n].sem, 1)

            for n in ("Wq", "Wk", "Wv"):
                weight_high(n)
            act.wait_ge(fills_ready.sem, 1)

            def other_weights():
                act.wait_ge(small_loaded.sem, 16 * SMALL)
                act.activation(x1t_hi[:, 0, :, :], column["bv"][:, :].unsqueeze(2).to_broadcast([128, C, N]),
                               ACT.Copy).then_inc(bv_ready.sem, 1)
                for n in ("Wf", "W1", "Hw"):
                    weight_high(n)
                act.wait_ge(heads_ready.sem, 4)
                for g in range(2):
                    act.activation(dst_row[0:36, g, :, :], row_head[:, :].unsqueeze(2).to_broadcast([36, H1, N]),
                                   ACT.Copy).then_inc(flat_ready.sem, 1)


            def body(turn):
                now, prev = turn.now, turn.prev

                def queries_keys(j):
                    act.wait_ge(qk_mm[j].sem, now(qk_mm[j]))
                    act.wait_ge(sc_mm[1].sem, prev(sc_mm[1]))
                    bank = lin_bank(f"qk{j}")
                    act.activation(q_hi[:, j, :], bank[:, 0:2 * N], ACT.Identity, bias=column["bq"][:, j:j + 1])
                    for half in range(2):
                        p = slice(64 * half, 64 * half + 64)
                        last = act.activation(k_hi[p, j, :, half, :],
                                              bank[p, 2 * N:4 * N].rearrange("p (g n) -> p g n", g=2),
                                              ACT.Identity, bias=column["bk"][p, j:j + 1])
                    last.then_inc(qk_hi[j].sem, 2)

                def x1_high(g):
                    act.wait_ge(x1t_mm[g].sem, now(x1t_mm[g]))
                    act.wait_ge(g_mm[g].sem, prev(g_mm[g]))
                    act.wait_ge(h_mm[g].sem, prev(h_mm[g]))
                    act.activation(x1t_hi[:, g, :, :].rearrange("p c n -> p (c n)"), tp_bank(f"x1t{g}")[:, 0:D],
                                   ACT.Copy).then_inc(x1t_h[g].sem, 1)

                def keep_x1(g):
                    act.wait_ge(x1_ready[g].sem, prev(x1_ready[g]))
                    act.wait_ge(y2_ready[g].sem, now(y2_ready[g]))
                    act.activation(x1_kept[:, g, :], x1[:, g, :], ACT.Copy).then_inc(x1_copied[g].sem, 1)

                def hidden_tanh(g):
                    act.wait_ge(h_mm[g].sem, now(h_mm[g]))
                    act.wait_ge(sd_prod[g].sem, prev(sd_prod[g]))
                    act.activation(th[:, g, :], lin_bank(f"h{g}")[:, 0:D], ACT.Tanh).then_inc(h_tanh[g].sem, 1)

                def hidden_part1(g):
                    act.wait_ge(f_mm[g].sem, now(f_mm[g]))
                    act.activation(h_part[0][:, g, :, 0:E1],
                                   lin_bank(f"h{g}")[:, 0:D].rearrange("p (a e) -> p a e", a=H1),
                                   ACT.Copy).then_inc(h_done[0][g].sem, 1)

                def hidden_copy(g):
                    act.wait_ge(h_mm[g].sem, now(h_mm[g]))
                    act.wait_ge(h_done[2][g].sem, prev(h_done[2][g]))
                    act.activation(h_res[:, g, :], lin_bank(f"h{g}")[:, 0:D], ACT.Copy).then_inc(h_raw[g].sem, 1)

                def hidden_part2(g):
                    act.wait_ge(h_r[g].sem, now(h_r[g]))
                    act.activation(h_part[1][:, g, :, 0:E1], h_res[:, g, :].rearrange("p (a e) -> p a e", a=H1),
                                   ACT.Copy).then_inc(h_done[1][g].sem, 1)

                def value_part1(g):
                    act.wait_ge(v_mm[g].sem, now(v_mm[g]))
                    act.wait_ge(ctx_mm[g].sem, prev(ctx_mm[g]))
                    act.activation(v_part[0][:, g, :, 0:E0],
                                   lin_bank(f"v{g}")[:, 0:D].rearrange("p (a e) -> p a e", a=H0),
                                   ACT.Copy).then_inc(v_done[0][g].sem, 1)

                def value_copy(g):
                    act.wait_ge(v_mm[g].sem, now(v_mm[g]))
                    act.wait_ge(v_done[2][g].sem, prev(v_done[2][g]))
                    act.activation(v_res[:, g, :], lin_bank(f"v{g}")[:, 0:D], ACT.Copy).then_inc(v_raw[g].sem, 1)

                def value_part2(g):
                    act.wait_ge(v_r[g].sem, now(v_r[g]))
                    act.activation(v_part[1][:, g, :, 0:E0], v_res[:, g, :].rearrange("p (a e) -> p a e", a=H0),
                                   ACT.Copy).then_inc(v_done[1][g].sem, 1)

                def source_target_copy():
                    act.wait_ge(sdt_mm.sem, now(sdt_mm))
                    act.wait_ge(z_mm[1].sem, prev(z_mm[1]))
                    for step in dst_flat:
                        act.wait_ge(step.sem, prev(step))
                    act.activation(sd_t[:, :, :].rearrange("p g n -> p (g n)"),
                                   tp_bank("sdt")[:, :].bitcast(BF16)[0:64 + 3 * H1, 0:2 * N], ACT.Copy)\
                        .then_inc(sd_copied.sem, 2)

                def gate_tanh(g):
                    act.wait_ge(g_mm[g].sem, now(g_mm[g]))
                    act.wait_ge(f_gated[g].sem, now(f_gated[g]))
                    act.activation(gate[:, g, :], lin_bank(f"g{g}")[:, 0:D], ACT.Tanh, scale=0.5)\
                        .then_inc(g_tanh[g].sem, 1)

                def gate_plus_one(g):
                    act.wait_ge(g_tanh[g].sem, now(g_tanh[g]))
                    act.activation(gate[:, g, :], gate[:, g, :], ACT.Copy, bias=1.0).then_inc(g_plus[g].sem, 1)

                def scores_exp(g):
                    act.wait_ge(sc_shift[g].sem, now(sc_shift[g]))
                    act.wait_ge(pt_mm[1][g].sem, prev(pt_mm[1][g]))
                    act.wait_ge(pt_mm[0][g].sem, prev(pt_mm[0][g]))
                    for h in range(H0):
                        last = act.activation(p0[:, g, N * h:N * (h + 1)], zp[:, h // 4, N * (h % 4):N * (h % 4 + 1)],
                                              ACT.Exp, bias=p0_shift[:, g, h:h + 1], scale=SCALE0)
                    last.then_inc(sc_exp[g].sem, 1)

                def z_copy(g):
                    act.wait_ge(z_mm[g].sem, now(z_mm[g]))
                    for k in range(3):
                        act.wait_ge(wt_mm[k][g].sem, now(wt_mm[k][g]))
                    act.activation(z[:, g, :], zp[:, :, :].rearrange("p b n -> p (b n)"), ACT.Copy)\
                        .then_inc(z_copied[g].sem, 1)

                def weights0_high(g, half):
                    act.wait_ge(pt_mm[half][g].sem, now(pt_mm[half][g]))
                    act.wait_ge(ctx_mm[g].sem, prev(ctx_mm[g]))
                    act.activation(p0t_hi[:, g, 3 * N * half:3 * N * (half + 1)], tp_bank(f"pt{g}{half}")[:, 0:3 * N],
                                   ACT.Copy, scale=PSCALE).then_inc(pt_hi[half][g].sem, 1)

                def context_high(g):
                    act.wait_ge(ct_mm[g].sem, now(ct_mm[g]))
                    act.wait_ge(pr_mm[g].sem, prev(pr_mm[g]))
                    act.activation(ctx_hi[:, g, :, :].rearrange("p c n -> p (c n)"), tp_bank(f"ct{g}")[:, 0:D],
                                   ACT.Copy).then_inc(ct_hi[g].sem, 1)

                def norm0(g):
                    act.wait_ge(norm0_shift[g].sem, now(norm0_shift[g]))
                    act.wait_ge(x1t_mm[g].sem, now(x1t_mm[g]))
                    act.wait_ge(x1_copied[g].sem, now(x1_copied[g]))
                    act.activation(x1[:, g, :], y[:, g, :], ACT.Identity, bias=shift0[:, g, :], scale=rstd[:, g, :])\
                        .then_inc(x1_ready[g].sem, 1)

                def z_exponent(g):
                    act.wait_ge(z_sub[g].sem, now(z_sub[g]))
                    act.activation(z[:, g, :], z[:, g, :], ACT.Exp).then_inc(z_exp[g].sem, 1)

                def weights1_high(g, k):
                    act.wait_ge(wt_mm[k][g].sem, now(wt_mm[k][g]))
                    act.wait_ge(f_mm[g].sem, prev(f_mm[g]))
                    act.activation(p1t_hi[:, g, 4 * N * k:4 * N * (k + 1)], tp_bank(f"wt{g}{k}")[:, :], ACT.Copy,
                                   scale=PSCALE).then_inc(wt_hi[k][g].sem, 1)

                def elu_exp(g):
                    act.wait_ge(f_min[g].sem, now(f_min[g]))
                    act.activation(f_neg[:, g, :], f_neg[:, g, :], ACT.Exp).then_inc(f_exp[g].sem, 1)

                def norm1(g):
                    act.wait_ge(norm1_shift[g].sem, now(norm1_shift[g]))
                    act.wait_ge(stored[g].sem, prev(stored[g]))
                    act.activation(out_tile[:, g, :], y2[:, g, :], ACT.Identity, bias=shift1[:, g, :],
                                   scale=rstd2[:, g, :]).then_inc(out_ready[g].sem, 1)

                def next_x_high():
                    act.wait_ge(xt_loaded.sem, now(xt_loaded))
                    for j in range(C):
                        act.wait_ge(qk_mm[j].sem, now(qk_mm[j]))
                    act.wait_ge(v_mm[0].sem, now(v_mm[0]))
                    act.wait_ge(v_mm[1].sem, now(v_mm[1]))
                    act.activation(xt_hi[:, :, :].rearrange("p c n -> p (c n)"),
                                   xt_raw[:, :, :].rearrange("p c n -> p (c n)"), ACT.Copy).then_inc(xt_hi_made.sem, 2)

                turn.late(0, context_high, 1)
                turn.late(1, gate_tanh, 1)
                turn.late(1, z_copy, 1)
                turn.late(1, gate_plus_one, 1)
                turn.late(1, z_exponent, 0)
                turn.late(1, keep_x1, 1)
                turn.step(2, weights1_high, 0, 0)
                turn.step(0, queries_keys, 0)
                turn.step(2, weights1_high, 0, 1)
                turn.step(0, queries_keys, 1)
                turn.late(0, norm0, 0)
                turn.step(2, weights1_high, 0, 2)
                turn.step(0, value_part1, 0)
                turn.late(1, z_exponent, 1)
                turn.step(1, x1_high, 0)
                turn.step(0, value_copy, 0)
                turn.step(0, queries_keys, 2)
                turn.late(0, norm0, 1)
                turn.step(0, value_part2, 0)
                turn.step(1, hidden_tanh, 0)
                turn.step(1, x1_high, 1)
                turn.step(2, weights1_high, 1, 0)
                turn.step(1, hidden_part1, 0)
                turn.step(1, hidden_copy, 0)
                turn.step(2, elu_exp, 0)
                turn.step(1, hidden_tanh, 1)
                turn.step(2, weights1_high, 1, 1)
                turn.step(2, weights1_high, 1, 2)
                turn.step(0, scores_exp, 0)
                turn.step(0, value_part1, 1)
                turn.step(0, value_copy, 1)
                turn.step(0, weights0_high, 0, 1)
                turn.step(1, hidden_part1, 1)
                turn.step(1, hidden_copy, 1)
                turn.late(2, norm1, 0)
                turn.step(1, source_target_copy)
                turn.step(0, weights0_high, 0, 0)
                turn.step(0, value_part2, 1)
                turn.step(0, scores_exp, 1)
                turn.step(2, elu_exp, 1)
                turn.step(0, weights0_high, 1, 1)
                turn.step(0, weights0_high, 1, 0)
                turn.late(2, norm1, 1)
                turn.step(1, gate_tanh, 0)
                turn.step(1, z_copy, 0)
                turn.step(-1, next_x_high)
                turn.step(1, hidden_part2, 0)
                turn.step(1, hidden_part2, 1)
                turn.step(0, context_high, 0)
                turn.step(1, gate_plus_one, 0)
                turn.step(1, keep_x1, 0)

            turns(act, passed, body, other_weights)

        @block.vector
        def _(dve):
            dve.memset(k_hi[:, :, :, :, :].rearrange("p a b c n -> p (a b c n)").bitcast(F32), 0.0)
            dve.memset(k_lo[:, :, :, :, :].rearrange("p a b c n -> p (a b c n)").bitcast(F32), 0.0)
            for i in range(3):
                dve.memset(v_part[i][:, :, :, E0:], 1.0 if i == 0 else 0.0)
                dve.memset(h_part[i][:, :, :, E1:], 1.0 if i == 0 else 0.0)
            dve.memset(sd_parts[:, :, 0, 3 * H1:3 * H1 + 3], 1.0)
            dve.memset(sd_parts[:, :, 0, 3 * H1 + 3:], 0.0)
            dve.memset(sd_parts[:, :, 1, 3 * H1:], 0.0)
            dve.memset(ones_bf[:, :], 1.0)
            dve.memset(half_neg[:, :], -0.5).then_inc(fills_ready.sem, 1)
            def weight_low(n):
                dve.wait_ge(w_hi_ready[n].sem, 1)
                dve.tensor_tensor(w_lo[n][:, :, :].rearrange("p c d -> p (c d)"), staging[n],
                                  w_hi[n][:, :, :].rearrange("p c d -> p (c d)").bitcast(F32), ALU.subtract)\
                    .then_inc(w_lo_ready[n].sem, 1)

            for n in ("Wq", "Wk", "Wv"):
                weight_low(n)
            dve.wait_ge(fills_ready.sem, 1)

            def other_weights():
                dve.wait_ge(small_loaded.sem, 16 * SMALL)
                dve.wait_ge(bias_row_loaded.sem, 32)
                dve.wait_ge(bv_ready.sem, 1)
                dve.tensor_tensor(x1t_lo[:, 0, :, :], column["bv"][:, :].unsqueeze(2).to_broadcast([128, C, N]),
                                  x1t_hi[:, 0, :, :].bitcast(F32), ALU.subtract).then_inc(bv_ready.sem, 1)
                for n in ("Wf", "W1", "Hw"):
                    weight_low(n)


            def body(turn):
                now, prev = turn.now, turn.prev

                def queries_keys(j):
                    dve.wait_ge(qk_hi[j].sem, now(qk_hi[j]))
                    dve.wait_ge(sc_mm[1].sem, prev(sc_mm[1]))
                    bank = lin_bank(f"qk{j}")
                    dve.scalar_tensor_tensor(out=q_lo[:, j, :], in0=bank[:, 0:2 * N],
                                             scalar=column["bq"][:, j:j + 1], in1=q_hi[:, j, :].bitcast(F32),
                                             op0=ALU.add, op1=ALU.subtract)
                    for half in range(2):
                        p = slice(64 * half, 64 * half + 64)
                        last = dve.scalar_tensor_tensor(
                            out=k_lo[p, j, :, half, :],
                            in0=bank[p, 2 * N:4 * N].rearrange("p (g n) -> p g n", g=2),
                            scalar=column["bk"][p, j:j + 1], in1=k_hi[p, j, :, half, :].bitcast(F32),
                            op0=ALU.add, op1=ALU.subtract)
                    last.then_inc(qk_lo[j].sem, 2)

                def x1_low(g):
                    dve.wait_ge(x1t_h[g].sem, now(x1t_h[g]))
                    dve.wait_ge(g_mm[g].sem, prev(g_mm[g]))
                    dve.wait_ge(h_mm[g].sem, prev(h_mm[g]))
                    dve.tensor_tensor(x1t_lo[:, g, :, :].rearrange("p c n -> p (c n)"), tp_bank(f"x1t{g}")[:, 0:D],
                                      x1t_hi[:, g, :, :].rearrange("p c n -> p (c n)").bitcast(F32), ALU.subtract)\
                        .then_inc(x1t_l[g].sem, 1)

                def source_target_sums(g):
                    dve.wait_ge(sd_prod[g].sem, now(sd_prod[g]))
                    dve.tensor_reduce(sd[:, g, :, :], prod[:, g, :].rearrange("p (s a e) -> p s a e", s=2, a=H1),
                                      AX.X, ALU.add).then_inc(sd_sum[g].sem, 1)

                def source_target_part1():
                    dve.wait_ge(sd_sum[0].sem, now(sd_sum[0]))
                    dve.wait_ge(sd_sum[1].sem, now(sd_sum[1]))
                    dve.wait_ge(sdt_mm.sem, prev(sdt_mm))
                    for g in range(2):
                        last = dve.tensor_copy(sd_parts[:, g, :, 0:H1], sd[:, g, :, :])
                    last.then_inc(sd_1.sem, 2)

                def source_target_residue():
                    dve.wait_ge(sd_1.sem, now(sd_1))
                    for g in range(2):
                        last = dve.tensor_tensor(sd_res[:, g, :, :], sd[:, g, :, :], sd_parts[:, g, :, 0:H1], ALU.subtract)
                    last.then_inc(sd_r.sem, 2)

                def source_target_part2():
                    dve.wait_ge(sd_r.sem, now(sd_r))
                    for g in range(2):
                        last = dve.tensor_copy(sd_parts[:, g, :, H1:2 * H1], sd_res[:, g, :, :])
                    last.then_inc(sd_2.sem, 2)

                def source_target_part3():
                    dve.wait_ge(sd_2.sem, now(sd_2))
                    for g in range(2):
                        last = dve.tensor_tensor(sd_parts[:, g, :, 2 * H1:3 * H1], sd_res[:, g, :, :],
                                                 sd_parts[:, g, :, H1:2 * H1], ALU.subtract)
                    last.then_inc(sd_3.sem, 2)

                def bias_row_parts():
                    dve.wait_ge(bv_mm.sem, 1)
                    dve.tensor_tensor(bias_row[:, 0, :], bias_row[:, 0, :], fp[0:1, 0:D], ALU.add).then_inc(bias_split.sem, 1)
                    dve.wait_ge(bias_split.sem, 1)
                    dve.tensor_copy(bias_parts[:, 0, :, :], bias_row[:, :, :]).then_inc(bias_split.sem, 1)
                    dve.wait_ge(bias_split.sem, 2)
                    dve.tensor_tensor(bias_res[:, :, :], bias_row[:, :, :], bias_parts[:, 0, :, :], ALU.subtract)\
                        .then_inc(bias_split.sem, 1)
                    dve.wait_ge(bias_split.sem, 3)
                    dve.tensor_copy(bias_parts[:, 1, :, :], bias_res[:, :, :]).then_inc(bias_split.sem, 1)
                    dve.wait_ge(bias_split.sem, 4)
                    dve.tensor_tensor(bias_res[:, :, :], bias_res[:, :, :], bias_parts[:, 1, :, :], ALU.subtract)\
                        .then_inc(bias_split.sem, 1)
                    dve.wait_ge(bias_split.sem, 5)
                    dve.tensor_copy(bias_parts[:, 2, :, :], bias_res[:, :, :]).then_inc(bias_split.sem, 1)

                def scores_max(g):
                    if turn.starts(0) and g == 0:
                        bias_row_parts()
                    dve.wait_ge(sc_mm[g].sem, now(sc_mm[g]))
                    s = zp[:, 0:2, :].rearrange("p b n -> p (b n)")[:, 0:H0 * N].rearrange("p (a n) -> p a n", a=H0)
                    dve.tensor_reduce(p0_max[:, g, :], s, AX.X, ALU.max).then_inc(sc_max[g].sem, 1)

                def scores_shift(g):
                    dve.wait_ge(sc_max[g].sem, now(sc_max[g]))
                    dve.wait_ge(sc_exp[g].sem, prev(sc_exp[g]))
                    dve.tensor_scalar(p0_shift[:, g, :], p0_max[:, g, :], -SCALE0, None, ALU.mult)\
                        .then_inc(sc_shift[g].sem, 1)

                def weights0_low(g, half):
                    bank = tp_bank(f"pt{g}{half}")
                    c = slice(3 * N * half, 3 * N * (half + 1))
                    dve.wait_ge(pt_hi[half][g].sem, now(pt_hi[half][g]))
                    dve.wait_ge(ctx_mm[g].sem, prev(ctx_mm[g]))
                    dve.scalar_tensor_tensor(out=p0t_lo[:, g, c], in0=bank[:, 0:3 * N], scalar=PSCALE,
                                             in1=p0t_hi[:, g, c], op0=ALU.mult, op1=ALU.subtract)\
                        .then_inc(pt_lo[half][g].sem, 1)

                def context_inverse(g):
                    dve.wait_ge(ctx_mm[g].sem, now(ctx_mm[g]))
                    s = fp[:, 0:H0 * (E0 + 1)].rearrange("p (a e) -> p a e", a=H0)
                    dve.reciprocal(ctx_rcp[:, g, :].unsqueeze(2), s[:, :, E0:]).then_inc(ctx_inv[g].sem, 1)

                def context_norm(g):
                    dve.wait_ge(ctx_inv[g].sem, now(ctx_inv[g]))
                    s = fp[:, 0:H0 * (E0 + 1)].rearrange("p (a e) -> p a e", a=H0)
                    dve.tensor_tensor(ctx_n[:, g, :].rearrange("p (a e) -> p a e", a=H0), s[:, :, 0:E0],
                                      ctx_rcp[:, g, :].unsqueeze(2).to_broadcast([128, H0, E0]), ALU.mult)\
                        .then_inc(ctx_ready[g].sem, 1)

                def context_low(g):
                    dve.wait_ge(ct_hi[g].sem, now(ct_hi[g]))
                    dve.wait_ge(pr_mm[g].sem, prev(pr_mm[g]))
                    dve.tensor_tensor(ctx_lo[:, g, :, :].rearrange("p c n -> p (c n)"), tp_bank(f"ct{g}")[:, 0:D],
                                      ctx_hi[:, g, :, :].rearrange("p c n -> p (c n)").bitcast(F32), ALU.subtract)\
                        .then_inc(ct_lo[g].sem, 1)

                def add_residual(g):
                    dve.wait_ge(pr_mm[g].sem, now(pr_mm[g]))
                    dve.wait_ge(x_loaded.sem, prev(x_loaded))
                    dve.wait_ge(x1_ready[g].sem, prev(x1_ready[g]))
                    dve.tensor_tensor(y[:, g, :], lin_bank(f"pr{g}")[:, 0:D], x_raw[:, g, :], ALU.add).then_inc(y_ready[g].sem, 1)

                def stats0(g):
                    dve.wait_ge(y_ready[g].sem, now(y_ready[g]))
                    dve.bn_stats(stats[:, g, :], y[:, g, :]).then_inc(y_stats[g].sem, 1)

                def moments0(g):
                    dve.wait_ge(y_stats[g].sem, now(y_stats[g]))
                    turn.apart()
                    dve.bn_aggr(moments[:, g, :], stats[:, g, :]).then_inc(y_mom[g].sem, 1)

                def variance0(g):
                    dve.wait_ge(y_mom[g].sem, now(y_mom[g]))
                    dve.tensor_scalar(rstd[:, g, :], moments[:, g, 1:2], EPS, None, ALU.add).then_inc(y_var[g].sem, 1)

                def shift_norm0(g):
                    dve.wait_ge(y_rstd[g].sem, now(y_rstd[g]))
                    dve.wait_ge(x1_ready[g].sem, prev(x1_ready[g]))
                    dve.scalar_tensor_tensor(out=shift0[:, g, :], in0=moments[:, g, 0:1], scalar=-1.0,
                                             in1=rstd[:, g, :], op0=ALU.mult, op1=ALU.mult)\
                        .then_inc(norm0_shift[g].sem, 1)

                def z_leak(g):
                    dve.wait_ge(z_copied[g].sem, now(z_copied[g]))
                    dve.scalar_tensor_tensor(out=z[:, g, :], in0=z[:, g, :], scalar=0.2, in1=z[:, g, :],
                                             op0=ALU.mult, op1=ALU.max).then_inc(z_leaky[g].sem, 1)

                def z_maxima(g):
                    dve.wait_ge(z_leaky[g].sem, now(z_leaky[g]))
                    dve.wait_ge(z_sub[g].sem, prev(z_sub[g]))
                    dve.tensor_reduce(z_max[:, g, :], z[:, g, :].rearrange("p (a n) -> p a n", a=H1),
                                      AX.X, ALU.max).then_inc(z_maxed[g].sem, 1)

                def weights1_low(g, k):
                    bank = tp_bank(f"wt{g}{k}")
                    c = slice(4 * N * k, 4 * N * (k + 1))
                    dve.wait_ge(wt_hi[k][g].sem, now(wt_hi[k][g]))
                    dve.wait_ge(f_mm[g].sem, prev(f_mm[g]))
                    dve.scalar_tensor_tensor(out=p1t_lo[:, g, c], in0=bank[:, :], scalar=PSCALE,
                                             in1=p1t_hi[:, g, c], op0=ALU.mult, op1=ALU.subtract)\
                        .then_inc(wt_lo[k][g].sem, 1)

                def features_inverse(g):
                    dve.wait_ge(f_mm[g].sem, now(f_mm[g]))
                    s = fp[:, 0:H1 * (E1 + 1)].rearrange("p (a e) -> p a e", a=H1)
                    dve.reciprocal(f_rcp[:, g, :].unsqueeze(2), s[:, :, E1:]).then_inc(f_inv[g].sem, 1)

                def features_norm(g):
                    dve.wait_ge(f_inv[g].sem, now(f_inv[g]))
                    s = fp[:, 0:H1 * (E1 + 1)].rearrange("p (a e) -> p a e", a=H1)
                    dve.wait_ge(f_diff[g].sem, prev(f_diff[g]))
                    dve.tensor_tensor(f[:, g, :].rearrange("p (a e) -> p a e", a=H1), s[:, :, 0:E1],
                                      f_rcp[:, g, :].unsqueeze(2).to_broadcast([128, H1, E1]), ALU.mult)\
                        .then_inc(f_norm[g].sem, 1)

                def elu(g):
                    dve.wait_ge(f_exp[g].sem, now(f_exp[g]))
                    dve.scalar_tensor_tensor(out=f[:, g, :], in0=f_neg[:, g, :], scalar=-1.0, in1=f[:, g, :],
                                             op0=ALU.add, op1=ALU.max).then_inc(f_elu[g].sem, 1)

                def mix(g):
                    dve.wait_ge(f_gated[g].sem, now(f_gated[g]))
                    dve.wait_ge(x1_copied[g].sem, prev(x1_copied[g]))
                    dve.wait_ge(out_ready[g].sem, prev(out_ready[g]))
                    dve.scalar_tensor_tensor(out=y2[:, g, :], in0=f[:, g, :], scalar=0.25, in1=x1_kept[:, g, :],
                                             op0=ALU.mult, op1=ALU.add).then_inc(y2_ready[g].sem, 1)

                def stats1(g):
                    dve.wait_ge(y2_ready[g].sem, now(y2_ready[g]))
                    dve.bn_stats(stats2[:, g, :], y2[:, g, :]).then_inc(y2_stats[g].sem, 1)

                def moments1(g):
                    dve.wait_ge(y2_stats[g].sem, now(y2_stats[g]))
                    turn.apart()
                    dve.bn_aggr(moments2[:, g, :], stats2[:, g, :]).then_inc(y2_mom[g].sem, 1)

                def variance1(g):
                    dve.wait_ge(y2_mom[g].sem, now(y2_mom[g]))
                    dve.tensor_scalar(rstd2[:, g, :], moments2[:, g, 1:2], EPS / 4, None, ALU.add)\
                        .then_inc(y2_var[g].sem, 1)

                def shift_norm1(g):
                    dve.wait_ge(y2_rstd[g].sem, now(y2_rstd[g]))
                    dve.wait_ge(out_ready[g].sem, prev(out_ready[g]))
                    dve.scalar_tensor_tensor(out=shift1[:, g, :], in0=moments2[:, g, 0:1], scalar=-1.0,
                                             in1=rstd2[:, g, :], op0=ALU.mult, op1=ALU.mult)\
                        .then_inc(norm1_shift[g].sem, 1)

                turn.late(0, context_inverse, 1)
                turn.late(2, variance1, 0)
                turn.late(0, context_norm, 1)
                turn.late(1, z_leak, 0)
                turn.late(0, context_low, 0)
                turn.late(1, z_maxima, 0)
                turn.late(0, context_low, 1)
                turn.late(2, mix, 1)
                turn.late(0, add_residual, 0)
                turn.late(1, z_leak, 1)
                turn.late(0, add_residual, 1)
                turn.late(0, stats0, 0)
                turn.late(1, z_maxima, 1)
                turn.late(0, moments0, 0)
                turn.late(0, variance0, 0)
                turn.step(2, weights1_low, 0, 0)
                turn.step(0, queries_keys, 0)
                turn.step(2, weights1_low, 0, 1)
                turn.late(0, shift_norm0, 0)
                turn.step(0, queries_keys, 1)
                turn.late(2, stats1, 1)
                turn.late(2, moments1, 1)
                turn.late(0, stats0, 1)
                turn.late(0, moments0, 1)
                turn.late(0, variance0, 1)
                turn.step(2, weights1_low, 0, 2)
                turn.step(1, x1_low, 0)
                turn.late(2, variance1, 1)
                turn.step(2, features_inverse, 0)
                turn.late(0, shift_norm0, 1)
                turn.step(2, features_norm, 0)
                turn.step(0, queries_keys, 2)
                turn.step(1, x1_low, 1)
                turn.step(2, weights1_low, 1, 0)
                turn.step(0, scores_max, 0)
                turn.step(2, elu, 0)
                turn.step(0, scores_shift, 0)
                turn.step(1, source_target_sums, 0)
                turn.step(2, weights1_low, 1, 1)
                turn.step(2, weights1_low, 1, 2)
                turn.step(1, source_target_sums, 1)
                turn.step(1, source_target_part1)
                turn.late(2, shift_norm1, 0)
                turn.step(1, source_target_residue)
                turn.step(1, source_target_part2)
                turn.step(2, features_inverse, 1)
                turn.step(0, weights0_low, 0, 1)
                turn.step(1, source_target_part3)
                turn.step(2, features_norm, 1)
                turn.step(0, scores_max, 1)
                turn.step(0, scores_shift, 1)
                turn.step(0, weights0_low, 0, 0)
                turn.step(2, mix, 0)
                turn.step(2, stats1, 0)
                turn.step(2, moments1, 0)
                turn.step(0, context_inverse, 0)
                turn.step(0, context_norm, 0)
                turn.late(2, shift_norm1, 1)
                turn.step(2, elu, 1)
                turn.step(0, weights0_low, 1, 1)
                turn.step(0, weights0_low, 1, 0)

            turns(dve, passed, body, other_weights)

        @block.gpsimd
        def _(pool):
            pool.memset(ident[:, :], 1.0).then_inc(ones_ready.sem, 1)
            pool.memset(ident_bf[:, :], 1.0).then_inc(ones_ready.sem, 1)
            pool.wait_ge(ones_ready.sem, 2)
            for tile in (ident, ident_bf):
                pool.affine_select(out=tile[:, :], in_=tile[:, :], compare_op=ALU.is_equal, fill=0.0, base=0,
                                   pattern=[[-1, 128]], channel_multiplier=1).then_inc(consts_ready.sem, 1)
            pool.memset(row_head[:, :], 0.0).then_inc(heads_ready.sem, 1)
            for part in range(3):
                pool.wait_ge(heads_ready.sem, 1 + part)
                pool.affine_select(out=row_head[:, :], in_=row_head[:, :], compare_op=ALU.not_equal, fill=1.0,
                                   base=-H1 * part, pattern=[[-1, H1]], channel_multiplier=1)\
                    .then_inc(heads_ready.sem, 1)
            pool.memset(rstd[:, :, :], 1.0).then_inc(consts_ready.sem, 1)
            pool.wait_ge(fills_ready.sem, 1)

            def biases_loaded():
                pool.wait_ge(small_loaded.sem, 16 * SMALL)

            def body(turn):
                now, prev = turn.now, turn.prev

                def mask0_bias():
                    pool.wait_ge(adj0_loaded.sem, prev(adj0_loaded))
                    pool.wait_ge(sc_mm[1].sem, prev(sc_mm[1]))
                    turn.apart()
                    pool.tensor_scalar(mask0[:, :, :], adj0[:, :, :], -1.0, MASKED, ALU.add, ALU.mult)\
                        .then_inc(mask0_ready.sem, 2)

                def mask1_bias():
                    pool.wait_ge(adj1_loaded.sem, prev(adj1_loaded))
                    pool.wait_ge(z_mm[1].sem, prev(z_mm[1]))
                    turn.apart()
                    pool.tensor_scalar(mask1[:, :, :], adj1[:, :, :], -1.0, MASKED, ALU.add, ALU.mult)\
                        .then_inc(mask1_ready.sem, 2)

                def source_target_products(g):
                    pool.wait_ge(h_tanh[g].sem, now(h_tanh[g]))
                    pool.wait_ge(sd_sum[g].sem, prev(sd_sum[g]))
                    pool.tensor_tensor(prod[:, g, :].rearrange("p (s d) -> p s d", s=2),
                                       th[:, g:g + 1, :].to_broadcast([128, 2, D]),
                                       rows["w_sd"][:, :].rearrange("p (s d) -> p s d", s=2), ALU.mult)\
                        .then_inc(sd_prod[g].sem, 1)

                def hidden_residue(g):
                    pool.wait_ge(h_done[0][g].sem, now(h_done[0][g]))
                    pool.wait_ge(h_raw[g].sem, now(h_raw[g]))
                    hs = h_res[:, g, :].rearrange("p (a e) -> p a e", a=H1)
                    pool.tensor_tensor(hs, hs, h_part[0][:, g, :, 0:E1], ALU.subtract).then_inc(h_r[g].sem, 1)

                def hidden_part3(g):
                    pool.wait_ge(h_done[1][g].sem, now(h_done[1][g]))
                    pool.wait_ge(f_mm[g].sem, now(f_mm[g]))
                    pool.tensor_tensor(h_part[2][:, g, :, 0:E1], h_res[:, g, :].rearrange("p (a e) -> p a e", a=H1),
                                       h_part[1][:, g, :, 0:E1], ALU.subtract).then_inc(h_done[2][g].sem, 1)

                def value_residue(g):
                    pool.wait_ge(v_done[0][g].sem, now(v_done[0][g]))
                    pool.wait_ge(v_raw[g].sem, now(v_raw[g]))
                    vs = v_res[:, g, :].rearrange("p (a e) -> p a e", a=H0)
                    pool.tensor_tensor(vs, vs, v_part[0][:, g, :, 0:E0], ALU.subtract).then_inc(v_r[g].sem, 1)

                def value_part3(g):
                    pool.wait_ge(v_done[1][g].sem, now(v_done[1][g]))
                    pool.tensor_tensor(v_part[2][:, g, :, 0:E0], v_res[:, g, :].rearrange("p (a e) -> p a e", a=H0),
                                       v_part[1][:, g, :, 0:E0], ALU.subtract).then_inc(v_done[2][g].sem, 1)

                def next_x_low():
                    pool.wait_ge(xt_hi_made.sem, now(xt_hi_made))
                    pool.tensor_tensor(xt_lo[:, :, :].rearrange("p c n -> p (c n)"),
                                       xt_raw[:, :, :].rearrange("p c n -> p (c n)"),
                                       xt_hi[:, :, :].rearrange("p c n -> p (c n)").bitcast(F32), ALU.subtract)\
                        .then_inc(xt_split.sem, 2)

                def deviation0(g):
                    pool.wait_ge(y_var[g].sem, now(y_var[g]))
                    pool.tensor_tensor(rstd[:, g, :], rstd[:, g, :], half_neg[:, :], ALU.pow).then_inc(y_rstd[g].sem, 1)

                def deviation1(g):
                    pool.wait_ge(y2_var[g].sem, now(y2_var[g]))
                    pool.tensor_tensor(rstd2[:, g, :], rstd2[:, g, :], half_neg[:, :], ALU.pow).then_inc(y2_rstd[g].sem, 1)

                def z_subtract(g):
                    pool.wait_ge(z_maxed[g].sem, now(z_maxed[g]))
                    zs = z[:, g, :].rearrange("p (a n) -> p a n", a=H1)
                    pool.tensor_tensor(zs, zs, z_max[:, g, :].unsqueeze(2).to_broadcast([128, H1, N]), ALU.subtract)\
                        .then_inc(z_sub[g].sem, 1)

                def features_bias(g):
                    pool.wait_ge(f_norm[g].sem, now(f_norm[g]))
                    fs = f[:, g, :].rearrange("p (a e) -> p a e", a=H1)
                    pool.tensor_tensor(fs, fs, rows["b1"][:, :].unsqueeze(1).to_broadcast([128, H1, E1]), ALU.add)\
                        .then_inc(f_bias[g].sem, 1)

                def features_negative(g):
                    pool.wait_ge(f_bias[g].sem, now(f_bias[g]))
                    pool.wait_ge(f_elu[g].sem, prev(f_elu[g]))
                    turn.apart()
                    pool.tensor_scalar(f_neg[:, g, :], f[:, g, :], 0.0, None, ALU.min).then_inc(f_min[g].sem, 1)

                def features_difference(g):
                    pool.wait_ge(f_elu[g].sem, now(f_elu[g]))
                    pool.wait_ge(x1_copied[g].sem, prev(x1_copied[g]))
                    pool.tensor_tensor(f[:, g, :], f[:, g, :], x1_kept[:, g, :], ALU.subtract).then_inc(f_diff[g].sem, 1)

                def gated_features(g):
                    pool.wait_ge(f_diff[g].sem, now(f_diff[g]))
                    pool.wait_ge(g_plus[g].sem, prev(g_plus[g]))
                    pool.tensor_tensor(f[:, g, :], f[:, g, :], gate[:, g, :], ALU.mult).then_inc(f_gated[g].sem, 1)

                turn.late(2, gated_features, 1)
                turn.late(-1, next_x_low)
                turn.late(1, z_subtract, 0)
                turn.late(1, hidden_part3, 0)
                turn.late(0, deviation0, 0)
                turn.late(1, z_subtract, 1)
                turn.late(1, hidden_part3, 1)
                turn.late(0, deviation0, 1)
                turn.late(2, deviation1, 0)
                turn.step(0, value_residue, 0)
                turn.step(0, mask0_bias)
                turn.step(2, features_bias, 0)
                turn.step(2, features_negative, 0)
                turn.step(1, source_target_products, 0)
                turn.step(1, source_target_products, 1)
                turn.step(2, features_difference, 0)
                turn.step(1, mask1_bias)
                turn.step(2, gated_features, 0)
                turn.step(0, value_residue, 1)
                turn.step(0, value_part3, 0)
                turn.step(2, features_bias, 1)
                turn.step(2, features_negative, 1)
                turn.late(2, deviation1, 1)
                turn.step(0, value_part3, 1)
                turn.step(1, hidden_residue, 0)
                turn.step(2, features_difference, 1)
                turn.step(1, hidden_residue, 1)

            turns(pool, passed, body, biases_loaded)


def kernel(x, adj, L0_gnn_Wq, L0_gnn_bq, L0_gnn_Wk, L0_gnn_bk, L0_gnn_Wv, L0_gnn_bv, L0_gnn_Wf, L0_gnn_bf,
           L1_gnn_W, L1_gnn_b, L1_gnn_w_src, L1_gnn_w_dst, L1_gnn_H_w, L1_gnn_H_b):
    import numpy as np
    import concourse.bacc as bacc
    from concourse.bass_utils import run_bass_kernel_spmd

    nc = bacc.Bacc("TRN2", target_bir_lowering=False, num_devices=1)
    arrays = {}

    def given(name, a):
        a = np.ascontiguousarray(a)
        arrays[name] = a
        return nc.dram_tensor(name, a.shape, mybir.dt.from_np(a.dtype), kind="ExternalInput").ap()

    def chunked(a):
        return np.asarray(a).reshape(C, 128, D).transpose(1, 0, 2).reshape(128, C * D)

    x, adj = np.asarray(x), np.asarray(adj)
    x_d = given("x", x)
    x_t = given("x_t", x.reshape(PAIRS, 2 * N, C, 128).transpose(0, 3, 2, 1))
    adj_d = given("adj", adj)
    weights = {
        "Wq": given("Wq", chunked(L0_gnn_Wq)),
        "Wk": given("Wk", chunked(L0_gnn_Wk)),
        "Wv": given("Wv", chunked(L0_gnn_Wv)),
        "Wf": given("Wf", chunked(L0_gnn_Wf)),
        "W1": given("W1", chunked(np.asarray(L1_gnn_W).transpose(1, 0, 2).reshape(D, D))),
        "Hw": given("Hw", chunked(np.asarray(L1_gnn_H_w).T)),
    }
    biases = {
        "bq": given("bq", np.asarray(L0_gnn_bq).reshape(C, 128).T),
        "bk": given("bk", np.asarray(L0_gnn_bk).reshape(C, 128).T),
        "bv": given("bv", np.asarray(L0_gnn_bv).reshape(C, 128).T),
    }
    w_sd = np.concatenate([np.asarray(L1_gnn_w_src).reshape(D), np.asarray(L1_gnn_w_dst).reshape(D)])
    row_biases = {"bf": given("bf", L0_gnn_bf), "b1": given("b1", L1_gnn_b),
                  "Hb": given("Hb", L1_gnn_H_b), "w_sd": given("w_sd", w_sd)}
    out = nc.dram_tensor("out", (GRAPHS, N, D), F32, kind="ExternalOutput").ap()
    two_layer_graph_attention(nc, x_d, x_t, adj_d, weights, biases, row_biases, out)
    r = run_bass_kernel_spmd(nc, [arrays], core_ids=[0])
    return r.results[0]["out"]
```
